# Optimizing a Trainium2 kernel written in Bass

```python
import numpy as np
import jax
import jax.numpy as jnp

def _softmax(x, axis=-1):
    return jax.nn.softmax(x, axis=axis)

def _gelu(x):
    return jax.nn.gelu(x, approximate=True)

def _silu(x):
    return jax.nn.silu(x)

def _sigmoid(x):
    return jax.nn.sigmoid(x)

def _layernorm(x, axis=-1, eps=1e-05):
    m = jnp.mean(x, axis=axis, keepdims=True)
    v = jnp.var(x, axis=axis, keepdims=True)
    return (x - m) / jnp.sqrt(v + eps)

def _scatter_add(tgt, idx, src, axis=0):
    return tgt.at[idx].add(src)

def _segment_sum(src, seg, n):
    return jax.ops.segment_sum(src, seg, n)
kernel_name = 'mk_gps_d1_gnn_r8_7e26f8'

def setup_inputs(seed: int=0):
    np.random.seed(seed)
    _w = jnp.asarray

    def _rec_inputs():
        import jax
        import jax.numpy as jnp
        _gk = jax.random.key(seed)
        x = -0.0003713 + 1 * jax.random.normal(jax.random.fold_in(_gk, 1), (6250, 256), jnp.float32)
        _s = jax.random.randint(jax.random.fold_in(_gk, 2), (100000,), 0, 6250, jnp.int32)
        _d = jax.random.randint(jax.random.fold_in(_gk, 3), (100000,), 0, 6250, jnp.int32)
        _loop = jnp.arange(6250, dtype=jnp.int32)
        src = jnp.concatenate([_s, _d, _loop])
        dst = jnp.concatenate([_d, _s, _loop])
        _o = jnp.argsort(dst, stable=True)
        src = src[_o]
        dst = dst[_o]
        return (x, src, dst)
    x, src, dst = _rec_inputs()

    def _L0_gnn_setup():
        import jax, jax.numpy as jnp
        import numpy as np
        N = 6250
        E = 100000
        IN_C = 256
        HEADS = 8
        OUT_C = 32
        NEG_SLOPE = 0.2
        key = jax.random.key(seed)
        k1, k2, k3, k4, k5 = jax.random.split(key, 5)
        x = jax.random.normal(k1, (N, IN_C), dtype=jnp.float32)
        edge_index = jax.random.randint(k2, (2, E), 0, N, dtype=jnp.int64)
        W = jax.random.normal(k3, (IN_C, HEADS * OUT_C), dtype=jnp.float32) * (1.0 / np.sqrt(IN_C))
        attn_l = jax.random.normal(k4, (1, HEADS, OUT_C), dtype=jnp.float32) * 0.1
        attn_r = jax.random.normal(k5, (1, HEADS, OUT_C), dtype=jnp.float32) * 0.1
        bias = jnp.zeros((HEADS * OUT_C,), dtype=jnp.float32)
        return {'x': x, 'edge_index': edge_index, 'W': W, 'attn_l': attn_l, 'attn_r': attn_r, 'bias': bias}
    _L0_gnn_all = _L0_gnn_setup()
    _L0_gnn_in = {k: v for k, v in _L0_gnn_all.items() if k in ('W', 'attn_l', 'attn_r', 'bias')}
    del _L0_gnn_all

    def _L0_mix_setup():
        import math
        import jax, jax.numpy as jnp
        import numpy as np
        EPS_DIV = 1e-07
        EPS_NORM = 1e-12

        def _l2_normalize(x, axis):
            n = jnp.sqrt(jnp.sum(x * x, axis=axis, keepdims=True))
            return x / jnp.maximum(n, EPS_NORM)
        key = jax.random.key(seed)
        ks = jax.random.split(key, 5)
        b, N, C = (8, 512, 256)
        x = jax.random.normal(ks[0], (b, N, C), dtype=jnp.float32)
        W_qkv = jax.random.normal(ks[1], (C, 3 * C), dtype=jnp.float32) * (1.0 / math.sqrt(C))
        b_qkv = jax.random.normal(ks[2], (3 * C,), dtype=jnp.float32) * 0.02
        W_out = jax.random.normal(ks[3], (C, C), dtype=jnp.float32) * (1.0 / math.sqrt(C))
        b_out = jax.random.normal(ks[4], (C,), dtype=jnp.float32) * 0.02
        return {'x': x, 'W_qkv': W_qkv, 'b_qkv': b_qkv, 'W_out': W_out, 'b_out': b_out}
    _L0_mix_all = _L0_mix_setup()
    _L0_mix_in = {k: v for k, v in _L0_mix_all.items() if k in ('W_qkv', 'b_qkv', 'W_out', 'b_out')}
    del _L0_mix_all

    def _L0_ffn_setup():
        import math
        import jax, jax.numpy as jnp
        import numpy as np
        CAPACITY_FACTOR = 1.25
        TOP_K = 2
        LN_EPS = 1e-05

        def _layer_norm(x, gamma, beta):
            mu = jnp.mean(x, axis=-1, keepdims=True)
            var = jnp.var(x, axis=-1, keepdims=True)
            return (x - mu) * jax.lax.rsqrt(var + LN_EPS) * gamma + beta
        key = jax.random.key(seed)
        ks = jax.random.split(key, 4)
        B, S, D, F, E = (8, 512, 256, 512, 8)
        x = jax.random.normal(ks[0], (B, S, D), dtype=jnp.float32)
        Wr = jax.random.normal(ks[1], (D, E), dtype=jnp.float32) / np.sqrt(D)
        br = jnp.zeros((E,), jnp.float32)
        W1 = jax.random.normal(ks[2], (E, D, F), dtype=jnp.float32) / np.sqrt(D)
        b1 = jnp.zeros((E, F), jnp.float32)
        W2 = jax.random.normal(ks[3], (E, F, D), dtype=jnp.float32) / np.sqrt(F)
        b2 = jnp.zeros((E, D), jnp.float32)
        gamma = jnp.ones((D,), jnp.float32)
        beta = jnp.zeros((D,), jnp.float32)
        return {'x': x, 'Wr': Wr, 'br': br, 'W1': W1, 'b1': b1, 'W2': W2, 'b2': b2, 'gamma': gamma, 'beta': beta}
    _L0_ffn_all = _L0_ffn_setup()
    _L0_ffn_in = {k: v for k, v in _L0_ffn_all.items() if k in ('Wr', 'br', 'W1', 'b1', 'W2', 'b2', 'gamma', 'beta')}
    del _L0_ffn_all
    return {'x': x, 'src': src, 'dst': dst, 'L0_gnn_W': _L0_gnn_in['W'], 'L0_gnn_attn_l': _L0_gnn_in['attn_l'], 'L0_gnn_attn_r': _L0_gnn_in['attn_r'], 'L0_gnn_bias': _L0_gnn_in['bias'], 'L0_mix_W_qkv': _L0_mix_in['W_qkv'], 'L0_mix_b_qkv': _L0_mix_in['b_qkv'], 'L0_mix_W_out': _L0_mix_in['W_out'], 'L0_mix_b_out': _L0_mix_in['b_out'], 'L0_ffn_Wr': _L0_ffn_in['Wr'], 'L0_ffn_br': _L0_ffn_in['br'], 'L0_ffn_W1': _L0_ffn_in['W1'], 'L0_ffn_b1': _L0_ffn_in['b1'], 'L0_ffn_W2': _L0_ffn_in['W2'], 'L0_ffn_b2': _L0_ffn_in['b2'], 'L0_ffn_gamma': _L0_ffn_in['gamma'], 'L0_ffn_beta': _L0_ffn_in['beta']}

def reference(x, src, dst, L0_gnn_W, L0_gnn_attn_l, L0_gnn_attn_r, L0_gnn_bias, L0_mix_W_qkv, L0_mix_b_qkv, L0_mix_W_out, L0_mix_b_out, L0_ffn_Wr, L0_ffn_br, L0_ffn_W1, L0_ffn_b1, L0_ffn_W2, L0_ffn_b2, L0_ffn_gamma, L0_ffn_beta):
    import jax
    import jax.numpy as jnp

    def _L0_gnn_ref(x, edge_index, W, attn_l, attn_r, bias):
        import jax, jax.numpy as jnp
        import numpy as np
        N = 6250
        E = 100000
        IN_C = 256
        HEADS = 8
        OUT_C = 32
        NEG_SLOPE = 0.2
        n = x.shape[0]
        h = (x @ W).reshape(n, HEADS, OUT_C)
        a1 = jnp.sum(h * attn_l, axis=-1)
        a2 = jnp.sum(h * attn_r, axis=-1)
        src, dst = (edge_index[0], edge_index[1])
        e = a1[src] + a2[dst]
        e = jax.nn.leaky_relu(e, negative_slope=NEG_SLOPE)
        seg_max = jax.ops.segment_max(e, dst, num_segments=n)
        seg_max = jnp.where(jnp.isfinite(seg_max), seg_max, 0.0)
        ex = jnp.exp(e - seg_max[dst])
        denom = jax.ops.segment_sum(ex, dst, num_segments=n)
        alpha = ex / denom[dst]
        message = h[src] * alpha[:, :, None]
        out = jax.ops.segment_sum(message, dst, num_segments=n)
        out = out.reshape(n, HEADS * OUT_C)
        return out + bias

    def _L0_mix_ref(x, W_qkv, b_qkv, W_out, b_out):
        import math
        import jax, jax.numpy as jnp
        import numpy as np
        EPS_DIV = 1e-07
        EPS_NORM = 1e-12

        def _l2_normalize(x, axis):
            n = jnp.sqrt(jnp.sum(x * x, axis=axis, keepdims=True))
            return x / jnp.maximum(n, EPS_NORM)
        b, N, C = x.shape
        qkv = x @ W_qkv + b_qkv
        q, k, v = jnp.split(qkv, 3, axis=2)
        q = q - jnp.mean(q, axis=2, keepdims=True)
        k = k - jnp.mean(k, axis=2, keepdims=True)
        q2 = q * q
        k2 = k * k
        q2s = jnp.sum(q2, axis=2, keepdims=True)
        k2s = jnp.sum(k2, axis=2, keepdims=True)
        k2 = _l2_normalize(k2 / (k2s + EPS_DIV), axis=-2)
        q2 = _l2_normalize(q2 / (q2s + EPS_DIV), axis=-1)
        kv = jnp.einsum('bnc,bnd->bcd', k2, v)
        t2 = jnp.einsum('bnc,bcd->bnd', q2, kv) / math.sqrt(N)
        attn = v + t2
        return attn @ W_out + b_out

    def _L0_ffn_ref(x, Wr, br, W1, b1, W2, b2, gamma, beta):
        import math
        import jax, jax.numpy as jnp
        import numpy as np
        CAPACITY_FACTOR = 1.25
        TOP_K = 2
        LN_EPS = 1e-05

        def _layer_norm(x, gamma, beta):
            mu = jnp.mean(x, axis=-1, keepdims=True)
            var = jnp.var(x, axis=-1, keepdims=True)
            return (x - mu) * jax.lax.rsqrt(var + LN_EPS) * gamma + beta
        B, S, D = x.shape
        E = Wr.shape[1]
        N = B * S
        K = TOP_K
        logits = jnp.mean(x, axis=1) @ Wr + br
        routing_weights = jax.nn.softmax(logits, axis=-1)
        capacity = float(math.ceil(N * CAPACITY_FACTOR / E))
        expected_loads = routing_weights.sum(axis=0) * (N / B)
        scale = jnp.where(expected_loads > capacity, capacity / expected_loads, 1.0)
        routing_weights = jax.nn.softmax(routing_weights * scale, axis=-1)
        rw_tok = jnp.broadcast_to(routing_weights[:, None, :], (B, S, E)).reshape(N, E)
        top_w, top_i = jax.lax.top_k(rw_tok, K)
        top_w = jax.nn.softmax(top_w, axis=-1)
        xf = x.reshape(N, D)
        h = jax.nn.gelu(jnp.einsum('nd,edf->enf', xf, W1) + b1[:, None, :], approximate=False)
        y = jnp.einsum('enf,efd->end', h, W2) + b2[:, None, :]
        w_dense = jnp.zeros((N, E), x.dtype).at[jnp.arange(N)[:, None], top_i].add(top_w)
        out = jnp.einsum('ne,end->nd', w_dense, y).reshape(B, S, D)
        out = _layer_norm(out + x, gamma, beta)
        return out
    edge_index = jnp.stack([src, dst])
    xn = _layernorm(x, axis=-1)
    x = x + _L0_gnn_ref(xn, edge_index, L0_gnn_W, L0_gnn_attn_l, L0_gnn_attn_r, L0_gnn_bias) + _L0_mix_ref(xn[None], L0_mix_W_qkv, L0_mix_b_qkv, L0_mix_W_out, L0_mix_b_out)[0]
    x = x + _L0_ffn_ref(_layernorm(x, axis=-1)[None], L0_ffn_Wr, L0_ffn_br, L0_ffn_W1, L0_ffn_b1, L0_ffn_W2, L0_ffn_b2, L0_ffn_gamma, L0_ffn_beta)[0]
    return x

_drawn_inputs = setup_inputs


def setup_inputs(seed=0):
    import zlib

    import numpy as np

    out = dict(_drawn_inputs(seed))
    spreads = {'L0_gnn_bias': (0.0, 0.1),
     'L0_ffn_br': (0.0, 0.1),
     'L0_ffn_b1': (0.0, 0.45),
     'L0_ffn_b2': (0.0, 0.305),
     'L0_ffn_gamma': (1.0, 0.2),
     'L0_ffn_beta': (0.0, 0.1)}
    factors = {'L0_mix_b_out': 4.192}
    for name, (base, spread) in spreads.items():
        noise = np.random.default_rng([zlib.crc32(name.encode()), seed]).standard_normal(out[name].shape)
        drawn = base * np.exp(spread * noise) if base else spread * noise
        out[name] = jnp.asarray(drawn.astype(out[name].dtype))
    for name, factor in factors.items():
        out[name] = (out[name] * factor).astype(out[name].dtype)
    return out
```

```python
import math
from contextlib import ExitStack

import concourse.bass as bass
from concourse import mybir

F32 = mybir.dt.float32
BF16 = mybir.dt.bfloat16
I32 = mybir.dt.int32
ALU = mybir.AluOpType
ACT = mybir.ActivationFunctionType
AX = mybir.AxisListType
RMAX = bass.bass_isa.ReduceOp.max

P = 128
N = 6250
C = 256
H = 8
HC = C // H
KC = C // P
NT = -(-N // P)
LAST = N - (NT - 1) * P
E = 206250
G = 2
EG = G * P
U = -(-E // EG)
STEPS = U + NT - 1
SB = 4
TB = SB * G
NB = -(-STEPS // SB)
R3 = 3
IT = NB // R3
KCH = -(-(NB * SB + SB) // P)
KS = KCH * P
UCH = -(-U // P)
NONE = 16384
TW = C + H
PARTS = 3
AW = 2 * H
NE = 8
F = 512
FC = F // P
TOP = 2
CAPACITY = float(math.ceil(N * 1.25 / NE))
SLOPE = 0.2
LN_EPS = 1e-5
EPS_DIV = 1e-7
EPS_NORM = 1e-12
TINY = 1e-30
XP = 7
NXP = NT // XP
XH = 4 * XP
XD = NT - 10
FG = 3
HB = [2, 3, 7, 2, 3, 7, 2, 3]
HB_BEFORE = [-1, 0, -2] + [f - 2 for f in range(3, len(HB))]
NG = NT // FG

A2_LAST = NT - 1
B_FIRST = A2_LAST + 1
B_LAST = B_FIRST + (NT - 1) // R3
assert NB == IT * R3 + 1 and NT == FG * NG + 1 and (NT - 1) % R3 == 0 and B_LAST < IT


def wait(eng, sem, count):
    if isinstance(count, int) and count <= 0:
        return
    eng.wait_ge(sem, count)


class Chain:

    def __init__(self, eng, sem, base=0):
        self.eng, self.sem, self.n = eng, sem, base

    def __call__(self, ins):
        ins.then_inc(self.sem, 1)
        self.n = self.n + 1
        self.eng.wait_ge(self.sem, self.n)


def build(nc, x, src, dst, W, attn_l, attn_r, gnn_bias, W_qkv, b_qkv, W_out, b_out,
          Wr, br, W1, b1, W2, b2, gamma, beta, out):
    h_tab = nc.dram_tensor("h_tab", [NT * P, TW], F32).ap()
    xn_d = nc.dram_tensor("xn_d", [NT, P, C], F32).ap()
    xnt_d = nc.dram_tensor("xnt_d", [NT, P, C], F32).ap()
    q2t_d = nc.dram_tensor("q2t_d", [NT, P, C], F32).ap()

    with ExitStack() as ctx:
        def sb(name, shape, dt=F32):
            return ctx.enter_context(nc.sbuf_tensor(name, shape, dt))

        def sem(name):
            return ctx.enter_context(nc.semaphore(name))

        def sems(name, n):
            return [sem(f"{name}{i}") for i in range(n)]

        bank = [ctx.enter_context(nc.psum_tensor(f"bank{i}", [P, 512], F32)) for i in range(8)]

        X = sb("X", [P, NT, C])
        acc = sb("acc", [P, NT * TW])
        WORK = R3 * TB * (TW + P + P // 2)
        work = sb("work", [P, WORK])
        a2c = sb("a2c", [P, NT * AW])
        a2p = sb("a2p", [P, NT * PARTS * AW], BF16)
        a1t = sb("a1t", [P, NT, H])
        cols = sb("cols", [P, 2 * KS * G])
        srcT = cols[:, 0:KS * G].bitcast(I32)
        dstT = cols[:, KS * G:2 * KS * G]
        t_acc = sb("t_acc", [1, KS], I32)
        t_a2c = sb("t_a2c", [1, KS], I32)
        idx = sb("idx", [P, R3, TB], I32)
        zb = sb("zb", [P, R3, 3, TB * H])
        ident = sb("ident", [P, P])
        iota_p = sb("iota_p", [P, P])
        ones = sb("ones", [P, P])
        wg = sb("wg", [P, KC, C + 2 * H])
        wqkv = sb("wqkv", [P, KC, 3 * C])
        kx = sb("kx", [P, KC, C + 2])
        wout = kx[:, :, 0:C]
        wvo = sb("wvo", [P, KC, C])
        kvw = sb("kvw", [P, KC, C])
        bqk = sb("bqk", [1, 2, C])
        rows = sb("rows", [1, 3, C])
        bv_col = sb("bv_col", [P, KC])
        bvo = sb("bvo", [P, C])
        bvx = kvw[:, 0, :].rearrange("p (k n) -> p k n", k=KC)
        stat = sb("stat", [P, NT, 6])
        sc = sb("sc", [P, 4, NT])
        nq = sb("nq", [P, NT])
        mean = sb("mean", [P, NT])
        rstd = sb("rstd", [P, NT])
        xn_c = sb("xn_c", [P, C + 1])
        xnt_c = sb("xnt_c", [P, KC, P])
        q2t_c = sb("q2t_c", [P, KC, P])
        q2 = sb("q2", [P, C])
        k2 = sb("k2", [P, C])
        sq = sb("sq", [P, C])
        qs = sb("qs", [P, 8])
        small = sb("small", [P, 32])
        amax = sb("amax", [P, 4, 2 * H])
        b2w = kvw[:, 0, :]
        wr_sb = sb("wr_sb", [P, KC, NE])
        mcol = sb("mcol", [P, KC])
        route = sb("route", [1, 16, NE])
        route_i = sb("route_i", [1, TOP], I32)
        wsel = sb("wsel", [P, TOP])
        b2r = rows

        RW = TB * TW
        ring = [work[:, q * RW:(q + 1) * RW].rearrange("p (j w) -> p j w", w=TW) for q in range(R3)]
        s0 = R3 * RW
        hot = [work[:, s0 + q * TB * P:s0 + (q + 1) * TB * P].rearrange("p (j d) -> p j d", d=P)
               for q in range(R3)]
        s1 = s0 + R3 * TB * P
        hotT = [work[:, s1 + q * TB * P // 2:s1 + (q + 1) * TB * P // 2].bitcast(BF16).rearrange("p (j d) -> p j d", d=P)
                for q in range(R3)]
        o = 0

        def view(n):
            nonlocal o
            o += n
            return work[:, o - n:o]
        xn_a = [view(C) for _ in range(2)]
        xnt_a = [view(C).rearrange("p (k n) -> p k n", k=KC) for _ in range(2)]
        h_a = [view(C + 2 * H) for _ in range(2)]
        prod = view(KC * C).rearrange("p (k n) -> p k n", k=KC)
        attn = view(2 * C).rearrange("p (a n) -> p a n", a=2)
        wvT = view(KC * C).rearrange("p (k n) -> p k n", k=KC)
        kio = view(KS)
        cmp = view(KS)
        kcol = view(KCH)
        uio = view(UCH)
        fcol = view(UCH)
        ucol = view(KCH)
        tcol = view(KCH)
        lastd = view(UCH).bitcast(I32)
        lastt = view(UCH).bitcast(I32)
        ucol_i = view(KCH).bitcast(I32)
        iotai = cmp.bitcast(I32)
        urow = view(2 * KS).rearrange("p (a n) -> p a n", a=2)
        f_src = view(KCH * EG).rearrange("p (c e) -> p c e", e=EG)
        f_dst = view(KCH * EG).rearrange("p (c e) -> p c e", e=EG)
        g_src, g_dst = (f.bitcast(I32) for f in (f_src, f_dst))
        assert o <= WORK, (o, WORK)
        o = 0
        w1_sb = view(TOP * KC * F).rearrange("p (e k f) -> p e k f", e=TOP, k=KC)
        w2_sb = view(TOP * FC * C).rearrange("p (e f d) -> p e f d", e=TOP, f=FC)
        b1_sb = view(TOP * FC).rearrange("p (e f) -> p e f", e=TOP)
        x2s = [view(FG * C).rearrange("p (t c) -> p t c", t=FG) for _ in range(2)]
        x2t = [view(KC * FG * P).rearrange("p (k n) -> p k n", k=KC) for _ in range(2)]
        hT = [a.rearrange("p (f n) -> p f n", f=TOP * FC)
              for a in (view(TOP * FC * FG * P), cols[:, 0:TOP * FC * FG * P])]
        y = [wqkv[:].rearrange("p k n -> p (k n)")[:, i * FG * C:(i + 1) * FG * C].rearrange("p (t c) -> p t c", t=FG)
             for i in range(2)]
        gb = view(2 * C).rearrange("p (a c) -> p a c", a=2)
        ystat = view(2 * FG * 6).rearrange("p (a t s) -> p a t s", a=2, s=6)
        ysc = view(2 * 6 * FG).rearrange("p (a s t) -> p a s t", a=2, s=6)
        assert o <= WORK, (o, WORK)

        def acc_tile(t):
            return acc[:, t * TW:(t + 1) * TW]

        var_ready = sem("var_ready")
        root_ready = sem("root_ready")
        x_loaded = sems("x_loaded", 7)
        w_loaded = sem("w_loaded")
        id_set = sem("id_set")
        iota_set = sem("iota_set")
        acc_zero = sem("acc_zero")
        dve_own = sem("dve_own")
        lastd_loaded = sem("lastd_loaded")
        lastd_clear = sem("lastd_clear")
        cmp_done = sem("cmp_done")
        u_counted = sem("u_counted")
        t_ready = sem("t_ready")
        ucol_ready = sem("ucol_ready")
        steps_gathered = sem("steps_gathered")
        f_ready = sem("f_ready")
        steps_turned = sem("steps_turned")
        steps_kept = sem("steps_kept")
        wg_ready = sem("wg_ready")
        wqk_ready = sem("wqk_ready")
        wvt_turned = sem("wvt_turned")
        wvt_kept = sem("wvt_kept")
        wvo_made = sem("wvo_made")
        wvo_kept = sem("wvo_kept")
        bvx_ready = sem("bvx_ready")
        crow_ready = sem("crow_ready")
        xn_ready = sem("xn_ready")
        xn_turned = sem("xn_turned")
        xnt_kept = sem("xnt_kept")
        h_made = sem("h_made")
        h_kept = sem("h_kept")
        a_kept = sem("a_kept")
        xn_stored = sems("xn_stored", 2)
        xnt_stored = sems("xnt_stored", 2)
        h_stored = sems("h_stored", 2)
        ext_ready = sem("ext_ready")
        ext_all = sem("ext_all")
        c_ready = sem("c_ready")
        idx_ready = sem("idx_ready")
        batch_begun = sem("batch_begun")
        gathered = sems("gathered", R3)
        hot_ready = sem("hot_ready")
        hot_turned = sem("hot_turned")
        hotT_kept = sem("hotT_kept")
        a2c_picked = sem("a2c_picked")
        z_own = sem("z_own")
        u_ready = sem("u_ready")
        ex_ready = sem("ex_ready")
        msg_ready = sem("msg_ready")
        summed = sem("summed")
        added = sem("added")
        xnt_loaded = sem("xnt_loaded")
        xn_loaded = sem("xn_loaded")
        qk_made = sem("qk_made")
        roots = sem("roots")
        q2_squared = sem("q2_squared")
        q_own = sem("q_own")
        k2_ready = sem("k2_ready")
        k2_squared = sem("k2_squared")
        kx_added = sem("kx_added")
        q2_turned = sem("q2_turned")
        q2t_kept = sem("q2t_kept")
        q2t_stored = sem("q2t_stored")
        kx_kept = sem("kx_kept")
        kx_turned = sem("kx_turned")
        kxt_kept = sem("kxt_kept")
        kvw_made = sem("kvw_made")
        kvw_ready = sem("kvw_ready")
        mix_loaded = sem("mix_loaded")
        mix_made = sem("mix_made")
        mix_added = sem("mix_added")
        msg_scaled = sem("msg_scaled")
        x1_made = sem("x1_made")
        x2_late = sem("x2_late")
        x2_scaled = sem("x2_scaled")
        x2_ready = sem("x2_ready")
        mean_made = sem("mean_made")
        mean_kept = sem("mean_kept")
        logits_made = sem("logits_made")
        soft_in = sem("soft_in")
        soft_out = sem("soft_out")
        route_ready = sem("route_ready")
        e_loaded = sem("e_loaded")
        wsel_made = sem("wsel_made")
        w2_scaled = sem("w2_scaled")
        b2_ready = sem("b2_ready")
        b2_made = sem("b2_made")
        x2_staged = sem("x2_staged")
        x2_turned = sem("x2_turned")
        x2t_kept = sem("x2t_kept")
        hid_made = sem("hid_made")
        hid_kept = sem("hid_kept")
        y_made = sem("y_made")
        y_added = sem("y_added")
        y_own = sem("y_own")
        y_ready = sem("y_ready")
        out_stored = sems("out_stored", 2)

        block = ctx.enter_context(nc.Block())

        xv = x[0:(NT - 1) * P, :].rearrange("(t p) c -> p t c", p=P)
        XC = (NT - 1) // 6
        NX = 4 * TOP + 2
        NW = 12

        def phases(eng, batch):
            def three(i, side, first=False):
                for q in range(R3):
                    batch(i, q, side, first)
            three(0, "qk")
            with eng.Fori(1, A2_LAST) as i:
                three(i, "qk")
            three(A2_LAST, "qk")
            yield
            three(B_FIRST, "mix", True)
            with eng.Fori(B_FIRST + 1, B_LAST) as i:
                three(i, "mix")
            three(B_LAST, "mix_end")
            with eng.Fori(B_LAST + 1, IT) as i:
                three(i, "")
            batch(IT, 0, "", False)

        def pairs(eng, tile):
            tile(0, 0)
            tile(1, 1)
            with eng.Fori(1, (NT - 1) // 2) as i:
                tile(i * 2, 0)
                tile(i * 2 + 1, 1)
            tile(NT - 1, 0)

        def half(t, p):
            return t // 2 if isinstance(t, int) else (t - p) // 2

        @block.sync
        def _(sp):
            for c in range(6):
                sp.dma_start(X[:, c * XC:(c + 1) * XC, :], xv[:, c * XC:(c + 1) * XC, :]).then_inc(x_loaded[c], 16)
            sp.wait_ge(dve_own, 1)
            sp.dma_start(X[0:LAST, NT - 1, :], x[(NT - 1) * P:N, :]).then_inc(x_loaded[6], 16)

            def tile(t, p):
                sp.wait_ge(xn_ready, t + 1)
                sp.dma_start(xn_d[bass.ds(t, 1)].rearrange("o p c -> p (o c)"), xn_a[p]).then_inc(xn_stored[p], 16)
                sp.wait_ge(xnt_kept, t + 1)
                sp.dma_start(xnt_d[bass.ds(t, 1)].rearrange("o p c -> p (o c)"),
                             xnt_a[p].rearrange("p k n -> p (k n)")).then_inc(xnt_stored[p], 16)
                sp.wait_ge(h_kept, t + 1)
                sp.dma_start(h_tab[bass.ds(t * P, P), :], h_a[p][:, 0:TW]).then_inc(h_stored[p], 16)
            pairs(sp, tile)

            n0, n1 = (NT + 1) // 2, NT // 2
            for s in (xn_stored, xnt_stored):
                sp.wait_ge(s[0], 16 * n0)
                sp.wait_ge(s[1], 16 * n1)

            def store_q2t(t):
                sp.wait_ge(q2t_kept, t + 1)
                sp.dma_start(q2t_d[bass.ds(t, 1)].rearrange("o p c -> p (o c)"),
                             q2t_c[:].rearrange("p k n -> p (k n)")).then_inc(q2t_stored, 16)

            def batch(i, q, side, first):
                if side == "qk" and q == 0:
                    wait(sp, qk_made, i)
                    sp.dma_start(xnt_c[:].rearrange("p k n -> p (k n)"),
                                 xnt_d[bass.ds(i, 1)].rearrange("o p c -> p (o c)")).then_inc(xnt_loaded, 16)
                    wait(sp, kx_added, i)
                    sp.dma_start(xn_c[:, 0:C], xn_d[bass.ds(i, 1)].rearrange("o p c -> p (o c)")).then_inc(xn_loaded, 16)
                    if not (isinstance(i, int) and i == 0):
                        store_q2t(i - 1)
                if side == "mix" or (side == "mix_end" and q == 0):
                    t = (i - B_FIRST) * R3 + q
                    if first and q == 0:
                        sp.wait_ge(q2t_stored, 16 * NT)
                        sp.wait_ge(qk_made, NT)
                    wait(sp, mix_made, t)
                    sp.dma_start(xnt_c[:].rearrange("p k n -> p (k n)"),
                                 xnt_d[bass.ds(t, 1)].rearrange("o p c -> p (o c)")).then_inc(mix_loaded, 16)
                    sp.dma_start(q2t_c[:].rearrange("p k n -> p (k n)"),
                                 q2t_d[bass.ds(t, 1)].rearrange("o p c -> p (o c)")).then_inc(mix_loaded, 16)
            for _ in phases(sp, batch):
                store_q2t(NT - 1)

            sp.wait_ge(route_ready, 1)
            sp.dma_start(gb[:, 0, :], gamma.unsqueeze(0).to_broadcast([P, C])).then_inc(e_loaded, 16)
            sp.dma_start(gb[:, 1, :], beta.unsqueeze(0).to_broadcast([P, C])).then_inc(e_loaded, 16)
            for e in range(TOP):
                n = sp.value_load(route_i[0:1, e:e + 1], min_val=0, max_val=NE - 1)
                sp.dma_start(w1_sb[:, e], W1[bass.ds(n, 1)].rearrange("o (k p) f -> p (o k) f", p=P)).then_inc(e_loaded, 16)
                sp.dma_start(w2_sb[:, e], W2[bass.ds(n, 1)].rearrange("o (f p) d -> p (o f) d", p=P)).then_inc(e_loaded, 16)
                sp.dma_start(b1_sb[:, e, :], b1[bass.ds(n, 1)].rearrange("o (f p) -> p (o f)", p=P),
                             allow_slow_non_contiguous=True).then_inc(e_loaded, 16)
                sp.dma_start(b2r[:, e, :], b2[bass.ds(n, 1)]).then_inc(e_loaded, 16)

            def store(g, p):
                sp.wait_ge(y_ready, g + 1)
                if isinstance(g, int) and g == NG:
                    sp.dma_start(out[g * FG * P:N, :], y[p][0:LAST, 0, :]).then_inc(out_stored[p], 16)
                    return
                sp.dma_start(out[bass.ds(g * FG * P, FG * P), :].rearrange("(t p) c -> p t c", p=P),
                             y[p][:, :, :]).then_inc(out_stored[p], 16)
            with sp.Fori(0, NG // 2) as i:
                store(i * 2, 0)
                store(i * 2 + 1, 1)
            store(NG, 0)
            sp.wait_ge(out_stored[0], 16 * (NG // 2 + 1))
            sp.wait_ge(out_stored[1], 16 * (NG // 2))

        @block.gpsimd
        def _(pool):
            nc.gpsimd.memset(ident[:], 0.0).then_inc(id_set, 1)
            nc.gpsimd.memset(ones[:], 1.0).then_inc(id_set, 1)
            pool.wait_ge(id_set, 1)
            nc.gpsimd.affine_select(out=ident[:], in_=ident[:], compare_op=ALU.not_equal, fill=1.0, base=0,
                                    pattern=[[-1, P]], channel_multiplier=1).then_inc(id_set, 1)
            nc.gpsimd.iota(iotai, pattern=[[1, KS]], base=0, channel_multiplier=0).then_inc(iota_set, 1)
            nc.gpsimd.iota(kcol.bitcast(I32), pattern=[[P, KCH]], base=0, channel_multiplier=1).then_inc(iota_set, 1)
            nc.gpsimd.iota(uio.bitcast(I32), pattern=[[P, UCH]], base=0, channel_multiplier=1).then_inc(iota_set, 1)
            nc.gpsimd.memset(acc[:], 0.0).then_inc(acc_zero, 1)

            pool.wait_ge(ucol_ready, 1)
            for c in range(KCH):
                for g, table in ((g_src, src), (g_dst, dst)):
                    nc.gpsimd.indirect_dma_start(
                        out=g[:, c, :], out_offset=None, in_=table,
                        in_offset=bass.IndirectOffsetOnAxis(ap=ucol_i[:, c:c + 1], axis=0)).then_inc(steps_gathered, 16)
            pool.wait_ge(ext_ready, 1)
            nc.gpsimd.partition_all_reduce(amax[:, 1, :], amax[:, 0, :], P, RMAX).then_inc(ext_all, 1)

            pool.wait_ge(h_stored[0], 16 * ((NT + 1) // 2))
            pool.wait_ge(h_stored[1], 16 * (NT // 2))
            pool.wait_ge(steps_kept, 2 * KCH)
            pool.wait_ge(wvo_kept, 1)

            def batch(i, q, side, first):
                b = i * R3 + q
                pool.wait_ge(idx_ready, b + 1)
                wait(pool, summed, SB * (b - R3 + 1))
                pool.sem_inc(batch_begun, 1)
                for j in range(TB):
                    nc.gpsimd.indirect_dma_start(
                        out=ring[q][:, j, :], out_offset=None, in_=h_tab,
                        in_offset=bass.IndirectOffsetOnAxis(ap=idx[:, q, j:j + 1], axis=0)).then_inc(gathered[q], 16)
            for _ in phases(pool, batch):
                pass

            def stage(g, p, n):
                wait(pool, x2_turned, g - 1)
                a3 = acc[:].rearrange("p (t w) -> p t w", w=TW)
                nc.gpsimd.tensor_copy(x2s[p][:, 0:n, :], a3[:, bass.ds(g * FG, n), 0:C]).then_inc(x2_staged, 1)

            pool.wait_ge(x2_ready, XD)
            pool.wait_ge(x2_late, NT - XD)
            stage(0, 0, FG)
            stage(1, 1, FG)
            with pool.Fori(1, NG // 2) as i:
                stage(i * 2, 0, FG)
                stage(i * 2 + 1, 1, FG)
            stage(NG, 0, 1)

        @block.scalar
        def _(act):
            for dst_ap, src_ap in (
                (wg[:, :, 0:C], W.rearrange("(k p) n -> p k n", p=P)),
                (attn[:, 0, :], attn_l.rearrange("a h j -> a (h j)").to_broadcast([P, C])),
                (attn[:, 1, :], attn_r.rearrange("a h j -> a (h j)").to_broadcast([P, C])),
                (wqkv[:], W_qkv.rearrange("(k p) n -> p k n", p=P)),
                (wout[:], W_out.rearrange("(k p) n -> p k n", p=P)),
                (bqk[:].rearrange("a k n -> a (k n)"), b_qkv[0:2 * C].unsqueeze(0)),
                (bv_col[:, 0:1], b_qkv[2 * C:2 * C + P].unsqueeze(1)),
                (bv_col[:, 1:2], b_qkv[2 * C + P:3 * C].unsqueeze(1)),
                (rows[:, 0, :], gnn_bias.unsqueeze(0)),
                (rows[:, 1, :], b_out.unsqueeze(0)),
                (wr_sb[:], Wr.rearrange("(k p) n -> p k n", p=P)),
                (route[:, 0, :], br.unsqueeze(0)),
            ):
                act.dma_start(dst_ap, src_ap).then_inc(w_loaded, 16)
            act.wait_ge(lastd_clear, 1)
            for c in range(UCH):
                n = min(P, U - c * P)
                act.dma_start(lastd[0:n, c:c + 1], dst[c * P:c * P + n, EG - 1:EG],
                              allow_slow_non_contiguous=True).then_inc(lastd_loaded, 16)

            def root(n, r):
                act.wait_ge(var_ready, n + 1)
                nc.scalar.activation(r, r, ACT.Sqrt).then_inc(root_ready, 1)

            act.wait_ge(wvt_turned, 1)
            nc.scalar.copy(wvT.rearrange("p k n -> p (k n)"), bank[5][:]).then_inc(wvt_kept, 1)

            root(0, rstd[:])

            def tile(t, p):
                act.wait_ge(xn_turned, t + 1)
                wait(act, h_made, t - 1)
                wait(act, xnt_stored[p], 16 * half(t, p) if not (isinstance(t, int) and t < 2) else 0)
                nc.scalar.copy(xnt_a[p].rearrange("p k n -> p (k n)"), bank[p][:, 0:C]).then_inc(xnt_kept, 1)
                act.wait_ge(h_made, t + 1)
                wait(act, h_stored[p], 16 * half(t, p) if not (isinstance(t, int) and t < 2) else 0)
                wait(act, a_kept, t - 1)
                nc.scalar.copy(h_a[p], bank[2 + p][:, 0:C + 2 * H]).then_inc(h_kept, 1)
            pairs(act, tile)

            for c in range(KCH):
                act.wait_ge(steps_turned, c + 1)
                pt = bank[6 + c % 2][:].rearrange("p (a g k) -> p a k g", a=2, g=G)
                nc.scalar.copy(srcT[:, c * P * G:(c + 1) * P * G].rearrange("p (k g) -> p k g", g=G), pt[:, 0]).then_inc(steps_kept, 1)
                nc.scalar.copy(dstT[:, c * P * G:(c + 1) * P * G].rearrange("p (k g) -> p k g", g=G), pt[:, 1]).then_inc(steps_kept, 1)
            act.wait_ge(steps_kept, 2 * KCH)

            def index(b, q):
                nc.scalar.copy(idx[:, q, :], srcT[:, bass.ds(b * TB, TB)]).then_inc(idx_ready, 1)

            def turned(b, q):
                wait(act, a2c_picked, b - R3 + 1)
                for k in range(2):
                    act.wait_ge(hot_turned, b * 2 + k + 1)
                    nc.scalar.copy(hotT[q][:, k * 4:k * 4 + 4, :].rearrange("p j d -> p (j d)"),
                                   bank[k][:]).then_inc(hotT_kept, 1)

            def weights(b, q):
                act.wait_ge(u_ready, b + 1)
                nc.scalar.activation(ring[q][:, :, C:TW], zb[:, q, 2, :].rearrange("p (j h) -> p j h", h=H),
                                     ACT.Exp).then_inc(ex_ready, 1)

            for q in range(R3):
                index(q, q)
            act.wait_ge(hot_ready, 1)
            turned(0, 0)
            weights(0, 0)

            def batch(i, q, side, first):
                b = i * R3 + q
                last = isinstance(i, int) and i == IT
                if not last:
                    act.wait_ge(gathered[q], 16 * TB * (i + 1))
                    index(b + R3, q)
                    turned(b + 1, (q + 1) % R3)
                    weights(b + 1, (q + 1) % R3)
                if side == "qk":
                    if q == 1:
                        act.wait_ge(qk_made, i + 1)
                        wait(act, q2_turned, i)
                        nc.scalar.activation(q2[:], bank[5][:, 0:C], ACT.Square, accum_out=qs[:, 0:1]).then_inc(q2_squared, 1)
                        nc.scalar.activation(k2[:], bank[5][:, C:2 * C], ACT.Square, accum_out=qs[:, 1:2]).then_inc(q2_squared, 1)
                    if q == 2:
                        act.wait_ge(k2_ready, i + 1)
                        nc.scalar.activation(sq[:], q2[:], ACT.Square, accum_out=nq[:, bass.ds(i, 1)]).then_inc(k2_squared, 1)
                        act.wait_ge(k2_squared, i * 2 + 1)
                        nc.scalar.activation(sq[:], k2[:], ACT.Square).then_inc(k2_squared, 1)
                if (side == "qk" and q == 0 and not (isinstance(i, int) and i == 0)):
                    keep_q2t(i - 1)

            def keep_q2t(t):
                act.wait_ge(q2_turned, t + 1)
                wait(act, q2t_stored, 16 * t)
                nc.scalar.copy(q2t_c[:].rearrange("p k n -> p (k n)"), bank[5][:, 0:C]).then_inc(q2t_kept, 1)

            for _ in phases(act, batch):
                keep_q2t(NT - 1)
                act.wait_ge(kx_turned, 1)
                nc.scalar.copy(wqkv[:].rearrange("p k n -> p (k n)")[:, 0:2 * C], bank[5][:]).then_inc(kxt_kept, 1)
                act.wait_ge(k2_squared, 2 * NT)
                nc.scalar.activation(nq[:], nq[:], ACT.Sqrt).then_inc(roots, 1)
                act.wait_ge(kx_kept, 1)
                nc.scalar.activation(small[:, 16:16 + KC], kx[:, :, C + 1], ACT.Sqrt).then_inc(roots, 1)

            for n, (a, e, e_act) in enumerate(((0, XH, XH), (XH, NT, XD))):
                root(1 + n, rstd[:, a:e])
                act.wait_ge(x2_scaled, n + 1)
                for t in range(a, e_act):
                    nc.scalar.activation(acc_tile(t)[:, 0:C], X[:, t, :], ACT.Identity, bias=sc[:, 3, t:t + 1],
                                         scale=rstd[:, t:t + 1]).then_inc(x2_ready, 1)
            act.wait_ge(mean_made, 1)
            nc.scalar.copy(sq[0:1, :], bank[0][0:1, 0:C]).then_inc(mean_kept, 1)
            act.wait_ge(mean_made, 2)
            nc.scalar.copy(mcol[:], bank[1][:, 16:16 + KC]).then_inc(mean_kept, 1)
            act.wait_ge(soft_in, 1)
            nc.scalar.activation(route[:, 2, :], route[:, 1, :], ACT.Exp).then_inc(soft_out, 1)
            act.wait_ge(soft_in, 2)
            nc.scalar.activation(route[:, 6, :], route[:, 5, :], ACT.Exp).then_inc(soft_out, 1)
            act.wait_ge(soft_in, 3)
            nc.scalar.activation(route[:, 12, 0:1], route[:, 11, 0:1], ACT.Exp).then_inc(soft_out, 1)

            def x2_out(g, p, n):
                act.wait_ge(x2_turned, g + 1)
                for k in range(KC):
                    nc.scalar.copy(x2t[p][:, k, 0:n * P], bank[k][:, 0:n * P]).then_inc(x2t_kept, 1)

            def hidden(g, p, n, roots=True):
                for f in range(TOP * FC):
                    if f == FC and roots:
                        root(g + 1, ysc[:, p, 5, :])
                    act.wait_ge(hid_made, g * (TOP * FC) + f + 1)
                    nc.scalar.activation(hT[p][:, f, 0:n * P], bank[HB[f]][:, 0:n * P], ACT.Gelu,
                                         bias=b1_sb[:, f // FC, f % FC:f % FC + 1]).then_inc(hid_kept, 1)
            x2_out(0, 0, FG)
            act.wait_ge(e_loaded, 16 * NX)
            hidden(0, 0, FG, False)
            x2_out(1, 1, FG)
            hidden(1, 1, FG, False)
            with act.Fori(1, NG // 2) as i:
                for p in range(2):
                    x2_out(i * 2 + p, p, FG)
                    hidden(i * 2 + p, p, FG)
            x2_out(NG, 0, 1)
            hidden(NG, 0, 1)
            root(NG + 2, ysc[:, 1, 5, :])
            root(NG + 3, ysc[:, 0, 5, 0:1])

        @block.tensor
        def _(pe):
            mm = nc.tensor.matmul
            turn = nc.tensor.transpose
            pe.wait_ge(id_set, 3)
            pe.wait_ge(w_loaded, 16 * NW)
            for d in range(KC):
                for j in range(KC):
                    ins = turn(bank[5][:, (d * KC + j) * P:(d * KC + j + 1) * P],
                               wqkv[:, j, 2 * C + d * P:2 * C + (d + 1) * P], ident[:])
            ins.then_inc(wvt_turned, 1)
            pe.wait_ge(wvt_kept, 1)
            for j in range(KC):
                for d in range(KC):
                    mm(bank[4][:, j * C:(j + 1) * C], wvT[:, d, j * P:(j + 1) * P], wout[:, d, :],
                       start=(d == 0), stop=(d == KC - 1))
            pe.wait_ge(bvx_ready, 1)
            for d in range(KC):
                ins = mm(bank[3][:, 0:C], bvx[:, d, :], wout[:, d, :], start=(d == 0), stop=(d == KC - 1))
            ins.then_inc(wvo_made, 1)

            pe.wait_ge(cmp_done, 1)
            for c in range(KCH):
                mm(bank[6][:, c:c + 1], cmp[:, c * P:(c + 1) * P], ones[:, 0:1], start=True, stop=True)
            for k in range(2):
                ins = mm(bank[7 - k][0:1, 8:8 + KS // 2], ones[:, 0:1], cmp[:, k * (KS // 2):(k + 1) * (KS // 2)],
                         start=True, stop=True)
            ins.then_inc(u_counted, 1)

            pe.wait_ge(wg_ready, 1)
            pe.wait_ge(wvo_kept, 1)

            def tile(t, p):
                pe.wait_ge(xn_ready, t + 1)
                wait(pe, xnt_kept, t - 1)
                for k in range(KC):
                    ins = turn(bank[p][:, k * P:(k + 1) * P], xn_a[p][:, k * P:(k + 1) * P], ident[:])
                ins.then_inc(xn_turned, 1)
                pe.wait_ge(xnt_kept, t + 1)
                wait(pe, h_kept, t - 1)
                for k in range(KC):
                    ins = mm(bank[2 + p][:, 0:C + 2 * H], xnt_a[p][:, k, :], wg[:, k, :], start=(k == 0), stop=(k == KC - 1))
                ins.then_inc(h_made, 1)
            pairs(pe, tile)

            pe.wait_ge(f_ready, 2)
            for c in range(KCH):
                wait(pe, steps_kept, 2 * (c - 1))
                for a, f in enumerate((f_src, f_dst)):
                    for g in range(G):
                        o_ = (a * G + g) * P
                        ins = turn(bank[6 + c % 2][:, o_:o_ + P], f[:, c, g * P:(g + 1) * P], ident[:])
                ins.then_inc(steps_turned, 1)

            def turned(b, q):
                pe.wait_ge(hot_ready, b + 1)
                for k in range(2):
                    wait(pe, hotT_kept, b * 2 + k - 1)
                    for j in range(4):
                        ins = turn(bank[k][:, j * P:(j + 1) * P], hot[q][:, k * 4 + j, :], ident[:])
                    ins.then_inc(hot_turned, 1)

            def pick(b, q):
                _, ts = nc.values_load_multi_w_load_instructions(
                    t_a2c[0:1, bass.ds(b * SB, SB)], engines=[mybir.EngineType.PE], min_val=0,
                    max_val=(NT - 1) * PARTS * AW, skip_runtime_bounds_check_because="steps' node tiles are clamped")
                pe.wait_ge(hotT_kept, b * 2 + 2)
                wait(pe, u_ready, b)
                for j in range(TB):
                    for k in range(PARTS):
                        ins = mm(bank[2][:, j * AW:(j + 1) * AW], hotT[q][:, j, :],
                                 a2p[:, bass.ds(ts[j // G] + k * AW, AW)], start=(k == 0), stop=(k == PARTS - 1))
                ins.then_inc(a2c_picked, 1)

            pe.wait_ge(t_ready, 1)
            pe.wait_ge(a_kept, NT)
            pe.wait_ge(h_kept, NT)
            pe.wait_ge(steps_kept, 2 * KCH)
            turned(0, 0)
            pe.wait_ge(c_ready, 1)
            pick(0, 0)
            pe.wait_ge(wqk_ready, 1)

            def batch(i, q, side, first):
                b = i * R3 + q
                last = isinstance(i, int) and i == IT
                if not last:
                    turned(b + 1, (q + 1) % R3)
                for s in range(SB):
                    if s % 2 == 0:
                        pe.wait_ge(msg_ready, b * 2 + s // 2 + 1)
                    if s == 2 and not last:
                        pick(b + 1, (q + 1) % R3)
                    wait(pe, added, b * SB + s - 1)
                    for g in range(G):
                        ins = mm(bank[3 + s % 2][:, 0:TW], hot[q][:, s * G + g, :], ring[q][:, s * G + g, :],
                                 start=(g == 0), stop=(g == G - 1))
                    ins.then_inc(summed, 1)
                if side == "qk":
                    if q == 0:
                        pe.wait_ge(xnt_loaded, (i + 1) * 16)
                        wait(pe, q2t_kept, i)
                        mm(bank[5][:], ones[0:1, :], bqk[:].rearrange("a k n -> a (k n)"), start=True, stop=False)
                        for k in range(KC):
                            ins = mm(bank[5][:], xnt_c[:, k, :], wqkv[:, k, 0:2 * C], start=False, stop=(k == KC - 1))
                        ins.then_inc(qk_made, 1)
                    if q == 2:
                        end = isinstance(i, int) and i == A2_LAST
                        begin = isinstance(i, int) and i == 0
                        n = LAST if end else P
                        pe.wait_ge(xn_loaded, (i + 1) * 16)
                        pe.wait_ge(k2_squared, i * 2 + 2)
                        for k in range(KC):
                            mm(bank[6 + k][:, 0:C + 1], k2[0:n, k * P:(k + 1) * P], xn_c[0:n, :],
                               start=begin, stop=end, skip_group_check=True)
                            ins = mm(bank[6 + k][:, C + 1:C + 2], sq[0:n, k * P:(k + 1) * P], ones[0:n, 0:1],
                                     start=False, stop=end, skip_group_check=True)
                        ins.then_inc(kx_added, 1)
                        for k in range(KC):
                            ins = turn(bank[5][:, k * P:(k + 1) * P], q2[:, k * P:(k + 1) * P], ident[:])
                        ins.then_inc(q2_turned, 1)
                if side == "mix" or (side == "mix_end" and q == 0):
                    t = (i - B_FIRST) * R3 + q
                    if first and q == 0:
                        pe.wait_ge(kvw_ready, 1)
                        pe.wait_ge(crow_ready, 1)
                    pe.wait_ge(mix_loaded, (t + 1) * 32)
                    wait(pe, mix_added, t * 2)
                    mm(bank[5][:, 0:C], ones[0:1, :], rows[0:1, 2, :], start=True, stop=False)
                    for k in range(KC):
                        mm(bank[5][:, 0:C], xnt_c[:, k, :], wvo[:, k, :], start=False, stop=(k == KC - 1))
                    for k in range(KC):
                        ins = mm(bank[6][:, 0:C], q2t_c[:, k, :], kvw[:, k, :], start=(k == 0), stop=(k == KC - 1))
                    ins.then_inc(mix_made, 1)

            for _ in phases(pe, batch):
                pe.wait_ge(kx_kept, 1)
                pe.wait_ge(q2t_kept, NT)
                for j in range(KC):
                    for k in range(KC):
                        ins = turn(bank[5][:, (j * KC + k) * P:(j * KC + k + 1) * P], kx[:, k, j * P:(j + 1) * P], ident[:])
                ins.then_inc(kx_turned, 1)
                pe.wait_ge(kxt_kept, 1)
                kxT = wqkv[:].rearrange("p k n -> p (k n)")
                for k in range(KC):
                    for j in range(KC):
                        ins = mm(bank[6 + k][:, 0:C], kxT[:, (j * KC + k) * P:(j * KC + k + 1) * P], wvo[:, j, :],
                                 start=(j == 0), stop=(j == KC - 1))
                ins.then_inc(kvw_made, 1)

            def x2_in(g, p, n):
                pe.wait_ge(x2_staged, g + 1)
                wait(pe, x2t_kept, g * KC)
                for k in range(KC):
                    for j in range(n):
                        ins = turn(bank[k][:, j * P:(j + 1) * P], x2s[p][:, j, k * P:(k + 1) * P], ident[:])
                ins.then_inc(x2_turned, 1)

            for t in range(NT):
                n = LAST if t == NT - 1 else P
                if t < XD:
                    pe.wait_ge(x2_ready, t + 1)
                else:
                    pe.wait_ge(x2_late, t - XD + 1)
                ins = mm(bank[0][0:1, 0:C], ones[0:n, 0:1], acc_tile(t)[0:n, 0:C], start=(t == 0), stop=(t == NT - 1))
            ins.then_inc(mean_made, 1)
            pe.wait_ge(mean_kept, 1)
            for k in range(KC):
                ins = mm(bank[1][:, 16 + k:17 + k], sq[0:1, k * P:(k + 1) * P], ones[0:1, 0:1], start=True, stop=True)
            ins.then_inc(mean_made, 1)
            pe.wait_ge(mean_kept, 2)
            for k in range(KC):
                ins = mm(bank[1][0:1, 0:NE], mcol[:, k:k + 1], wr_sb[:, k, :], start=(k == 0), stop=(k == KC - 1))
            ins.then_inc(logits_made, 1)
            pe.wait_ge(soft_in, 1)
            x2_in(0, 0, FG)
            pe.wait_ge(route_ready, 1)
            mm(bank[4][:, 0:TOP], ones[0:1, :], route[0:1, 14, 0:TOP], start=True, stop=True).then_inc(wsel_made, 1)
            pe.wait_ge(b2_ready, 1)
            mm(bank[6][:, 0:C], ones[0:1, :], b2r[0:1, 2, :], start=True, stop=True).then_inc(b2_made, 1)

            def hidden(g, p, n):
                pe.wait_ge(x2t_kept, (g + 1) * KC)
                for f in range(TOP * FC):
                    before = HB_BEFORE[f]
                    wait(pe, hid_kept, g * (TOP * FC) + before)
                    for k in range(KC):
                        ins = mm(bank[HB[f]][:, 0:n * P], w1_sb[:, f // FC, k, (f % FC) * P:(f % FC + 1) * P],
                                 x2t[p][:, k, 0:n * P], start=(k == 0), stop=(k == KC - 1))
                    ins.then_inc(hid_made, 1)

            def down(g, p, n):
                pe.wait_ge(hid_kept, (g + 1) * (TOP * FC))
                for j in range(n):
                    wait(pe, y_added, g * FG + j - FG + 1)
                    for f in range(TOP * FC):
                        ins = mm(bank[4 + j][:, 0:C], hT[p][:, f, j * P:(j + 1) * P], w2_sb[:, f // FC, f % FC, :],
                                 start=(f == 0), stop=(f == TOP * FC - 1))
                    ins.then_inc(y_made, 1)
            pe.wait_ge(e_loaded, 16 * NX)
            hidden(0, 0, FG)
            x2_in(1, 1, FG)
            pe.wait_ge(w2_scaled, 1)
            for g in range(2):
                hidden(g + 1, 1 - g, FG)
                x2_in(g + 2, g, FG)
                down(g, g, FG)
            with pe.Fori(1, NG // 2 - 1) as i:
                for p in range(2):
                    hidden(i * 2 + p + 1, 1 - p, FG)
                    x2_in(i * 2 + p + 2, p, FG)
                    down(i * 2 + p, p, FG)
            hidden(NG - 1, 1, FG)
            x2_in(NG, 0, 1)
            down(NG - 2, 0, FG)
            hidden(NG, 0, 1)
            down(NG - 1, 1, FG)
            down(NG, 0, 1)

        @block.vector
        def _(dve):
            v = nc.vector
            own = Chain(dve, dve_own)

            def ln_stats(link, n, st, s, m, r):
                v.tensor_tensor(s[1], st[:, :, 2], st[:, :, 5], ALU.add).then_inc(link.sem, 1)
                v.tensor_tensor(s[2], st[:, :, 1], st[:, :, 4], ALU.add).then_inc(link.sem, 1)
                link.n = link.n + 2
                link(v.tensor_tensor(s[0], st[:, :, 1], st[:, :, 4], ALU.subtract))
                link(v.scalar_tensor_tensor(out=s[0], in0=s[0], scalar=C / 4.0, in1=s[0], op0=ALU.mult, op1=ALU.mult))
                v.tensor_scalar(m, s[2], 0.5, None, ALU.mult).then_inc(link.sem, 1)
                link.n = link.n + 1
                link(v.tensor_tensor(s[1], s[1], s[0], ALU.add))
                v.tensor_scalar(r, s[1], 1.0 / C, LN_EPS, ALU.mult, ALU.add).then_inc(var_ready, 1)
                dve.wait_ge(root_ready, n + 1)
                link(v.reciprocal(r, r))

            own(v.memset(X[:, NT - 1, :], 0.0))
            v.memset(lastd, 1 << 20).then_inc(lastd_clear, 1)

            dve.wait_ge(iota_set, 3)
            v.tensor_copy(iota_p[:], iotai[:, 0:P])
            v.tensor_copy(kio, iotai).then_inc(dve_own, 1)
            own.n += 1
            own(v.tensor_copy(ucol, kcol.bitcast(I32)))
            v.tensor_copy(kcol, ucol)
            own(v.tensor_copy(tcol[:, 0:UCH], uio.bitcast(I32)))
            dve.wait_ge(lastd_loaded, 16 * UCH)
            dve.wait_ge(lastd_clear, 1)
            own(v.tensor_scalar(lastt, lastd, 7, None, ALU.arith_shift_right))
            own(v.tensor_scalar(fcol, lastt, float(NT - 1), None, ALU.min))
            own(v.tensor_tensor(fcol, fcol, tcol[:, 0:UCH], ALU.add))
            own(v.tensor_scalar(cmp, kio, fcol[:, 0:1], None, ALU.is_gt))
            for c in range(1, UCH):
                ins = v.scalar_tensor_tensor(out=cmp, in0=kio, scalar=fcol[:, c:c + 1], in1=cmp, op0=ALU.is_gt, op1=ALU.add)
                own(ins)
            dve.sem_inc(cmp_done, 1)

            dve.wait_ge(w_loaded, 16 * NW)
            for a in range(2):
                for k in range(KC):
                    ins = v.tensor_tensor(prod[:, k, :], wg[:, k, 0:C], attn[:, a, :], ALU.mult)
                    ins.then_inc(dve_own, 1)
                    own.n += 1
                dve.wait_ge(dve_own, own.n)
                for k in range(KC):
                    ins = v.tensor_reduce(wg[:, k, C + a * H:C + (a + 1) * H], prod[:, k, :].rearrange("p (h j) -> p h j", h=H),
                                          AX.X, ALU.add)
                    own(ins)
            dve.sem_inc(wg_ready, 1)

            own(v.tensor_copy(bvx, bv_col[:].unsqueeze(2).to_broadcast([P, KC, P])))
            dve.sem_inc(bvx_ready, 1)

            dve.wait_ge(u_counted, 1)
            v.tensor_scalar(ucol, bank[6][:, 0:KCH], float(U), None, ALU.min).then_inc(dve_own, 1)
            own(v.tensor_copy(urow[0:1, 0, 0:KS // 2], bank[7][0:1, 8:8 + KS // 2]))
            own.n += 1
            own(v.tensor_copy(urow[0:1, 0, KS // 2:KS], bank[6][0:1, 8:8 + KS // 2]))
            v.tensor_copy(ucol_i, ucol).then_inc(ucol_ready, 1)
            own(v.tensor_tensor(tcol, kcol, bank[6][:, 0:KCH], ALU.subtract))
            own(v.tensor_scalar(tcol, tcol, float(NT - 1), float(P), ALU.min, ALU.mult))
            own(v.tensor_tensor(urow[0:1, 1, :], kio[0:1, :], urow[0:1, 0, :], ALU.subtract))
            own(v.tensor_scalar(urow[0:1, 1, :], urow[0:1, 1, :], float(NT - 1), None, ALU.min))
            v.tensor_scalar(t_acc[:], urow[0:1, 1, :], float(TW), None, ALU.mult).then_inc(dve_own, 1)
            own.n += 1
            own(v.tensor_scalar(t_a2c[:], urow[0:1, 1, :], float(PARTS * AW), None, ALU.mult))
            dve.sem_inc(t_ready, 1)

            dve.wait_ge(wvo_made, 1)
            own(v.tensor_copy(wvo[:].rearrange("p k n -> p (k n)"), bank[4][:]))
            own(v.tensor_copy(bvo[:], bank[3][:, 0:C]))
            own(v.tensor_tensor(rows[:, 2, :], rows[:, 0, :], rows[:, 1, :], ALU.add))
            own(v.tensor_tensor(rows[:, 2, :], rows[:, 2, :], bvo[0:1, :], ALU.add))
            dve.sem_inc(wvo_kept, 1)
            dve.sem_inc(crow_ready, 1)

            for c in range(7):
                dve.wait_ge(x_loaded[c], 16)
                for t in range(c * XC, min((c + 1) * XC, NT)):
                    ins = v.bn_stats(stat[:, t, :], X[:, t, :])
            ins.then_inc(dve_own, 1)
            own.n += 1
            dve.wait_ge(dve_own, own.n)
            ln_stats(own, 0, stat, [sc[:, n, :] for n in range(4)], mean[:], rstd[:])

            def tile(t, p):
                wait(dve, xn_turned, t - 1)
                wait(dve, xn_stored[p], 16 * half(t, p) if not (isinstance(t, int) and t < 2) else 0)
                v.tensor_scalar(xn_a[p].unsqueeze(1), X[:, bass.ds(t, 1), :], mean[:, bass.ds(t, 1)],
                                rstd[:, bass.ds(t, 1)], ALU.subtract, ALU.mult).then_inc(xn_ready, 1)
                if not (isinstance(t, int) and t == 0):
                    keep(t - 1, 1 - p)

            def keep(t, p):
                dve.wait_ge(h_kept, t + 1)
                v.tensor_copy(a1t[:, bass.ds(t, 1), :], h_a[p][:, C:C + H].unsqueeze(1))
                v.tensor_copy(a2c[:, bass.ds(t * AW, H)], h_a[p][:, C + H:C + 2 * H]).then_inc(a_kept, 1)
            pairs(dve, tile)
            keep(NT - 1, 0)

            dve.wait_ge(a_kept, NT)
            v.tensor_reduce(amax[:, 0, 0:H], a1t[:].rearrange("p t h -> p h t"), AX.X, ALU.max).then_inc(dve_own, 1)
            own.n += 1
            own(v.tensor_reduce(amax[:, 2, 0:H], a1t[:].rearrange("p t h -> p h t"), AX.X, ALU.min))
            own(v.tensor_scalar(amax[:, 0, H:2 * H], amax[:, 2, 0:H], -1.0, None, ALU.mult))
            dve.sem_inc(ext_ready, 1)
            dve.wait_ge(ext_all, 1)
            a2v = a2c[:].rearrange("p (t a) -> p t a", a=AW)
            cz = a1t[:]
            own(v.tensor_tensor(cz, a2v[:, :, 0:H], amax[:, 1, 0:H].unsqueeze(1).to_broadcast([P, NT, H]), ALU.add))
            own(v.scalar_tensor_tensor(out=a2v[:, :, H:AW], in0=cz, scalar=SLOPE, in1=cz, op0=ALU.mult, op1=ALU.max))
            for k in range(PARTS):
                part = a2p[:].rearrange("p (t k a) -> p t k a", k=PARTS, a=AW)[:, :, k, :]
                own(v.tensor_copy(part, a2v))
                if k < PARTS - 1:
                    own(v.tensor_tensor(a2v, a2v, part, ALU.subtract))
            dve.sem_inc(c_ready, 1)

            dve.wait_ge(steps_gathered, 16 * 2 * KCH)
            v.tensor_copy(f_src.rearrange("p c e -> p (c e)"), g_src.rearrange("p c e -> p (c e)")).then_inc(f_ready, 1)
            for c in range(KCH):
                ins = v.tensor_scalar(f_dst[:, c, :], g_dst[:, c, :], tcol[:, c:c + 1], None, ALU.subtract)
            ins.then_inc(f_ready, 1)

            w4 = wqkv[:, :, 0:2 * C].rearrange("p k (a n) -> p k a n", a=2)
            own(v.tensor_reduce(small[:, 0:4].rearrange("p (k a) -> p k a", a=2), w4, AX.X, ALU.add))
            v.tensor_reduce(small[0:1, 4:6], bqk[:], AX.X, ALU.add).then_inc(dve_own, 1)
            own.n += 1
            own(v.tensor_scalar(small[:, 8:12], small[:, 0:4], -1.0 / C, None, ALU.mult))
            own(v.tensor_scalar(small[0:1, 12:14], small[0:1, 4:6], -1.0 / C, None, ALU.mult))
            for k in range(KC):
                for a in range(2):
                    own(v.tensor_scalar(w4[:, k, a, :], w4[:, k, a, :], small[:, 8 + 2 * k + a:9 + 2 * k + a], None, ALU.add))
            for a in range(2):
                own(v.tensor_scalar(bqk[:, a, :], bqk[:, a, :], small[0:1, 12 + a:13 + a], None, ALU.add))
            own(v.memset(xn_c[:, C:C + 1], 1.0))
            dve.sem_inc(wqk_ready, 1)

            def one_hots(b, q):
                wait(dve, summed, (b - R3 + 1) * SB)
                v.tensor_tensor(hot[q], iota_p[:].unsqueeze(1).to_broadcast([P, TB, P]),
                                dstT[:, bass.ds(b * TB, TB)].unsqueeze(2).to_broadcast([P, TB, P]),
                                ALU.is_equal).then_inc(hot_ready, 1)

            dve.wait_ge(steps_kept, 2 * KCH)
            dve.wait_ge(h_stored[0], 16 * ((NT + 1) // 2))
            dve.wait_ge(h_stored[1], 16 * (NT // 2))
            dve.wait_ge(xnt_stored[0], 16 * ((NT + 1) // 2))
            dve.wait_ge(xnt_stored[1], 16 * (NT // 2))
            dve.wait_ge(acc_zero, 1)

            def exponents(b, q, n):
                dve.wait_ge(gathered[q], n * 16 * TB)
                dve.wait_ge(a2c_picked, b + 1)
                z = [zb[:, q, k, :].rearrange("p (j h) -> p j h", h=H) for k in range(3)]
                pk = bank[2][:, 0:TB * AW].rearrange("p (j a) -> p j a", a=AW)
                link = Chain(dve, z_own, b * 2)
                link(v.tensor_tensor(z[0], ring[q][:, :, C:TW], pk[:, :, 0:H], ALU.add))
                link(v.scalar_tensor_tensor(out=z[1], in0=z[0], scalar=SLOPE, in1=z[0], op0=ALU.mult, op1=ALU.max))
                v.tensor_tensor(z[2], z[1], pk[:, :, H:AW], ALU.subtract).then_inc(u_ready, 1)

            one_hots(0, 0)
            one_hots(1, 1)
            exponents(0, 0, 1)

            def batch(i, q, side, first):
                b = i * R3 + q
                last = isinstance(i, int) and i == IT
                _, ts = nc.values_load_multi_w_load_instructions(
                    t_acc[0:1, bass.ds(b * SB, SB)], engines=[mybir.EngineType.DVE], min_val=0,
                    max_val=(NT - 1) * TW, skip_runtime_bounds_check_because="steps' node tiles are clamped")
                dve.wait_ge(ex_ready, b + 1)
                for k in range(2):
                    m = ring[q][:, k * 4:k * 4 + 4, 0:C].rearrange("p j (h c) -> p j h c", h=H)
                    ex = ring[q][:, k * 4:k * 4 + 4, C:TW].unsqueeze(3).to_broadcast([P, 4, H, HC])
                    v.tensor_tensor(m, m, ex, ALU.mult).then_inc(msg_ready, 1)

                def add(s):
                    dve.wait_ge(summed, b * SB + s + 1)
                    wait(dve, added, b * SB + s)
                    a = acc[:, bass.ds(ts[s], TW)]
                    v.tensor_tensor(a, bank[3 + s % 2][:, 0:TW], a, ALU.add).then_inc(added, 1)
                add(0)
                if not last:
                    one_hots(b + 2, (q + 2) % R3)
                add(1)
                if not last:
                    exponents(b + 1, (q + 1) % R3, i + 1 if q < 2 else i + 2)
                add(2)
                if side == "qk" and q == 2:
                    dve.wait_ge(q2_squared, (i + 1) * 2)
                    lq = Chain(dve, q_own, i * 2)
                    lq(v.tensor_scalar(qs[:, 2:4], qs[:, 0:2], EPS_DIV, None, ALU.add))
                    lq(v.reciprocal(qs[:, 4:6], qs[:, 2:4]))
                    v.tensor_scalar(q2[:], q2[:], qs[:, 4:5], None, ALU.mult)
                    v.tensor_scalar(k2[:], k2[:], qs[:, 5:6], None, ALU.mult).then_inc(k2_ready, 1)
                add(3)
                if side == "mix" or (side == "mix_end" and q < 2):
                    t = (i - B_FIRST) * R3 + q - 1
                    if not (first and q == 0):
                        dve.wait_ge(mix_made, t + 1)
                        xt = X[:, bass.ds(t, 1), :]
                        v.tensor_tensor(xt, xt, bank[5][:, 0:C].unsqueeze(1), ALU.add).then_inc(mix_added, 1)
                        dve.wait_ge(mix_added, t * 2 + 1)
                        v.scalar_tensor_tensor(out=xt, in0=bank[6][:, 0:C].unsqueeze(1), scalar=nq[:, bass.ds(t, 1)],
                                               in1=xt, op0=ALU.mult, op1=ALU.add).then_inc(mix_added, 1)

            for _ in phases(dve, batch):
                dve.wait_ge(kx_added, NT)
                for k in range(KC):
                    ins = v.tensor_copy(kx[:, k, :], bank[6 + k][:, 0:C + 2])
                    own(ins)
                dve.sem_inc(kx_kept, 1)
                kn = small[:, 16:16 + KC]
                dve.wait_ge(roots, 2)
                own(v.tensor_scalar(kn, kn, EPS_NORM, None, ALU.max))
                own(v.reciprocal(small[:, 20:20 + KC], kn))
                own(v.tensor_scalar(nq[:], nq[:], EPS_NORM, None, ALU.max))
                own(v.reciprocal(nq[:], nq[:]))
                dve.wait_ge(kvw_made, 1)
                for k in range(KC):
                    own(v.scalar_tensor_tensor(out=kvw[:, k, :], in0=bvo[:], scalar=kx[:, k, C:C + 1], in1=bank[6 + k][:, 0:C],
                                               op0=ALU.mult, op1=ALU.add))
                    own(v.tensor_scalar(kvw[:, k, :], kvw[:, k, :], small[:, 20 + k:21 + k], 1.0 / math.sqrt(N),
                                        ALU.mult, ALU.mult))
                dve.sem_inc(kvw_ready, 1)

            a3 = acc[:].rearrange("p (t w) -> p t w", w=TW)
            dve.wait_ge(added, NB * SB)
            den = a3[:, :, C:TW]
            own(v.tensor_scalar(a1t[:], den, TINY, None, ALU.max))
            own(v.reciprocal(a1t[:], a1t[:]))
            dve.wait_ge(mix_added, 2 * NT)
            for c in range(NXP + 2):
                if c < NXP:
                    m = a3[:, c * XP:(c + 1) * XP, 0:C].rearrange("p t (h c) -> p t h c", h=H)
                    r_ = a1t[:, c * XP:(c + 1) * XP, :].unsqueeze(3).to_broadcast([P, XP, H, HC])
                    v.tensor_tensor(m, m, r_, ALU.mult).then_inc(msg_scaled, 1)
                if 0 < c <= NXP:
                    dve.wait_ge(msg_scaled, c)
                    xc = X[:, (c - 1) * XP:c * XP, :]
                    v.tensor_tensor(xc, xc, a3[:, (c - 1) * XP:c * XP, 0:C], ALU.add).then_inc(x1_made, 1)
                if c > 1:
                    dve.wait_ge(x1_made, c - 1)
                    for t in range((c - 2) * XP, (c - 1) * XP):
                        ins = v.bn_stats(stat[:, t, :], X[:, t, :])
                    own(ins)
                for n, (a, e) in enumerate(((0, XH), (XH, NT))):
                    if e == (c - 1) * XP:
                        ln_stats(own, 1 + n, stat[:, a:e, :], [sc[:, k, a:e] for k in range(4)], mean[:, a:e], rstd[:, a:e])
                        own(v.scalar_tensor_tensor(out=sc[:, 3, a:e], in0=mean[:, a:e], scalar=-1.0, in1=rstd[:, a:e],
                                                   op0=ALU.mult, op1=ALU.mult))
                        dve.sem_inc(x2_scaled, 1)
            for t in range(XD, NT):
                v.tensor_scalar(acc_tile(t)[:, 0:C], X[:, t, :], mean[:, t:t + 1], rstd[:, t:t + 1],
                                ALU.subtract, ALU.mult).then_inc(x2_late, 1)

            def r(n, w=NE):
                return route[0:1, n, 0:w]
            io = iota_p[0:1, 0:NE]
            dve.wait_ge(logits_made, 1)
            own(v.scalar_tensor_tensor(out=r(1), in0=bank[1][0:1, 0:NE], scalar=1.0 / N, in1=r(0), op0=ALU.mult, op1=ALU.add))
            own(v.tensor_reduce(r(3, 1), r(1), AX.X, ALU.max))
            own(v.tensor_scalar(r(1), r(1), r(3, 1), None, ALU.subtract))
            dve.sem_inc(soft_in, 1)
            dve.wait_ge(soft_out, 1)
            own(v.tensor_reduce(r(3, 1), r(2), AX.X, ALU.add))
            own(v.reciprocal(r(4, 1), r(3, 1)))
            own(v.tensor_scalar(r(2), r(2), r(4, 1), None, ALU.mult))
            own(v.tensor_scalar(r(4), r(2), float(N), TINY, ALU.mult, ALU.max))
            own(v.reciprocal(r(4), r(4)))
            own(v.tensor_scalar(r(4), r(4), CAPACITY, 1.0, ALU.mult, ALU.min))
            own(v.tensor_tensor(r(5), r(2), r(4), ALU.mult))
            own(v.tensor_reduce(r(3, 1), r(5), AX.X, ALU.max))
            own(v.tensor_scalar(r(5), r(5), r(3, 1), None, ALU.subtract))
            dve.sem_inc(soft_in, 1)
            dve.wait_ge(soft_out, 2)
            own(v.tensor_reduce(r(3, 1), r(6), AX.X, ALU.add))
            own(v.reciprocal(r(4, 1), r(3, 1)))
            own(v.tensor_scalar(r(7), r(6), r(4, 1), None, ALU.mult))
            for e in range(TOP):
                own(v.tensor_reduce(r(8 + e, 1), r(7), AX.X, ALU.max))
                own(v.tensor_scalar(r(10), r(7), r(8 + e, 1), float(NE), ALU.is_lt, ALU.mult))
                own(v.tensor_tensor(r(10), r(10), io, ALU.add))
                own(v.tensor_reduce(route[0:1, 13, e:e + 1], r(10), AX.X, ALU.min))
                if e == 0:
                    own(v.tensor_scalar(r(10), io, route[0:1, 13, e:e + 1], 4.0, ALU.is_equal, ALU.mult))
                    own(v.tensor_tensor(r(7), r(7), r(10), ALU.subtract))
            own(v.tensor_tensor(r(11, 1), r(9, 1), r(8, 1), ALU.subtract))
            dve.sem_inc(soft_in, 1)
            own(v.tensor_copy(route_i[0:1, 0:TOP], route[0:1, 13, 0:TOP]))
            dve.wait_ge(soft_out, 3)
            own(v.tensor_scalar(r(15, 1), r(12, 1), 1.0, None, ALU.add))
            own(v.reciprocal(route[0:1, 14, 0:1], r(15, 1)))
            own(v.tensor_tensor(route[0:1, 14, 1:2], route[0:1, 14, 0:1], r(12, 1), ALU.mult))
            dve.sem_inc(route_ready, 1)
            dve.wait_ge(wsel_made, 1)
            own(v.tensor_copy(wsel[:], bank[4][:, 0:TOP]))
            dve.wait_ge(e_loaded, 16 * NX)
            own(v.tensor_scalar(b2r[:, 2, :], b2r[:, 0, :], wsel[0:1, 0:1], None, ALU.mult))
            own(v.scalar_tensor_tensor(out=b2r[:, 2, :], in0=b2r[:, 1, :], scalar=wsel[0:1, 1:2], in1=b2r[:, 2, :],
                                       op0=ALU.mult, op1=ALU.add))
            dve.sem_inc(b2_ready, 1)
            for e in range(TOP):
                w = w2_sb[:, e].rearrange("p f d -> p (f d)")
                own(v.tensor_scalar(w, w, wsel[:, e:e + 1], None, ALU.mult))
            dve.wait_ge(b2_made, 1)
            own(v.tensor_copy(b2w, bank[6][:, 0:C]))
            dve.sem_inc(w2_scaled, 1)

            def finish(g, p, n):
                link = Chain(dve, y_own, g * (n_links))
                base = link.n
                wait(dve, out_stored[p], 16 * half(g, p) if not (isinstance(g, int) and g < 2) else 0)
                for j in range(n):
                    dve.wait_ge(y_made, g * FG + j + 1)
                    v.tensor_tensor(y[p][:, j, :], bank[4 + j][:, 0:C],
                                    acc[:, bass.ds((g * FG + j) * TW, C)], ALU.add).then_inc(y_added, 1)
                dve.wait_ge(y_added, g * FG + n)
                yy = y[p][:, 0:n, :]

                def wide(a):
                    return a.unsqueeze(1).to_broadcast([P, n, C])
                link(v.tensor_tensor(yy, yy, wide(b2w), ALU.add))
                for j in range(n):
                    ins = v.bn_stats(ystat[:, p, j, :], y[p][:, j, :])
                link(ins)
                ln_stats(link, 3 + g, ystat[:, p, 0:n, :], [ysc[:, p, k, 0:n] for k in range(4)], ysc[:, p, 4, 0:n], ysc[:, p, 5, 0:n])
                for j in range(n):
                    ins = v.tensor_scalar(y[p][:, j, :], y[p][:, j, :], ysc[:, p, 4, j:j + 1], ysc[:, p, 5, j:j + 1],
                                          ALU.subtract, ALU.mult)
                link(ins)
                link(v.tensor_tensor(yy, yy, wide(gb[:, 0, :]), ALU.mult))
                link(v.tensor_tensor(yy, yy, wide(gb[:, 1, :]), ALU.add))
                v.tensor_tensor(yy, yy, X[:, bass.ds(g * FG, n), :], ALU.add).then_inc(y_ready, 1)
            n_links = 12
            finish(0, 0, FG)
            finish(1, 1, FG)
            with dve.Fori(1, NG // 2) as i:
                finish(i * 2, 0, FG)
                finish(i * 2 + 1, 1, FG)
            finish(NG, 0, 1)


_IN = ['x', 'src', 'dst', 'L0_gnn_W', 'L0_gnn_attn_l', 'L0_gnn_attn_r', 'L0_gnn_bias', 'L0_mix_W_qkv', 'L0_mix_b_qkv',
       'L0_mix_W_out', 'L0_mix_b_out', 'L0_ffn_Wr', 'L0_ffn_br', 'L0_ffn_W1', 'L0_ffn_b1', 'L0_ffn_W2', 'L0_ffn_b2',
       'L0_ffn_gamma', 'L0_ffn_beta']


def kernel(**inputs):
    import numpy as np
    import concourse.bacc as bacc
    from concourse.bass_utils import run_bass_kernel_spmd

    nc = bacc.Bacc("TRN2", target_bir_lowering=False, num_devices=1)
    arrays, args = {}, []
    for name in _IN:
        a = np.ascontiguousarray(inputs[name])
        if name in ('src', 'dst'):
            rows = np.full(((U + 1) * EG,), 0 if name == 'src' else NONE, a.dtype)
            rows[:E] = a
            a = rows.reshape(U + 1, EG)
        arrays[name] = a
        args.append(nc.dram_tensor(name, a.shape, mybir.dt.from_np(a.dtype), kind="ExternalInput").ap())
    args.append(nc.dram_tensor("out", (N, C), F32, kind="ExternalOutput").ap())
    build(nc, *args)
    r = run_bass_kernel_spmd(nc, [arrays], core_ids=[0])
    return r.results[0]["out"]
```

```python
import math
from contextlib import ExitStack

import concourse.bass as bass
from concourse import mybir

F32 = mybir.dt.float32
BF16 = mybir.dt.bfloat16
I32 = mybir.dt.int32
ALU = mybir.AluOpType
ACT = mybir.ActivationFunctionType
AX = mybir.AxisListType
RMAX = bass.bass_isa.ReduceOp.max

P = 128
N = 6250
C = 256
H = 8
HC = C // H
KC = C // P
NT = -(-N // P)
LAST = N - (NT - 1) * P
E = 206250
G = 2
EG = G * P
U = -(-E // EG)
STEPS = U + NT - 1
SB = 4
TB = SB * G
NB = -(-STEPS // SB)
A4 = 4
R3 = 3
IT = NB // R3
KCH = -(-(NB * SB + SB) // P)
KS = KCH * P
UCH = -(-U // P)
NONE = 16384
TW = C + H
PARTS = 3
AW = 2 * H
NE = 8
F = 512
FC = F // P
TOP = 2
CAPACITY = float(math.ceil(N * 1.25 / NE))
SLOPE = 0.2
LN_EPS = 1e-5
EPS_DIV = 1e-7
EPS_NORM = 1e-12
TINY = 1e-30
SPREAD = 40.0
BIG = 1e30
XP = 7
NXP = NT // XP
XH = 4 * XP
XD = NT - 10
FG = 3
HB = [2, 3, 7, 2, 3, 7, 2, 3]
HB_BEFORE = [-1, 0, -2] + [f - 2 for f in range(3, len(HB))]
NG = NT // FG

A2_LAST = NT - 1
B_FIRST = A2_LAST + 1
B_LAST = B_FIRST + (NT - 1) // R3
assert NB == IT * R3 + 1 and NT == FG * NG + 1 and (NT - 1) % R3 == 0 and (NT - 1) % A4 == 0 and B_LAST < IT


def wait(eng, sem, count):
    if isinstance(count, int) and count <= 0:
        return
    eng.wait_ge(sem, count)


class Chain:

    def __init__(self, eng, sem, base=0):
        self.eng, self.sem, self.n = eng, sem, base

    def __call__(self, ins):
        ins.then_inc(self.sem, 1)
        self.n = self.n + 1
        self.eng.wait_ge(self.sem, self.n)


def build(nc, x, src, dst, W, attn_l, attn_r, gnn_bias, W_qkv, b_qkv, W_out, b_out,
          Wr, br, W1, b1, W2, b2, gamma, beta, out):
    h_tab = nc.dram_tensor("h_tab", [NT * P, TW], F32).ap()
    xn_d = nc.dram_tensor("xn_d", [NT, P, C], F32).ap()
    xnt_d = nc.dram_tensor("xnt_d", [NT, P, C], F32).ap()
    q2t_d = nc.dram_tensor("q2t_d", [NT, P, C], F32).ap()

    with ExitStack() as ctx:
        def sb(name, shape, dt=F32):
            return ctx.enter_context(nc.sbuf_tensor(name, shape, dt))

        def sem(name):
            return ctx.enter_context(nc.semaphore(name))

        def sems(name, n):
            return [sem(f"{name}{i}") for i in range(n)]

        bank = [ctx.enter_context(nc.psum_tensor(f"bank{i}", [P, 512], F32)) for i in range(8)]

        X = sb("X", [P, NT, C])
        acc = sb("acc", [P, NT * TW])
        WORK = R3 * TB * (TW + P + P // 2)
        work = sb("work", [P, WORK])
        a2c = sb("a2c", [P, NT * AW])
        a2p = sb("a2p", [P, NT * PARTS * AW], BF16)
        a1t = sb("a1t", [P, NT, H])
        cols = sb("cols", [P, 2 * KS * G])
        srcT = cols[:, 0:KS * G].bitcast(I32)
        dstT = cols[:, KS * G:2 * KS * G]
        t_acc = sb("t_acc", [1, KS], I32)
        t_a2c = sb("t_a2c", [1, KS], I32)
        idx = sb("idx", [P, R3, TB], I32)
        zb = sb("zb", [P, R3, 3, TB * H])
        ident = sb("ident", [P, P])
        iota_p = sb("iota_p", [P, P])
        ones = sb("ones", [P, P])
        wg = sb("wg", [P, KC, C + 2 * H])
        wqkv = sb("wqkv", [P, KC, 3 * C])
        kx = sb("kx", [P, KC, C + 2])
        wout = kx[:, :, 0:C]
        wvo = sb("wvo", [P, KC, C])
        kvw = sb("kvw", [P, KC, C])
        bqk = sb("bqk", [1, 2, C])
        rows = sb("rows", [1, 3, C])
        bv_col = sb("bv_col", [P, KC])
        bvo = sb("bvo", [P, C])
        bvx = kvw[:, 0, :].rearrange("p (k n) -> p k n", k=KC)
        stat = sb("stat", [P, NT, 6])
        sc = sb("sc", [P, 4, NT])
        nq = sb("nq", [P, NT])
        mean = sb("mean", [P, NT])
        rstd = sb("rstd", [P, NT])
        xn_c = sb("xn_c", [P, C + 1])
        xnt_c = sb("xnt_c", [P, KC, P])
        q2t_c = sb("q2t_c", [P, KC, P])
        q2 = sb("q2", [P, C])
        k2 = sb("k2", [P, C])
        sq = sb("sq", [P, C])
        qs = sb("qs", [P, 8])
        small = sb("small", [P, 32])
        amax = sb("amax", [P, 4, 2 * H])
        seg_i = sb("seg_i", [P, 1], I32)
        flag = sb("flag", [1, 1], I32)
        b2w = kvw[:, 0, :]
        wr_sb = sb("wr_sb", [P, KC, NE])
        mcol = sb("mcol", [P, KC])
        route = sb("route", [1, 16, NE])
        route_i = sb("route_i", [1, TOP], I32)
        wsel = sb("wsel", [P, TOP])
        b2r = rows

        mix_in = [(xnt_c[:].rearrange("p k n -> p (k n)"), q2t_c[:].rearrange("p k n -> p (k n)")),
                  (q2[:], k2[:]), (sq[:], xn_c[:, 0:C])]

        RW = TB * TW
        ring = [work[:, q * RW:(q + 1) * RW].rearrange("p (j w) -> p j w", w=TW) for q in range(R3)]
        s0 = R3 * RW
        hot = [work[:, s0 + q * TB * P:s0 + (q + 1) * TB * P].rearrange("p (j d) -> p j d", d=P)
               for q in range(R3)]
        s1 = s0 + R3 * TB * P
        hotT = [work[:, s1 + q * TB * P // 2:s1 + (q + 1) * TB * P // 2].bitcast(BF16).rearrange("p (j d) -> p j d", d=P)
                for q in range(R3)]
        seg_rows = work[:, s1 + TB * P // 2:s1 + TB * P // 2 + TW]
        seg_onehot = hot[0][:, 0, :]
        seg_z = hot[1]
        seg_diag = hot[2]
        seg_mask = q2[:, 0:P]
        o = 0

        def view(n):
            nonlocal o
            o += n
            return work[:, o - n:o]
        prod = view(KC * C).rearrange("p (k n) -> p k n", k=KC)
        attn = view(2 * C).rearrange("p (a n) -> p a n", a=2)
        wvT = view(KC * C).rearrange("p (k n) -> p k n", k=KC)
        kio = view(KS)
        cmp = view(KS)
        kcol = view(KCH)
        uio = view(UCH)
        fcol = view(UCH)
        ucol = view(KCH)
        tcol = view(KCH)
        lastd = view(UCH).bitcast(I32)
        lastt = view(UCH).bitcast(I32)
        ucol_i = view(KCH).bitcast(I32)
        iotai = cmp.bitcast(I32)
        urow = view(2 * KS).rearrange("p (a n) -> p a n", a=2)
        f_src = view(KCH * EG).rearrange("p (c e) -> p c e", e=EG)
        f_dst = view(KCH * EG).rearrange("p (c e) -> p c e", e=EG)
        g_src, g_dst = (f.bitcast(I32) for f in (f_src, f_dst))
        assert o <= WORK, (o, WORK)
        o -= 2 * KCH * EG
        xn_a = [view(C) for _ in range(A4)]
        xnt_a = [view(C).rearrange("p (k n) -> p k n", k=KC) for _ in range(A4)]
        h_a = [view(C + 2 * H) for _ in range(A4)]
        assert o <= WORK, (o, WORK)
        o = 0
        w1_sb = view(TOP * KC * F).rearrange("p (e k f) -> p e k f", e=TOP, k=KC)
        w2_sb = view(TOP * FC * C).rearrange("p (e f d) -> p e f d", e=TOP, f=FC)
        b1_sb = view(TOP * FC).rearrange("p (e f) -> p e f", e=TOP)
        x2s = [view(FG * C).rearrange("p (t c) -> p t c", t=FG) for _ in range(2)]
        x2t = [view(KC * FG * P).rearrange("p (k n) -> p k n", k=KC) for _ in range(2)]
        hT = [a.rearrange("p (f n) -> p f n", f=TOP * FC)
              for a in (view(TOP * FC * FG * P), cols[:, 0:TOP * FC * FG * P])]
        y = [wqkv[:].rearrange("p k n -> p (k n)")[:, i * FG * C:(i + 1) * FG * C].rearrange("p (t c) -> p t c", t=FG)
             for i in range(2)]
        gb = view(2 * C).rearrange("p (a c) -> p a c", a=2)
        ystat = view(2 * FG * 6).rearrange("p (a t s) -> p a t s", a=2, s=6)
        ysc = view(2 * 6 * FG).rearrange("p (a s t) -> p a s t", a=2, s=6)
        assert o <= WORK, (o, WORK)

        def acc_tile(t):
            return acc[:, t * TW:(t + 1) * TW]

        var_ready = sem("var_ready")
        root_ready = sem("root_ready")
        x_measured = sem("x_measured")
        x_loaded = sems("x_loaded", 7)
        w_loaded = sem("w_loaded")
        id_set = sem("id_set")
        iota_set = sem("iota_set")
        acc_zero = sem("acc_zero")
        dve_own = sem("dve_own")
        lastd_loaded = sem("lastd_loaded")
        lastd_clear = sem("lastd_clear")
        cmp_done = sem("cmp_done")
        u_counted = sem("u_counted")
        t_ready = sem("t_ready")
        ucol_ready = sem("ucol_ready")
        steps_gathered = sem("steps_gathered")
        f_ready = sem("f_ready")
        steps_turned = sem("steps_turned")
        steps_kept = sem("steps_kept")
        wg_ready = sem("wg_ready")
        wqk_ready = sem("wqk_ready")
        wvt_turned = sem("wvt_turned")
        wvt_kept = sem("wvt_kept")
        wvo_made = sem("wvo_made")
        wvo_kept = sem("wvo_kept")
        bvx_ready = sem("bvx_ready")
        crow_ready = sem("crow_ready")
        xn_ready = sem("xn_ready")
        xn_turned = sem("xn_turned")
        xnt_kept = sem("xnt_kept")
        h_made = sem("h_made")
        h_kept = sem("h_kept")
        a_kept = sem("a_kept")
        xn_stored = sems("xn_stored", A4)
        xnt_stored = sems("xnt_stored", A4)
        h_stored = sems("h_stored", A4)
        ext_ready = sem("ext_ready")
        ext_all = sem("ext_all")
        flag_ready = sem("flag_ready")
        c_ready = sem("c_ready")
        seg_idx = sem("seg_idx")
        seg_begun = sem("seg_begun")
        seg_in = sem("seg_in")
        seg_hot = sem("seg_hot")
        seg_spread = sem("seg_spread")
        seg_own = sem("seg_own")
        idx_ready = sem("idx_ready")
        batch_begun = sem("batch_begun")
        gathered = sems("gathered", R3)
        hot_ready = sem("hot_ready")
        hot_turned = sem("hot_turned")
        hotT_kept = sem("hotT_kept")
        a2c_picked = sem("a2c_picked")
        z_own = sem("z_own")
        u_ready = sem("u_ready")
        ex_ready = sem("ex_ready")
        msg_ready = sem("msg_ready")
        summed = sem("summed")
        added = sem("added")
        xnt_loaded = sem("xnt_loaded")
        xn_loaded = sem("xn_loaded")
        qk_made = sem("qk_made")
        roots = sem("roots")
        q2_squared = sem("q2_squared")
        q_own = sem("q_own")
        k2_ready = sem("k2_ready")
        k2_squared = sem("k2_squared")
        kx_added = sem("kx_added")
        q2_turned = sem("q2_turned")
        q2t_kept = sem("q2t_kept")
        q2t_stored = sem("q2t_stored")
        kx_kept = sem("kx_kept")
        kx_turned = sem("kx_turned")
        kxt_kept = sem("kxt_kept")
        kvw_made = sem("kvw_made")
        kvw_ready = sem("kvw_ready")
        mix_loaded = sems("mix_loaded", R3)
        mix_made = sem("mix_made")
        mix_added = sem("mix_added")
        msg_scaled = sem("msg_scaled")
        x1_made = sem("x1_made")
        x2_late = sem("x2_late")
        x2_scaled = sem("x2_scaled")
        x2_ready = sem("x2_ready")
        mean_made = sem("mean_made")
        mean_kept = sem("mean_kept")
        logits_made = sem("logits_made")
        soft_in = sem("soft_in")
        soft_out = sem("soft_out")
        route_ready = sem("route_ready")
        e_loaded = sem("e_loaded")
        wsel_made = sem("wsel_made")
        w2_scaled = sem("w2_scaled")
        b2_ready = sem("b2_ready")
        b2_made = sem("b2_made")
        x2_staged = sem("x2_staged")
        x2_turned = sem("x2_turned")
        x2t_kept = sem("x2t_kept")
        hid_made = sem("hid_made")
        hid_kept = sem("hid_kept")
        y_made = sem("y_made")
        y_added = sem("y_added")
        y_own = sem("y_own")
        y_ready = sem("y_ready")
        out_stored = sems("out_stored", 2)

        block = ctx.enter_context(nc.Block())

        xv = x[0:(NT - 1) * P, :].rearrange("(t p) c -> p t c", p=P)
        XC = (NT - 1) // 6
        NX = 4 * TOP + 2
        NW = 12

        def phases(eng, batch):
            def three(i, side, first=False):
                for q in range(R3):
                    batch(i, q, side, first)
            three(0, "qk")
            with eng.Fori(1, A2_LAST) as i:
                three(i, "qk")
            three(A2_LAST, "qk")
            yield
            three(B_FIRST, "mix", True)
            with eng.Fori(B_FIRST + 1, B_LAST) as i:
                three(i, "mix")
            three(B_LAST, "mix_end")
            with eng.Fori(B_LAST + 1, IT) as i:
                three(i, "")
            batch(IT, 0, "", False)

        def quads(tile):
            def run(eng):
                for p in range(A4):
                    tile(p, p, 0)
                with eng.Fori(1, NT // A4) as i:
                    for p in range(A4):
                        tile(i * A4 + p, p, i)
                tile(NT - 1, 0, NT // A4)
            return run

        def all_stored(eng, sems_):
            for p in range(A4):
                eng.wait_ge(sems_[p], 16 * ((NT - 1 - p) // A4 + 1))

        @block.sync
        def _(sp):
            sp.wait_ge(lastd_clear, 1)
            for c in range(UCH):
                n = min(P, U - c * P)
                sp.dma_start(lastd[0:n, c:c + 1], dst[c * P:c * P + n, EG - 1:EG],
                             allow_slow_non_contiguous=True).then_inc(lastd_loaded, 16)
            for c in range(6):
                sp.dma_start(X[:, c * XC:(c + 1) * XC, :], xv[:, c * XC:(c + 1) * XC, :]).then_inc(x_loaded[c], 16)
            sp.wait_ge(dve_own, 1)
            sp.dma_start(X[0:LAST, NT - 1, :], x[(NT - 1) * P:N, :]).then_inc(x_loaded[6], 16)

            def tile(t, p, n):
                sp.wait_ge(xn_ready, t + 1)
                sp.dma_start(xn_d[bass.ds(t, 1)].rearrange("o p c -> p (o c)"), xn_a[p]).then_inc(xn_stored[p], 16)
                sp.wait_ge(xnt_kept, t + 1)
                sp.dma_start(xnt_d[bass.ds(t, 1)].rearrange("o p c -> p (o c)"),
                             xnt_a[p].rearrange("p k n -> p (k n)")).then_inc(xnt_stored[p], 16)
                sp.wait_ge(h_kept, t + 1)
                sp.dma_start(h_tab[bass.ds(t * P, P), :], h_a[p][:, 0:TW]).then_inc(h_stored[p], 16)
            quads(tile)(sp)
            all_stored(sp, xn_stored)
            all_stored(sp, xnt_stored)

            def store_q2t(t):
                sp.wait_ge(q2t_kept, t + 1)
                sp.dma_start(q2t_d[bass.ds(t, 1)].rearrange("o p c -> p (o c)"),
                             q2t_c[:].rearrange("p k n -> p (k n)")).then_inc(q2t_stored, 16)

            def batch(i, q, side, first):
                if side == "qk" and q == 0:
                    wait(sp, qk_made, i)
                    sp.dma_start(xnt_c[:].rearrange("p k n -> p (k n)"),
                                 xnt_d[bass.ds(i, 1)].rearrange("o p c -> p (o c)")).then_inc(xnt_loaded, 16)
                    wait(sp, kx_added, i)
                    sp.dma_start(xn_c[:, 0:C], xn_d[bass.ds(i, 1)].rearrange("o p c -> p (o c)")).then_inc(xn_loaded, 16)
                    if not (isinstance(i, int) and i == 0):
                        store_q2t(i - 1)
                if side == "mix" or (side == "mix_end" and q == 0):
                    t = (i - B_FIRST) * R3 + q
                    if first and q == 0:
                        sp.wait_ge(q2t_stored, 16 * NT)
                        sp.wait_ge(q2_turned, NT)
                    wait(sp, mix_made, t - R3 + 1)
                    sp.dma_start(mix_in[q][0], xnt_d[bass.ds(t, 1)].rearrange("o p c -> p (o c)")).then_inc(mix_loaded[q], 16)
                    sp.dma_start(mix_in[q][1], q2t_d[bass.ds(t, 1)].rearrange("o p c -> p (o c)")).then_inc(mix_loaded[q], 16)
            for _ in phases(sp, batch):
                store_q2t(NT - 1)

            sp.wait_ge(route_ready, 1)
            sp.dma_start(gb[:, 0, :], gamma.unsqueeze(0).to_broadcast([P, C])).then_inc(e_loaded, 16)
            sp.dma_start(gb[:, 1, :], beta.unsqueeze(0).to_broadcast([P, C])).then_inc(e_loaded, 16)
            for e in range(TOP):
                n = sp.value_load(route_i[0:1, e:e + 1], min_val=0, max_val=NE - 1)
                sp.dma_start(w1_sb[:, e], W1[bass.ds(n, 1)].rearrange("o (k p) f -> p (o k) f", p=P)).then_inc(e_loaded, 16)
                sp.dma_start(w2_sb[:, e], W2[bass.ds(n, 1)].rearrange("o (f p) d -> p (o f) d", p=P)).then_inc(e_loaded, 16)
                sp.dma_start(b1_sb[:, e, :], b1[bass.ds(n, 1)].rearrange("o (f p) -> p (o f)", p=P),
                             allow_slow_non_contiguous=True).then_inc(e_loaded, 16)
                sp.dma_start(b2r[:, e, :], b2[bass.ds(n, 1)]).then_inc(e_loaded, 16)

            def store(g, p):
                sp.wait_ge(y_ready, g + 1)
                if isinstance(g, int) and g == NG:
                    sp.dma_start(out[g * FG * P:N, :], y[p][0:LAST, 0, :]).then_inc(out_stored[p], 16)
                    return
                sp.dma_start(out[bass.ds(g * FG * P, FG * P), :].rearrange("(t p) c -> p t c", p=P),
                             y[p][:, :, :]).then_inc(out_stored[p], 16)
            with sp.Fori(0, NG // 2) as i:
                store(i * 2, 0)
                store(i * 2 + 1, 1)
            store(NG, 0)
            sp.wait_ge(out_stored[0], 16 * (NG // 2 + 1))
            sp.wait_ge(out_stored[1], 16 * (NG // 2))

        @block.gpsimd
        def _(pool):
            nc.gpsimd.memset(ident[:], 0.0).then_inc(id_set, 1)
            nc.gpsimd.memset(ones[:], 1.0).then_inc(id_set, 1)
            pool.wait_ge(id_set, 1)
            nc.gpsimd.affine_select(out=ident[:], in_=ident[:], compare_op=ALU.not_equal, fill=1.0, base=0,
                                    pattern=[[-1, P]], channel_multiplier=1).then_inc(id_set, 1)
            nc.gpsimd.iota(iotai, pattern=[[1, KS]], base=0, channel_multiplier=0).then_inc(iota_set, 1)
            nc.gpsimd.iota(kcol.bitcast(I32), pattern=[[P, KCH]], base=0, channel_multiplier=1).then_inc(iota_set, 1)
            nc.gpsimd.iota(uio.bitcast(I32), pattern=[[P, UCH]], base=0, channel_multiplier=1).then_inc(iota_set, 1)
            nc.gpsimd.memset(acc[:], 0.0).then_inc(acc_zero, 1)

            pool.wait_ge(ucol_ready, 1)
            for c in range(KCH):
                for g, table in ((g_src, src), (g_dst, dst)):
                    nc.gpsimd.indirect_dma_start(
                        out=g[:, c, :], out_offset=None, in_=table,
                        in_offset=bass.IndirectOffsetOnAxis(ap=ucol_i[:, c:c + 1], axis=0)).then_inc(steps_gathered, 16)
            pool.wait_ge(ext_ready, 1)
            nc.gpsimd.partition_all_reduce(amax[:, 1, :], amax[:, 0, :], P, RMAX).then_inc(ext_all, 1)

            for stored in (h_stored, xn_stored, xnt_stored):
                all_stored(pool, stored)
            pool.wait_ge(wvo_kept, 1)

            def batch(i, q, side, first):
                b = i * R3 + q
                pool.wait_ge(idx_ready, b + 1)
                wait(pool, summed, SB * (b - R3 + 1))
                pool.sem_inc(batch_begun, 1)
                for j in range(TB):
                    nc.gpsimd.indirect_dma_start(
                        out=ring[q][:, j, :], out_offset=None, in_=h_tab,
                        in_offset=bass.IndirectOffsetOnAxis(ap=idx[:, q, j:j + 1], axis=0)).then_inc(gathered[q], 16)
                if isinstance(i, int) and i == 0 and q == R3 - 1:
                    pool.wait_ge(flag_ready, 1)
                    wide = pool.value_load(flag[0:1, 0:1], min_val=0, max_val=1)
                    with pool.If(wide > 0):
                        seg_gathers()

            def seg_gathers():
                with pool.Fori(0, NB * TB) as j:
                    pool.wait_ge(seg_hot, j + 1)
                    nc.gpsimd.tensor_copy(seg_i[:], srcT[:, bass.ds(j, 1)]).then_inc(seg_idx, 1)
                    pool.wait_ge(seg_idx, j + 1)
                    pool.sem_inc(seg_begun, 1)
                    nc.gpsimd.indirect_dma_start(
                        out=seg_rows, out_offset=None, in_=h_tab,
                        in_offset=bass.IndirectOffsetOnAxis(ap=seg_i[:, 0:1], axis=0)).then_inc(seg_in, 16)
                pool.wait_ge(seg_hot, NB * TB + 1)

            for _ in phases(pool, batch):
                pass

            def stage(g, p, n):
                wait(pool, x2_turned, g - 1)
                a3 = acc[:].rearrange("p (t w) -> p t w", w=TW)
                nc.gpsimd.tensor_copy(x2s[p][:, 0:n, :], a3[:, bass.ds(g * FG, n), 0:C]).then_inc(x2_staged, 1)

            pool.wait_ge(x2_ready, XD)
            pool.wait_ge(x2_late, NT - XD)
            stage(0, 0, FG)
            stage(1, 1, FG)
            with pool.Fori(1, NG // 2) as i:
                stage(i * 2, 0, FG)
                stage(i * 2 + 1, 1, FG)
            stage(NG, 0, 1)

        @block.scalar
        def _(act):
            for dst_ap, src_ap in (
                (wg[:, :, 0:C], W.rearrange("(k p) n -> p k n", p=P)),
                (attn[:, 0, :], attn_l.rearrange("a h j -> a (h j)").to_broadcast([P, C])),
                (attn[:, 1, :], attn_r.rearrange("a h j -> a (h j)").to_broadcast([P, C])),
                (wqkv[:], W_qkv.rearrange("(k p) n -> p k n", p=P)),
                (wout[:], W_out.rearrange("(k p) n -> p k n", p=P)),
                (bqk[:].rearrange("a k n -> a (k n)"), b_qkv[0:2 * C].unsqueeze(0)),
                (bv_col[:, 0:1], b_qkv[2 * C:2 * C + P].unsqueeze(1)),
                (bv_col[:, 1:2], b_qkv[2 * C + P:3 * C].unsqueeze(1)),
                (rows[:, 0, :], gnn_bias.unsqueeze(0)),
                (rows[:, 1, :], b_out.unsqueeze(0)),
                (wr_sb[:], Wr.rearrange("(k p) n -> p k n", p=P)),
                (route[:, 0, :], br.unsqueeze(0)),
            ):
                act.dma_start(dst_ap, src_ap).then_inc(w_loaded, 16)
            def root(n, r):
                act.wait_ge(var_ready, n + 1)
                nc.scalar.activation(r, r, ACT.Sqrt).then_inc(root_ready, 1)

            act.wait_ge(wvt_turned, 1)
            nc.scalar.copy(wvT.rearrange("p k n -> p (k n)"), bank[5][:]).then_inc(wvt_kept, 1)

            for c in range(KCH):
                act.wait_ge(steps_turned, c + 1)
                pt = bank[6 + c % 2][:].rearrange("p (a g k) -> p a k g", a=2, g=G)
                nc.scalar.copy(srcT[:, c * P * G:(c + 1) * P * G].rearrange("p (k g) -> p k g", g=G), pt[:, 0]).then_inc(steps_kept, 1)
                nc.scalar.copy(dstT[:, c * P * G:(c + 1) * P * G].rearrange("p (k g) -> p k g", g=G), pt[:, 1]).then_inc(steps_kept, 1)
            act.wait_ge(steps_kept, 2 * KCH)


            root(0, rstd[:])

            def turned_xn(t, p, n):
                act.wait_ge(xn_turned, t + 1)
                wait(act, h_made, t - A4 + 1)
                wait(act, xnt_stored[p], n * 16)
                nc.scalar.copy(xnt_a[p].rearrange("p k n -> p (k n)"), bank[p % 2][:, 0:C]).then_inc(xnt_kept, 1)

            def tile(t, p, n):
                if not (isinstance(t, int) and t == NT - 1):
                    turned_xn(t + 1, (p + 1) % A4, n + (p + 1) // A4)
                act.wait_ge(h_made, t + 1)
                wait(act, h_stored[p], n * 16)
                wait(act, a_kept, t - A4 + 1)
                nc.scalar.copy(h_a[p], bank[2 + p % 2][:, 0:C + 2 * H]).then_inc(h_kept, 1)
            turned_xn(0, 0, 0)
            quads(tile)(act)

            def index(b, q):
                nc.scalar.copy(idx[:, q, :], srcT[:, bass.ds(b * TB, TB)]).then_inc(idx_ready, 1)

            def turned(b, q):
                wait(act, a2c_picked, b - R3 + 1)
                for k in range(2):
                    act.wait_ge(hot_turned, b * 2 + k + 1)
                    nc.scalar.copy(hotT[q][:, k * 4:k * 4 + 4, :].rearrange("p j d -> p (j d)"),
                                   bank[k][:]).then_inc(hotT_kept, 1)

            def weights(b, q):
                act.wait_ge(u_ready, b + 1)
                nc.scalar.activation(ring[q][:, :, C:TW], zb[:, q, 0, :].rearrange("p (j h) -> p j h", h=H),
                                     ACT.Exp).then_inc(ex_ready, 1)

            for q in range(R3):
                index(q, q)
            act.wait_ge(hot_ready, 1)
            turned(0, 0)
            weights(0, 0)

            def batch(i, q, side, first):
                b = i * R3 + q
                last = isinstance(i, int) and i == IT
                if not last:
                    act.wait_ge(gathered[q], 16 * TB * (i + 1))
                    index(b + R3, q)
                    turned(b + 1, (q + 1) % R3)
                    weights(b + 1, (q + 1) % R3)
                if side == "qk":
                    if q == 1:
                        act.wait_ge(qk_made, i + 1)
                        wait(act, q2_turned, i)
                        nc.scalar.activation(q2[:], bank[5][:, 0:C], ACT.Square, accum_out=qs[:, 0:1]).then_inc(q2_squared, 1)
                        nc.scalar.activation(k2[:], bank[5][:, C:2 * C], ACT.Square, accum_out=qs[:, 1:2]).then_inc(q2_squared, 1)
                    if q == 2:
                        act.wait_ge(k2_ready, i + 1)
                        nc.scalar.activation(sq[:], q2[:], ACT.Square, accum_out=nq[:, bass.ds(i, 1)]).then_inc(k2_squared, 1)
                        act.wait_ge(k2_squared, i * 2 + 1)
                        nc.scalar.activation(sq[:], k2[:], ACT.Square).then_inc(k2_squared, 1)
                if (side == "qk" and q == 0 and not (isinstance(i, int) and i == 0)):
                    keep_q2t(i - 1)

            def keep_q2t(t):
                act.wait_ge(q2_turned, t + 1)
                wait(act, q2t_stored, 16 * t)
                nc.scalar.copy(q2t_c[:].rearrange("p k n -> p (k n)"), bank[5][:, 0:C]).then_inc(q2t_kept, 1)

            for _ in phases(act, batch):
                keep_q2t(NT - 1)
                act.wait_ge(kx_turned, 1)
                nc.scalar.copy(wqkv[:].rearrange("p k n -> p (k n)")[:, 0:2 * C], bank[5][:]).then_inc(kxt_kept, 1)
                act.wait_ge(k2_squared, 2 * NT)
                nc.scalar.activation(nq[:], nq[:], ACT.Sqrt).then_inc(roots, 1)
                act.wait_ge(kx_kept, 1)
                nc.scalar.activation(small[:, 16:16 + KC], kx[:, :, C + 1], ACT.Sqrt).then_inc(roots, 1)

            for n, (a, e, e_act) in enumerate(((0, XH, XH), (XH, NT, XD))):
                root(1 + n, rstd[:, a:e])
                act.wait_ge(x2_scaled, n + 1)
                for t in range(a, e_act):
                    nc.scalar.activation(acc_tile(t)[:, 0:C], X[:, t, :], ACT.Identity, bias=sc[:, 3, t:t + 1],
                                         scale=rstd[:, t:t + 1]).then_inc(x2_ready, 1)
            act.wait_ge(mean_made, 1)
            nc.scalar.copy(sq[0:1, :], bank[0][0:1, 0:C]).then_inc(mean_kept, 1)
            act.wait_ge(mean_made, 2)
            nc.scalar.copy(mcol[:], bank[1][:, 16:16 + KC]).then_inc(mean_kept, 1)
            act.wait_ge(soft_in, 1)
            nc.scalar.activation(route[:, 2, :], route[:, 1, :], ACT.Exp).then_inc(soft_out, 1)
            act.wait_ge(soft_in, 2)
            nc.scalar.activation(route[:, 6, :], route[:, 5, :], ACT.Exp).then_inc(soft_out, 1)
            act.wait_ge(soft_in, 3)
            nc.scalar.activation(route[:, 12, 0:1], route[:, 11, 0:1], ACT.Exp).then_inc(soft_out, 1)

            def x2_out(g, p, n):
                act.wait_ge(x2_turned, g + 1)
                for k in range(KC):
                    nc.scalar.copy(x2t[p][:, k, 0:n * P], bank[k][:, 0:n * P]).then_inc(x2t_kept, 1)

            def hidden(g, p, n, roots=True):
                for f in range(TOP * FC):
                    if f == FC and roots:
                        root(g + 1, ysc[:, p, 5, :])
                    act.wait_ge(hid_made, g * (TOP * FC) + f + 1)
                    nc.scalar.activation(hT[p][:, f, 0:n * P], bank[HB[f]][:, 0:n * P], ACT.Gelu,
                                         bias=b1_sb[:, f // FC, f % FC:f % FC + 1]).then_inc(hid_kept, 1)
            x2_out(0, 0, FG)
            act.wait_ge(e_loaded, 16 * NX)
            hidden(0, 0, FG, False)
            x2_out(1, 1, FG)
            hidden(1, 1, FG, False)
            with act.Fori(1, NG // 2) as i:
                for p in range(2):
                    x2_out(i * 2 + p, p, FG)
                    hidden(i * 2 + p, p, FG)
            x2_out(NG, 0, 1)
            hidden(NG, 0, 1)
            root(NG + 2, ysc[:, 1, 5, :])
            root(NG + 3, ysc[:, 0, 5, 0:1])

        @block.tensor
        def _(pe):
            mm = nc.tensor.matmul
            turn = nc.tensor.transpose
            pe.wait_ge(id_set, 3)
            pe.wait_ge(cmp_done, 1)
            for c in range(KCH):
                mm(bank[6][:, c:c + 1], cmp[:, c * P:(c + 1) * P], ones[:, 0:1], start=True, stop=True)
            for k in range(2):
                ins = mm(bank[7 - k][0:1, 8:8 + KS // 2], ones[:, 0:1], cmp[:, k * (KS // 2):(k + 1) * (KS // 2)],
                         start=True, stop=True)
            ins.then_inc(u_counted, 1)

            pe.wait_ge(w_loaded, 16 * NW)
            for d in range(KC):
                for j in range(KC):
                    ins = turn(bank[5][:, (d * KC + j) * P:(d * KC + j + 1) * P],
                               wqkv[:, j, 2 * C + d * P:2 * C + (d + 1) * P], ident[:])
            ins.then_inc(wvt_turned, 1)
            pe.wait_ge(wvt_kept, 1)
            for j in range(KC):
                for d in range(KC):
                    mm(bank[4][:, j * C:(j + 1) * C], wvT[:, d, j * P:(j + 1) * P], wout[:, d, :],
                       start=(d == 0), stop=(d == KC - 1))
            pe.wait_ge(bvx_ready, 1)
            for d in range(KC):
                ins = mm(bank[3][:, 0:C], bvx[:, d, :], wout[:, d, :], start=(d == 0), stop=(d == KC - 1))
            ins.then_inc(wvo_made, 1)

            pe.wait_ge(f_ready, 2)
            for c in range(KCH):
                wait(pe, steps_kept, 2 * (c - 1))
                for a, f in enumerate((f_src, f_dst)):
                    for g in range(G):
                        o_ = (a * G + g) * P
                        ins = turn(bank[6 + c % 2][:, o_:o_ + P], f[:, c, g * P:(g + 1) * P], ident[:])
                ins.then_inc(steps_turned, 1)

            pe.wait_ge(wg_ready, 1)
            pe.wait_ge(wvo_kept, 1)

            def xn_in(t, p):
                pe.wait_ge(xn_ready, t + 1)
                wait(pe, xnt_kept, t - 1)
                for k in range(KC):
                    ins = turn(bank[p % 2][:, k * P:(k + 1) * P], xn_a[p][:, k * P:(k + 1) * P], ident[:])
                ins.then_inc(xn_turned, 1)

            def tile(t, p, n):
                if not (isinstance(t, int) and t == NT - 1):
                    xn_in(t + 1, (p + 1) % A4)
                pe.wait_ge(xnt_kept, t + 1)
                wait(pe, h_kept, t - 1)
                for k in range(KC):
                    ins = mm(bank[2 + p % 2][:, 0:C + 2 * H], xnt_a[p][:, k, :], wg[:, k, :], start=(k == 0), stop=(k == KC - 1))
                ins.then_inc(h_made, 1)
            xn_in(0, 0)
            quads(tile)(pe)


            def turned(b, q):
                pe.wait_ge(hot_ready, b + 1)
                for k in range(2):
                    wait(pe, hotT_kept, b * 2 + k - 1)
                    for j in range(4):
                        ins = turn(bank[k][:, j * P:(j + 1) * P], hot[q][:, k * 4 + j, :], ident[:])
                    ins.then_inc(hot_turned, 1)

            def pick(b, q):
                _, ts = nc.values_load_multi_w_load_instructions(
                    t_a2c[0:1, bass.ds(b * SB, SB)], engines=[mybir.EngineType.PE], min_val=0,
                    max_val=(NT - 1) * PARTS * AW, skip_runtime_bounds_check_because="steps' node tiles are clamped")
                pe.wait_ge(hotT_kept, b * 2 + 2)
                wait(pe, u_ready, b)
                for j in range(TB):
                    for k in range(PARTS):
                        ins = mm(bank[2][:, j * AW:(j + 1) * AW], hotT[q][:, j, :],
                                 a2p[:, bass.ds(ts[j // G] + k * AW, AW)], start=(k == 0), stop=(k == PARTS - 1))
                ins.then_inc(a2c_picked, 1)

            pe.wait_ge(t_ready, 1)
            pe.wait_ge(a_kept, NT)
            pe.wait_ge(h_kept, NT)
            pe.wait_ge(steps_kept, 2 * KCH)
            pe.wait_ge(flag_ready, 1)
            wide = pe.value_load(flag[0:1, 0:1], min_val=0, max_val=1)
            with pe.If(wide > 0):
                with pe.Fori(0, NB * TB) as j:
                    pe.wait_ge(seg_hot, j + 2)
                    turn(bank[0][:, 0:P], seg_onehot, ident[:])
                    for k in range(2):
                        ins = mm(bank[3 + k][:], ones[:], seg_diag[:, k * 4:k * 4 + 4, :].rearrange("p h e -> p (h e)"),
                                 start=True, stop=True)
                    ins.then_inc(seg_spread, 1)
                pe.wait_ge(seg_spread, NB * TB)
            turned(0, 0)
            pe.wait_ge(c_ready, 1)
            pick(0, 0)
            pe.wait_ge(wqk_ready, 1)

            def batch(i, q, side, first):
                b = i * R3 + q
                last = isinstance(i, int) and i == IT
                if not last:
                    turned(b + 1, (q + 1) % R3)
                for s in range(SB):
                    if s % 2 == 0:
                        pe.wait_ge(msg_ready, b * 2 + s // 2 + 1)
                    if s == 2 and not last:
                        pick(b + 1, (q + 1) % R3)
                    wait(pe, added, b * SB + s - 1)
                    for g in range(G):
                        ins = mm(bank[3 + s % 2][:, 0:TW], hot[q][:, s * G + g, :], ring[q][:, s * G + g, :],
                                 start=(g == 0), stop=(g == G - 1))
                    ins.then_inc(summed, 1)
                if side == "qk":
                    if q == 0:
                        pe.wait_ge(xnt_loaded, (i + 1) * 16)
                        wait(pe, q2t_kept, i)
                        mm(bank[5][:], ones[0:1, :], bqk[:].rearrange("a k n -> a (k n)"), start=True, stop=False)
                        for k in range(KC):
                            ins = mm(bank[5][:], xnt_c[:, k, :], wqkv[:, k, 0:2 * C], start=False, stop=(k == KC - 1))
                        ins.then_inc(qk_made, 1)
                    if q == 2:
                        end = isinstance(i, int) and i == A2_LAST
                        begin = isinstance(i, int) and i == 0
                        n = LAST if end else P
                        pe.wait_ge(xn_loaded, (i + 1) * 16)
                        pe.wait_ge(k2_squared, i * 2 + 2)
                        for k in range(KC):
                            mm(bank[6 + k][:, 0:C + 1], k2[0:n, k * P:(k + 1) * P], xn_c[0:n, :],
                               start=begin, stop=end, skip_group_check=True)
                            ins = mm(bank[6 + k][:, C + 1:C + 2], sq[0:n, k * P:(k + 1) * P], ones[0:n, 0:1],
                                     start=False, stop=end, skip_group_check=True)
                        ins.then_inc(kx_added, 1)
                        for k in range(KC):
                            ins = turn(bank[5][:, k * P:(k + 1) * P], q2[:, k * P:(k + 1) * P], ident[:])
                        ins.then_inc(q2_turned, 1)
                if side == "mix" or (side == "mix_end" and q == 0):
                    t = (i - B_FIRST) * R3 + q
                    if first and q == 0:
                        pe.wait_ge(kvw_ready, 1)
                        pe.wait_ge(crow_ready, 1)
                    pe.wait_ge(mix_loaded[q], (i - B_FIRST + 1) * 32)
                    xt, q2t = (a.rearrange("p (k n) -> p k n", k=KC) for a in mix_in[q])
                    wait(pe, mix_added, t * 2)
                    mm(bank[5][:, 0:C], ones[0:1, :], rows[0:1, 2, :], start=True, stop=False)
                    for k in range(KC):
                        mm(bank[5][:, 0:C], xt[:, k, :], wvo[:, k, :], start=False, stop=(k == KC - 1))
                    for k in range(KC):
                        ins = mm(bank[6][:, 0:C], q2t[:, k, :], kvw[:, k, :], start=(k == 0), stop=(k == KC - 1))
                    ins.then_inc(mix_made, 1)

            for _ in phases(pe, batch):
                pe.wait_ge(kx_kept, 1)
                pe.wait_ge(q2t_kept, NT)
                for j in range(KC):
                    for k in range(KC):
                        ins = turn(bank[5][:, (j * KC + k) * P:(j * KC + k + 1) * P], kx[:, k, j * P:(j + 1) * P], ident[:])
                ins.then_inc(kx_turned, 1)
                pe.wait_ge(kxt_kept, 1)
                kxT = wqkv[:].rearrange("p k n -> p (k n)")
                for k in range(KC):
                    for j in range(KC):
                        ins = mm(bank[6 + k][:, 0:C], kxT[:, (j * KC + k) * P:(j * KC + k + 1) * P], wvo[:, j, :],
                                 start=(j == 0), stop=(j == KC - 1))
                ins.then_inc(kvw_made, 1)

            def x2_in(g, p, n):
                pe.wait_ge(x2_staged, g + 1)
                wait(pe, x2t_kept, g * KC)
                for k in range(KC):
                    for j in range(n):
                        ins = turn(bank[k][:, j * P:(j + 1) * P], x2s[p][:, j, k * P:(k + 1) * P], ident[:])
                ins.then_inc(x2_turned, 1)

            for t in range(NT):
                n = LAST if t == NT - 1 else P
                if t < XD:
                    pe.wait_ge(x2_ready, t + 1)
                else:
                    pe.wait_ge(x2_late, t - XD + 1)
                ins = mm(bank[0][0:1, 0:C], ones[0:n, 0:1], acc_tile(t)[0:n, 0:C], start=(t == 0), stop=(t == NT - 1))
            ins.then_inc(mean_made, 1)
            pe.wait_ge(mean_kept, 1)
            for k in range(KC):
                ins = mm(bank[1][:, 16 + k:17 + k], sq[0:1, k * P:(k + 1) * P], ones[0:1, 0:1], start=True, stop=True)
            ins.then_inc(mean_made, 1)
            pe.wait_ge(mean_kept, 2)
            for k in range(KC):
                ins = mm(bank[1][0:1, 0:NE], mcol[:, k:k + 1], wr_sb[:, k, :], start=(k == 0), stop=(k == KC - 1))
            ins.then_inc(logits_made, 1)
            pe.wait_ge(soft_in, 1)
            x2_in(0, 0, FG)
            pe.wait_ge(route_ready, 1)
            mm(bank[4][:, 0:TOP], ones[0:1, :], route[0:1, 14, 0:TOP], start=True, stop=True).then_inc(wsel_made, 1)
            pe.wait_ge(b2_ready, 1)
            mm(bank[6][:, 0:C], ones[0:1, :], b2r[0:1, 2, :], start=True, stop=True).then_inc(b2_made, 1)

            def hidden(g, p, n):
                pe.wait_ge(x2t_kept, (g + 1) * KC)
                for f in range(TOP * FC):
                    before = HB_BEFORE[f]
                    wait(pe, hid_kept, g * (TOP * FC) + before)
                    for k in range(KC):
                        ins = mm(bank[HB[f]][:, 0:n * P], w1_sb[:, f // FC, k, (f % FC) * P:(f % FC + 1) * P],
                                 x2t[p][:, k, 0:n * P], start=(k == 0), stop=(k == KC - 1))
                    ins.then_inc(hid_made, 1)

            def down(g, p, n):
                pe.wait_ge(hid_kept, (g + 1) * (TOP * FC))
                for j in range(n):
                    wait(pe, y_added, g * FG + j - FG + 1)
                    for f in range(TOP * FC):
                        ins = mm(bank[4 + j][:, 0:C], hT[p][:, f, j * P:(j + 1) * P], w2_sb[:, f // FC, f % FC, :],
                                 start=(f == 0), stop=(f == TOP * FC - 1))
                    ins.then_inc(y_made, 1)
            pe.wait_ge(e_loaded, 16 * NX)
            hidden(0, 0, FG)
            x2_in(1, 1, FG)
            pe.wait_ge(w2_scaled, 1)
            for g in range(2):
                hidden(g + 1, 1 - g, FG)
                x2_in(g + 2, g, FG)
                down(g, g, FG)
            with pe.Fori(1, NG // 2 - 1) as i:
                for p in range(2):
                    hidden(i * 2 + p + 1, 1 - p, FG)
                    x2_in(i * 2 + p + 2, p, FG)
                    down(i * 2 + p, p, FG)
            hidden(NG - 1, 1, FG)
            x2_in(NG, 0, 1)
            down(NG - 2, 0, FG)
            hidden(NG, 0, 1)
            down(NG - 1, 1, FG)
            down(NG, 0, 1)

        @block.vector
        def _(dve):
            v = nc.vector
            own = Chain(dve, dve_own)

            def ln_stats(link, n, st, s, m, r):
                v.tensor_tensor(s[1], st[:, :, 2], st[:, :, 5], ALU.add).then_inc(link.sem, 1)
                v.tensor_tensor(s[2], st[:, :, 1], st[:, :, 4], ALU.add).then_inc(link.sem, 1)
                link.n = link.n + 2
                link(v.tensor_tensor(s[0], st[:, :, 1], st[:, :, 4], ALU.subtract))
                link(v.scalar_tensor_tensor(out=s[0], in0=s[0], scalar=C / 4.0, in1=s[0], op0=ALU.mult, op1=ALU.mult))
                v.tensor_scalar(m, s[2], 0.5, None, ALU.mult).then_inc(link.sem, 1)
                link.n = link.n + 1
                link(v.tensor_tensor(s[1], s[1], s[0], ALU.add))
                v.tensor_scalar(r, s[1], 1.0 / C, LN_EPS, ALU.mult, ALU.add).then_inc(var_ready, 1)
                dve.wait_ge(root_ready, n + 1)
                link(v.reciprocal(r, r))

            own(v.memset(X[:, NT - 1, :], 0.0))
            v.memset(lastd, 1 << 20).then_inc(lastd_clear, 1)

            dve.wait_ge(iota_set, 3)
            v.tensor_copy(iota_p[:], iotai[:, 0:P])
            v.tensor_copy(kio, iotai).then_inc(dve_own, 1)
            own.n += 1
            own(v.tensor_copy(ucol, kcol.bitcast(I32)))
            v.tensor_copy(kcol, ucol)
            own(v.tensor_copy(tcol[:, 0:UCH], uio.bitcast(I32)))
            dve.wait_ge(lastd_loaded, 16 * UCH)
            dve.wait_ge(lastd_clear, 1)
            own(v.tensor_scalar(lastt, lastd, 7, None, ALU.arith_shift_right))
            own(v.tensor_scalar(fcol, lastt, float(NT - 1), None, ALU.min))
            own(v.tensor_tensor(fcol, fcol, tcol[:, 0:UCH], ALU.add))
            own(v.tensor_scalar(cmp, kio, fcol[:, 0:1], None, ALU.is_gt))
            for c in range(1, UCH):
                ins = v.scalar_tensor_tensor(out=cmp, in0=kio, scalar=fcol[:, c:c + 1], in1=cmp, op0=ALU.is_gt, op1=ALU.add)
                own(ins)
            dve.sem_inc(cmp_done, 1)

            def measure(c):
                dve.wait_ge(x_loaded[c], 16)
                for t in range(c * XC, min((c + 1) * XC, NT)):
                    v.bn_stats(stat[:, t, :], X[:, t, :]).then_inc(x_measured, 1)

            measure(0)
            dve.wait_ge(u_counted, 1)
            v.tensor_scalar(ucol, bank[6][:, 0:KCH], float(U), None, ALU.min).then_inc(dve_own, 1)
            own(v.tensor_copy(urow[0:1, 0, 0:KS // 2], bank[7][0:1, 8:8 + KS // 2]))
            own.n += 1
            own(v.tensor_copy(urow[0:1, 0, KS // 2:KS], bank[6][0:1, 8:8 + KS // 2]))
            v.tensor_copy(ucol_i, ucol).then_inc(ucol_ready, 1)
            own(v.tensor_tensor(tcol, kcol, bank[6][:, 0:KCH], ALU.subtract))
            own(v.tensor_scalar(tcol, tcol, float(NT - 1), float(P), ALU.min, ALU.mult))
            own(v.tensor_tensor(urow[0:1, 1, :], kio[0:1, :], urow[0:1, 0, :], ALU.subtract))
            own(v.tensor_scalar(urow[0:1, 1, :], urow[0:1, 1, :], float(NT - 1), None, ALU.min))
            v.tensor_scalar(t_acc[:], urow[0:1, 1, :], float(TW), None, ALU.mult).then_inc(dve_own, 1)
            own.n += 1
            own(v.tensor_scalar(t_a2c[:], urow[0:1, 1, :], float(PARTS * AW), None, ALU.mult))
            dve.sem_inc(t_ready, 1)

            measure(1)

            dve.wait_ge(w_loaded, 16 * NW)
            for a in range(2):
                for k in range(KC):
                    ins = v.tensor_tensor(prod[:, k, :], wg[:, k, 0:C], attn[:, a, :], ALU.mult)
                    ins.then_inc(dve_own, 1)
                    own.n += 1
                dve.wait_ge(dve_own, own.n)
                for k in range(KC):
                    ins = v.tensor_reduce(wg[:, k, C + a * H:C + (a + 1) * H], prod[:, k, :].rearrange("p (h j) -> p h j", h=H),
                                          AX.X, ALU.add)
                    own(ins)
            dve.sem_inc(wg_ready, 1)

            own(v.tensor_copy(bvx, bv_col[:].unsqueeze(2).to_broadcast([P, KC, P])))
            dve.sem_inc(bvx_ready, 1)

            measure(2)

            dve.wait_ge(wvo_made, 1)
            own(v.tensor_copy(wvo[:].rearrange("p k n -> p (k n)"), bank[4][:]))
            own(v.tensor_copy(bvo[:], bank[3][:, 0:C]))
            own(v.tensor_tensor(rows[:, 2, :], rows[:, 0, :], rows[:, 1, :], ALU.add))
            own(v.tensor_tensor(rows[:, 2, :], rows[:, 2, :], bvo[0:1, :], ALU.add))
            dve.sem_inc(wvo_kept, 1)
            dve.sem_inc(crow_ready, 1)

            measure(3)

            dve.wait_ge(steps_gathered, 16 * 2 * KCH)
            v.tensor_copy(f_src.rearrange("p c e -> p (c e)"), g_src.rearrange("p c e -> p (c e)")).then_inc(f_ready, 1)
            for c in range(KCH):
                ins = v.tensor_scalar(f_dst[:, c, :], g_dst[:, c, :], tcol[:, c:c + 1], None, ALU.subtract)
            ins.then_inc(f_ready, 1)


            for c in range(4, 7):
                measure(c)
            dve.wait_ge(x_measured, NT)
            ln_stats(own, 0, stat, [sc[:, n, :] for n in range(4)], mean[:], rstd[:])

            dve.wait_ge(steps_kept, 2 * KCH)
            def tile(t, p, n):
                wait(dve, xn_turned, t - A4 + 1)
                wait(dve, xn_stored[p], n * 16)
                v.tensor_scalar(xn_a[p].unsqueeze(1), X[:, bass.ds(t, 1), :], mean[:, bass.ds(t, 1)],
                                rstd[:, bass.ds(t, 1)], ALU.subtract, ALU.mult).then_inc(xn_ready, 1)
                if not (isinstance(t, int) and t < 2):
                    keep(t - 2, (p - 2) % A4)

            def keep(t, p):
                dve.wait_ge(h_kept, t + 1)
                v.tensor_copy(a1t[:, bass.ds(t, 1), :], h_a[p][:, C:C + H].unsqueeze(1))
                v.tensor_copy(a2c[:, bass.ds(t * AW, H)], h_a[p][:, C + H:C + 2 * H]).then_inc(a_kept, 1)
            quads(tile)(dve)
            keep(NT - 2, (NT - 2) % A4)
            keep(NT - 1, (NT - 1) % A4)

            dve.wait_ge(a_kept, NT)
            v.tensor_reduce(amax[:, 0, 0:H], a1t[:].rearrange("p t h -> p h t"), AX.X, ALU.max).then_inc(dve_own, 1)
            own.n += 1
            own(v.tensor_reduce(amax[:, 2, 0:H], a1t[:].rearrange("p t h -> p h t"), AX.X, ALU.min))
            own(v.tensor_scalar(amax[:, 0, H:2 * H], amax[:, 2, 0:H], -1.0, None, ALU.mult))
            dve.sem_inc(ext_ready, 1)
            dve.wait_ge(ext_all, 1)
            a2v = a2c[:].rearrange("p (t a) -> p t a", a=AW)
            cz = a1t[:]
            own(v.tensor_tensor(small[:, 0:H], amax[:, 1, 0:H], amax[:, 1, H:2 * H], ALU.add))
            v.tensor_copy(cz, amax[:, 1, 0:H].unsqueeze(1).to_broadcast([P, NT, H])).then_inc(dve_own, 1)
            own.n += 1
            own(v.tensor_reduce(small[:, H:H + 1], small[:, 0:H], AX.X, ALU.max))
            own(v.tensor_scalar(flag[:], small[0:1, H:H + 1], SPREAD, None, ALU.is_gt))
            dve.sem_inc(flag_ready, 1)
            wide = dve.value_load(flag[0:1, 0:1], min_val=0, max_val=1)
            with dve.If(wide > 0):
                for stored in (h_stored, xn_stored, xnt_stored):
                    all_stored(dve, stored)
                dve.wait_ge(steps_kept, 2 * KCH)
                dve.wait_ge(acc_zero, 1)
                seg = acc[:].rearrange("p (t w) -> p t w", w=TW)[:, :, C:TW]
                link = Chain(dve, seg_own)
                link(v.memset(seg, -BIG))
                dve.sem_inc(seg_hot, 1)
                with dve.Fori(0, NB * SB) as k:
                    t = dve.value_load(t_acc[0:1, bass.ds(k, 1)], min_val=0, max_val=(NT - 1) * TW)
                    for g in range(G):
                        j = k * G + g
                        link = Chain(dve, seg_own, j * 5 + 1)
                        link(v.tensor_scalar(seg_onehot, iota_p[:], dstT[:, bass.ds(j, 1)], None, ALU.is_equal))
                        dve.wait_ge(seg_in, (j + 1) * 16)
                        v.tensor_tensor(seg_diag, ident[:].unsqueeze(1).to_broadcast([P, H, P]),
                                        seg_rows[:, C:TW].unsqueeze(2).to_broadcast([P, H, P]), ALU.mult).then_inc(seg_hot, 1)
                        dve.wait_ge(seg_spread, j + 1)
                        link(v.tensor_scalar(seg_mask, bank[0][:, 0:P], -1.0, BIG, ALU.add, ALU.mult))
                        for n in range(2):
                            ins = v.tensor_tensor(seg_z[:, n * 4:n * 4 + 4, :], bank[3 + n][:].rearrange("p (h e) -> p h e", h=4),
                                                  seg_mask.unsqueeze(1).to_broadcast([P, 4, P]), ALU.add)
                        link(ins)
                        link(v.tensor_reduce(small[:, 0:H], seg_z, AX.X, ALU.max))
                        at = acc[:, bass.ds(t + C, H)]
                        link(v.tensor_tensor(at, at, small[:, 0:H], ALU.max))
                link = Chain(dve, seg_own, NB * TB * 5 + 1)
                link(v.tensor_scalar(cz, seg, -BIG / 2, None, ALU.is_gt))
                link(v.tensor_tensor(cz, cz, seg, ALU.mult))
                link(v.memset(seg, 0.0))
            own(v.tensor_tensor(cz, a2v[:, :, 0:H], cz, ALU.add))
            own(v.scalar_tensor_tensor(out=a2v[:, :, H:AW], in0=cz, scalar=SLOPE, in1=cz, op0=ALU.mult, op1=ALU.max))
            for k in range(PARTS):
                part = a2p[:].rearrange("p (t k a) -> p t k a", k=PARTS, a=AW)[:, :, k, :]
                own(v.tensor_copy(part, a2v))
                if k < PARTS - 1:
                    own(v.tensor_tensor(a2v, a2v, part, ALU.subtract))
            dve.sem_inc(c_ready, 1)

            w4 = wqkv[:, :, 0:2 * C].rearrange("p k (a n) -> p k a n", a=2)
            own(v.tensor_reduce(small[:, 0:4].rearrange("p (k a) -> p k a", a=2), w4, AX.X, ALU.add))
            v.tensor_reduce(small[0:1, 4:6], bqk[:], AX.X, ALU.add).then_inc(dve_own, 1)
            own.n += 1
            own(v.tensor_scalar(small[:, 8:12], small[:, 0:4], -1.0 / C, None, ALU.mult))
            own(v.tensor_scalar(small[0:1, 12:14], small[0:1, 4:6], -1.0 / C, None, ALU.mult))
            for k in range(KC):
                for a in range(2):
                    own(v.tensor_scalar(w4[:, k, a, :], w4[:, k, a, :], small[:, 8 + 2 * k + a:9 + 2 * k + a], None, ALU.add))
            for a in range(2):
                own(v.tensor_scalar(bqk[:, a, :], bqk[:, a, :], small[0:1, 12 + a:13 + a], None, ALU.add))
            own(v.memset(xn_c[:, C:C + 1], 1.0))
            dve.sem_inc(wqk_ready, 1)

            def one_hots(b, q):
                wait(dve, summed, (b - R3 + 1) * SB)
                v.tensor_tensor(hot[q], iota_p[:].unsqueeze(1).to_broadcast([P, TB, P]),
                                dstT[:, bass.ds(b * TB, TB)].unsqueeze(2).to_broadcast([P, TB, P]),
                                ALU.is_equal).then_inc(hot_ready, 1)

            for stored in (h_stored, xn_stored, xnt_stored):
                all_stored(dve, stored)
            dve.wait_ge(acc_zero, 1)

            def exponents(b, q, n):
                dve.wait_ge(gathered[q], n * 16 * TB)
                dve.wait_ge(a2c_picked, b + 1)
                z = [zb[:, q, k, :].rearrange("p (j h) -> p j h", h=H) for k in range(3)]
                pk = bank[2][:, 0:TB * AW].rearrange("p (j a) -> p j a", a=AW)
                link = Chain(dve, z_own, b * 3)
                link(v.tensor_tensor(z[0], ring[q][:, :, C:TW], pk[:, :, 0:H], ALU.add))
                link(v.scalar_tensor_tensor(out=z[1], in0=z[0], scalar=SLOPE, in1=z[0], op0=ALU.mult, op1=ALU.max))
                link(v.tensor_tensor(z[2], z[1], pk[:, :, H:AW], ALU.subtract))
                v.tensor_scalar(z[0], z[2], 0.0, None, ALU.min).then_inc(u_ready, 1)

            one_hots(0, 0)
            one_hots(1, 1)
            exponents(0, 0, 1)

            def batch(i, q, side, first):
                b = i * R3 + q
                last = isinstance(i, int) and i == IT
                _, ts = nc.values_load_multi_w_load_instructions(
                    t_acc[0:1, bass.ds(b * SB, SB)], engines=[mybir.EngineType.DVE], min_val=0,
                    max_val=(NT - 1) * TW, skip_runtime_bounds_check_because="steps' node tiles are clamped")
                dve.wait_ge(ex_ready, b + 1)
                for k in range(2):
                    m = ring[q][:, k * 4:k * 4 + 4, 0:C].rearrange("p j (h c) -> p j h c", h=H)
                    ex = ring[q][:, k * 4:k * 4 + 4, C:TW].unsqueeze(3).to_broadcast([P, 4, H, HC])
                    v.tensor_tensor(m, m, ex, ALU.mult).then_inc(msg_ready, 1)

                def add(s):
                    dve.wait_ge(summed, b * SB + s + 1)
                    wait(dve, added, b * SB + s)
                    a = acc[:, bass.ds(ts[s], TW)]
                    v.tensor_tensor(a, bank[3 + s % 2][:, 0:TW], a, ALU.add).then_inc(added, 1)
                if side == "mix" or (side == "mix_end" and q < 2):
                    t = (i - B_FIRST) * R3 + q - 1
                    if not (first and q == 0):
                        dve.wait_ge(mix_made, t + 1)
                        xt = X[:, bass.ds(t, 1), :]
                        v.tensor_tensor(xt, xt, bank[5][:, 0:C].unsqueeze(1), ALU.add).then_inc(mix_added, 1)
                        dve.wait_ge(mix_added, t * 2 + 1)
                        v.scalar_tensor_tensor(out=xt, in0=bank[6][:, 0:C].unsqueeze(1), scalar=nq[:, bass.ds(t, 1)],
                                               in1=xt, op0=ALU.mult, op1=ALU.add).then_inc(mix_added, 1)
                add(0)
                if not last:
                    one_hots(b + 2, (q + 2) % R3)
                add(1)
                if not last:
                    exponents(b + 1, (q + 1) % R3, i + 1 if q < 2 else i + 2)
                add(2)
                if side == "qk" and q == 2:
                    dve.wait_ge(q2_squared, (i + 1) * 2)
                    lq = Chain(dve, q_own, i * 2)
                    lq(v.tensor_scalar(qs[:, 2:4], qs[:, 0:2], EPS_DIV, None, ALU.add))
                    lq(v.reciprocal(qs[:, 4:6], qs[:, 2:4]))
                    v.tensor_scalar(q2[:], q2[:], qs[:, 4:5], None, ALU.mult)
                    v.tensor_scalar(k2[:], k2[:], qs[:, 5:6], None, ALU.mult).then_inc(k2_ready, 1)
                add(3)
            for _ in phases(dve, batch):
                dve.wait_ge(kx_added, NT)
                for k in range(KC):
                    ins = v.tensor_copy(kx[:, k, :], bank[6 + k][:, 0:C + 2])
                    own(ins)
                dve.sem_inc(kx_kept, 1)
                kn = small[:, 16:16 + KC]
                dve.wait_ge(roots, 2)
                own(v.tensor_scalar(kn, kn, EPS_NORM, None, ALU.max))
                own(v.reciprocal(small[:, 20:20 + KC], kn))
                own(v.tensor_scalar(nq[:], nq[:], EPS_NORM, None, ALU.max))
                own(v.reciprocal(nq[:], nq[:]))
                dve.wait_ge(kvw_made, 1)
                for k in range(KC):
                    own(v.scalar_tensor_tensor(out=kvw[:, k, :], in0=bvo[:], scalar=kx[:, k, C:C + 1], in1=bank[6 + k][:, 0:C],
                                               op0=ALU.mult, op1=ALU.add))
                    own(v.tensor_scalar(kvw[:, k, :], kvw[:, k, :], small[:, 20 + k:21 + k], 1.0 / math.sqrt(N),
                                        ALU.mult, ALU.mult))
                dve.sem_inc(kvw_ready, 1)

            a3 = acc[:].rearrange("p (t w) -> p t w", w=TW)
            dve.wait_ge(added, NB * SB)
            den = a3[:, :, C:TW]
            own(v.tensor_scalar(a1t[:], den, TINY, None, ALU.max))
            own(v.reciprocal(a1t[:], a1t[:]))
            dve.wait_ge(mix_added, 2 * NT)
            for c in range(NXP + 2):
                if c < NXP:
                    m = a3[:, c * XP:(c + 1) * XP, 0:C].rearrange("p t (h c) -> p t h c", h=H)
                    r_ = a1t[:, c * XP:(c + 1) * XP, :].unsqueeze(3).to_broadcast([P, XP, H, HC])
                    v.tensor_tensor(m, m, r_, ALU.mult).then_inc(msg_scaled, 1)
                if 0 < c <= NXP:
                    dve.wait_ge(msg_scaled, c)
                    xc = X[:, (c - 1) * XP:c * XP, :]
                    v.tensor_tensor(xc, xc, a3[:, (c - 1) * XP:c * XP, 0:C], ALU.add).then_inc(x1_made, 1)
                if c > 1:
                    dve.wait_ge(x1_made, c - 1)
                    for t in range((c - 2) * XP, (c - 1) * XP):
                        ins = v.bn_stats(stat[:, t, :], X[:, t, :])
                    own(ins)
                for n, (a, e) in enumerate(((0, XH), (XH, NT))):
                    if e == (c - 1) * XP:
                        ln_stats(own, 1 + n, stat[:, a:e, :], [sc[:, k, a:e] for k in range(4)], mean[:, a:e], rstd[:, a:e])
                        own(v.scalar_tensor_tensor(out=sc[:, 3, a:e], in0=mean[:, a:e], scalar=-1.0, in1=rstd[:, a:e],
                                                   op0=ALU.mult, op1=ALU.mult))
                        dve.sem_inc(x2_scaled, 1)
            for t in range(XD, NT):
                v.tensor_scalar(acc_tile(t)[:, 0:C], X[:, t, :], mean[:, t:t + 1], rstd[:, t:t + 1],
                                ALU.subtract, ALU.mult).then_inc(x2_late, 1)

            def r(n, w=NE):
                return route[0:1, n, 0:w]
            io = iota_p[0:1, 0:NE]
            dve.wait_ge(logits_made, 1)
            own(v.scalar_tensor_tensor(out=r(1), in0=bank[1][0:1, 0:NE], scalar=1.0 / N, in1=r(0), op0=ALU.mult, op1=ALU.add))
            own(v.tensor_reduce(r(3, 1), r(1), AX.X, ALU.max))
            own(v.tensor_scalar(r(1), r(1), r(3, 1), None, ALU.subtract))
            dve.sem_inc(soft_in, 1)
            dve.wait_ge(soft_out, 1)
            own(v.tensor_reduce(r(3, 1), r(2), AX.X, ALU.add))
            own(v.reciprocal(r(4, 1), r(3, 1)))
            own(v.tensor_scalar(r(2), r(2), r(4, 1), None, ALU.mult))
            own(v.tensor_scalar(r(4), r(2), float(N), TINY, ALU.mult, ALU.max))
            own(v.reciprocal(r(4), r(4)))
            own(v.tensor_scalar(r(4), r(4), CAPACITY, 1.0, ALU.mult, ALU.min))
            own(v.tensor_tensor(r(5), r(2), r(4), ALU.mult))
            own(v.tensor_reduce(r(3, 1), r(5), AX.X, ALU.max))
            own(v.tensor_scalar(r(5), r(5), r(3, 1), None, ALU.subtract))
            dve.sem_inc(soft_in, 1)
            dve.wait_ge(soft_out, 2)
            own(v.tensor_reduce(r(3, 1), r(6), AX.X, ALU.add))
            own(v.reciprocal(r(4, 1), r(3, 1)))
            own(v.tensor_scalar(r(7), r(6), r(4, 1), None, ALU.mult))
            for e in range(TOP):
                own(v.tensor_reduce(r(8 + e, 1), r(7), AX.X, ALU.max))
                own(v.tensor_scalar(r(10), r(7), r(8 + e, 1), float(NE), ALU.is_lt, ALU.mult))
                own(v.tensor_tensor(r(10), r(10), io, ALU.add))
                own(v.tensor_reduce(route[0:1, 13, e:e + 1], r(10), AX.X, ALU.min))
                if e == 0:
                    own(v.tensor_scalar(r(10), io, route[0:1, 13, e:e + 1], 4.0, ALU.is_equal, ALU.mult))
                    own(v.tensor_tensor(r(7), r(7), r(10), ALU.subtract))
            own(v.tensor_tensor(r(11, 1), r(9, 1), r(8, 1), ALU.subtract))
            dve.sem_inc(soft_in, 1)
            own(v.tensor_copy(route_i[0:1, 0:TOP], route[0:1, 13, 0:TOP]))
            dve.wait_ge(soft_out, 3)
            own(v.tensor_scalar(r(15, 1), r(12, 1), 1.0, None, ALU.add))
            own(v.reciprocal(route[0:1, 14, 0:1], r(15, 1)))
            own(v.tensor_tensor(route[0:1, 14, 1:2], route[0:1, 14, 0:1], r(12, 1), ALU.mult))
            dve.sem_inc(route_ready, 1)
            dve.wait_ge(wsel_made, 1)
            own(v.tensor_copy(wsel[:], bank[4][:, 0:TOP]))
            dve.wait_ge(e_loaded, 16 * NX)
            own(v.tensor_scalar(b2r[:, 2, :], b2r[:, 0, :], wsel[0:1, 0:1], None, ALU.mult))
            own(v.scalar_tensor_tensor(out=b2r[:, 2, :], in0=b2r[:, 1, :], scalar=wsel[0:1, 1:2], in1=b2r[:, 2, :],
                                       op0=ALU.mult, op1=ALU.add))
            dve.sem_inc(b2_ready, 1)
            for e in range(TOP):
                w = w2_sb[:, e].rearrange("p f d -> p (f d)")
                own(v.tensor_scalar(w, w, wsel[:, e:e + 1], None, ALU.mult))
            dve.wait_ge(b2_made, 1)
            own(v.tensor_copy(b2w, bank[6][:, 0:C]))
            dve.sem_inc(w2_scaled, 1)

            def finish(g, p, n):
                link = Chain(dve, y_own, g * (n_links))
                base = link.n
                wait(dve, out_stored[p], 16 * ((g - p) // 2))
                for j in range(n):
                    dve.wait_ge(y_made, g * FG + j + 1)
                    v.tensor_tensor(y[p][:, j, :], bank[4 + j][:, 0:C],
                                    acc[:, bass.ds((g * FG + j) * TW, C)], ALU.add).then_inc(y_added, 1)
                dve.wait_ge(y_added, g * FG + n)
                yy = y[p][:, 0:n, :]

                def wide(a):
                    return a.unsqueeze(1).to_broadcast([P, n, C])
                link(v.tensor_tensor(yy, yy, wide(b2w), ALU.add))
                for j in range(n):
                    ins = v.bn_stats(ystat[:, p, j, :], y[p][:, j, :])
                link(ins)
                ln_stats(link, 3 + g, ystat[:, p, 0:n, :], [ysc[:, p, k, 0:n] for k in range(4)], ysc[:, p, 4, 0:n], ysc[:, p, 5, 0:n])
                for j in range(n):
                    ins = v.tensor_scalar(y[p][:, j, :], y[p][:, j, :], ysc[:, p, 4, j:j + 1], ysc[:, p, 5, j:j + 1],
                                          ALU.subtract, ALU.mult)
                link(ins)
                link(v.tensor_tensor(yy, yy, wide(gb[:, 0, :]), ALU.mult))
                link(v.tensor_tensor(yy, yy, wide(gb[:, 1, :]), ALU.add))
                v.tensor_tensor(yy, yy, X[:, bass.ds(g * FG, n), :], ALU.add).then_inc(y_ready, 1)
            n_links = 12
            finish(0, 0, FG)
            finish(1, 1, FG)
            with dve.Fori(1, NG // 2) as i:
                finish(i * 2, 0, FG)
                finish(i * 2 + 1, 1, FG)
            finish(NG, 0, 1)


_IN = ['x', 'src', 'dst', 'L0_gnn_W', 'L0_gnn_attn_l', 'L0_gnn_attn_r', 'L0_gnn_bias', 'L0_mix_W_qkv', 'L0_mix_b_qkv',
       'L0_mix_W_out', 'L0_mix_b_out', 'L0_ffn_Wr', 'L0_ffn_br', 'L0_ffn_W1', 'L0_ffn_b1', 'L0_ffn_W2', 'L0_ffn_b2',
       'L0_ffn_gamma', 'L0_ffn_beta']


def kernel(**inputs):
    import numpy as np
    import concourse.bacc as bacc
    from concourse.bass_utils import run_bass_kernel_spmd

    nc = bacc.Bacc("TRN2", target_bir_lowering=False, num_devices=1)
    arrays, args = {}, []
    for name in _IN:
        a = np.ascontiguousarray(inputs[name])
        if name in ('src', 'dst'):
            rows = np.full(((U + 1) * EG,), 0 if name == 'src' else NONE, a.dtype)
            rows[:E] = a
            a = rows.reshape(U + 1, EG)
        arrays[name] = a
        args.append(nc.dram_tensor(name, a.shape, mybir.dt.from_np(a.dtype), kind="ExternalInput").ap())
    args.append(nc.dram_tensor("out", (N, C), F32, kind="ExternalOutput").ap())
    build(nc, *args)
    r = run_bass_kernel_spmd(nc, [arrays], core_ids=[0])
    return r.results[0]["out"]
```

```python
import math
from contextlib import ExitStack

import concourse.bass as bass
from concourse import mybir

F32 = mybir.dt.float32
BF16 = mybir.dt.bfloat16
I32 = mybir.dt.int32
ALU = mybir.AluOpType
ACT = mybir.ActivationFunctionType
AX = mybir.AxisListType
RMAX = bass.bass_isa.ReduceOp.max

P = 128
N = 6250
C = 256
H = 8
HC = C // H
KC = C // P
NT = -(-N // P)
LAST = N - (NT - 1) * P
E = 206250
G = 2
EG = G * P
U = -(-E // EG)
STEPS = U + NT - 1
SB = 4
TB = SB * G
NB = -(-STEPS // SB)
A1 = 8
Q_MID = 2
R3 = 3
IT = NB // R3
KCH = -(-(NB * SB + SB) // P)
KS = KCH * P
UCH = -(-U // P)
NONE = 16384
TW = C + H
PARTS = 3
AW = 2 * H
NE = 8
F = 512
FC = F // P
TOP = 2
CAPACITY = float(math.ceil(N * 1.25 / NE))
SLOPE = 0.2
LN_EPS = 1e-5
EPS_DIV = 1e-7
EPS_NORM = 1e-12
TINY = 1e-30
SPREAD = 40.0
BIG = 1e30
XP = 7
NXP = NT // XP
XH = 4 * XP
XD = NT - 10
FG = 3
HB = [2, 3, 7, 2, 3, 7, 2, 3]
HB_BEFORE = [-1, 0, -2] + [f - 2 for f in range(3, len(HB))]
NG = NT // FG

A2_LAST = NT - 1
KV = A2_LAST + 1
B_FIRST = KV + 1
B_LAST = B_FIRST + (NT - 1) // R3
assert NB == IT * R3 + 1 and NT == FG * NG + 1 and (NT - 1) % R3 == 0 and (NT - 1) % A1 == 0 and B_LAST < IT
assert NT == 3 * A1 * Q_MID + 1


def wait(eng, sem, count):
    if isinstance(count, int) and count <= 0:
        return
    eng.wait_ge(sem, count)


class Chain:

    def __init__(self, eng, sem, base=0):
        self.eng, self.sem, self.n = eng, sem, base

    def __call__(self, ins):
        ins.then_inc(self.sem, 1)
        self.n = self.n + 1
        self.eng.wait_ge(self.sem, self.n)


def build(nc, x, src, dst, W, attn_l, attn_r, gnn_bias, W_qkv, b_qkv, W_out, b_out,
          Wr, br, W1, b1, W2, b2, gamma, beta, out):
    h_tab = nc.dram_tensor("h_tab", [NT * P, TW], F32).ap()
    xx_d = nc.dram_tensor("xx_d", [NT, P, 2 * C], F32).ap()
    xn_d, xnt_d = xx_d[:, :, 0:C], xx_d[:, :, C:2 * C]
    q2t_d = nc.dram_tensor("q2t_d", [NT, P, C], F32).ap()

    with ExitStack() as ctx:
        def sb(name, shape, dt=F32):
            return ctx.enter_context(nc.sbuf_tensor(name, shape, dt))

        def sem(name):
            return ctx.enter_context(nc.semaphore(name))

        def sems(name, n):
            return [sem(f"{name}{i}") for i in range(n)]

        bank = [ctx.enter_context(nc.psum_tensor(f"bank{i}", [P, 512], F32)) for i in range(8)]

        X = sb("X", [P, NT, C])
        acc = sb("acc", [P, NT * TW])
        WORK = R3 * TB * (TW + P + P // 2)
        work = sb("work", [P, WORK])
        a2c = sb("a2c", [P, NT * AW])
        a2p = sb("a2p", [P, NT * PARTS * AW], BF16)
        a1t = sb("a1t", [P, NT, H])
        cols = sb("cols", [P, 2 * KS * G])
        srcT = cols[:, 0:KS * G].bitcast(I32)
        dstT = cols[:, KS * G:2 * KS * G]
        t_acc = sb("t_acc", [1, KS], I32)
        t_a2c = sb("t_a2c", [1, KS], I32)
        idx = sb("idx", [P, R3, TB], I32)
        zb = sb("zb", [P, R3, 3, TB * H])
        ident = sb("ident", [P, P])
        iota_p = sb("iota_p", [P, P])
        ones = sb("ones", [P, P])
        wg = sb("wg", [P, KC, C + 2 * H])
        wqkv = sb("wqkv", [P, KC, 3 * C])
        kx = sb("kx", [P, KC, C + 2])
        wout = kx[:, :, 0:C]
        wvo = sb("wvo", [P, KC, C])
        kvw = sb("kvw", [P, KC, C])
        bqk = sb("bqk", [1, 2, C])
        rows = sb("rows", [1, 3, C])
        bv_col = sb("bv_col", [P, KC])
        bvo = sb("bvo", [P, C])
        bvx = kvw[:, 0, :].rearrange("p (k n) -> p k n", k=KC)
        stat = sb("stat", [P, NT, 6])
        sc = sb("sc", [P, 4, NT])
        nq = sb("nq", [P, NT])
        mean = sb("mean", [P, NT])
        rstd = sb("rstd", [P, NT])
        xn_c = sb("xn_c", [P, C + 1])
        xnt_c = sb("xnt_c", [P, KC, P])
        q2t_c = sb("q2t_c", [P, KC, P])
        q2 = sb("q2", [P, C])
        k2 = sb("k2", [P, C])
        sq = sb("sq", [P, C])
        qs = sb("qs", [P, 8])
        small = sb("small", [P, 32])
        amax = sb("amax", [P, 4, 2 * H])
        seg_i = sb("seg_i", [P, 1], I32)
        flag = sb("flag", [1, 1], I32)
        b2w = kvw[:, 0, :]
        wr_sb = sb("wr_sb", [P, KC, NE])
        mcol = sb("mcol", [P, KC])
        route = sb("route", [1, 16, NE])
        route_i = sb("route_i", [1, TOP], I32)
        wsel = sb("wsel", [P, TOP])
        b2r = rows

        mix_in = [(xnt_c[:].rearrange("p k n -> p (k n)"), q2t_c[:].rearrange("p k n -> p (k n)")),
                  (q2[:], k2[:]), (sq[:], xn_c[:, 0:C])]

        RW = TB * TW
        ring = [work[:, q * RW:(q + 1) * RW].rearrange("p (j w) -> p j w", w=TW) for q in range(R3)]
        s0 = R3 * RW
        hot = [work[:, s0 + q * TB * P:s0 + (q + 1) * TB * P].rearrange("p (j d) -> p j d", d=P)
               for q in range(R3)]
        s1 = s0 + R3 * TB * P
        hotT = [work[:, s1 + q * TB * P // 2:s1 + (q + 1) * TB * P // 2].bitcast(BF16).rearrange("p (j d) -> p j d", d=P)
                for q in range(R3)]
        wvT = work[:, s1:s1 + KC * C].rearrange("p (k n) -> p k n", k=KC)
        seg_rows = kx[:].rearrange("p k n -> p (k n)")[:, 0:TW]
        seg_onehot = k2[:, 0:P]
        seg_mask = q2[:, 0:P]
        seg_diag = hot[2]
        seg_z = work[:, s1 + TB * P // 2:s1 + 3 * TB * P // 2].rearrange("p (h e) -> p h e", h=H)
        o = 0

        def view(n):
            nonlocal o
            o += n
            return work[:, o - n:o]
        prod = view(KC * C).rearrange("p (k n) -> p k n", k=KC)
        attn = view(2 * C).rearrange("p (a n) -> p a n", a=2)
        kio = view(KS)
        cmp = view(KS)
        kcol = view(KCH)
        uio = view(UCH)
        fcol = view(UCH)
        ucol = view(KCH)
        tcol = view(KCH)
        lastd = view(UCH).bitcast(I32)
        lastt = view(UCH).bitcast(I32)
        ucol_i = view(KCH).bitcast(I32)
        iotai = cmp.bitcast(I32)
        urow = view(2 * KS).rearrange("p (a n) -> p a n", a=2)
        f_src = view(KCH * EG).rearrange("p (c e) -> p c e", e=EG)
        f_dst = view(KCH * EG).rearrange("p (c e) -> p c e", e=EG)
        g_src, g_dst = (f.bitcast(I32) for f in (f_src, f_dst))
        assert o <= WORK, (o, WORK)
        A_COLS = A1 * (2 * C + C + 2 * H)
        o = 0

        def early(n):
            nonlocal o
            o += n
            return acc[:, o - n:o]
        xx_a = [early(2 * C) for _ in range(A1)]
        xn_a = [a[:, 0:C] for a in xx_a]
        xnt_a = [a[:, C:2 * C].rearrange("p (k n) -> p k n", k=KC) for a in xx_a]
        h_a = [early(C + 2 * H) for _ in range(A1)]
        assert o == A_COLS
        o = 0
        w1_sb = view(TOP * KC * F).rearrange("p (e k f) -> p e k f", e=TOP, k=KC)
        w2_sb = view(TOP * FC * C).rearrange("p (e f d) -> p e f d", e=TOP, f=FC)
        b1_sb = view(TOP * FC).rearrange("p (e f) -> p e f", e=TOP)
        x2s = [view(FG * C).rearrange("p (t c) -> p t c", t=FG) for _ in range(2)]
        x2t = [view(KC * FG * P).rearrange("p (k n) -> p k n", k=KC) for _ in range(2)]
        hT = [a.rearrange("p (f n) -> p f n", f=TOP * FC)
              for a in (view(TOP * FC * FG * P), cols[:, 0:TOP * FC * FG * P])]
        y = [wqkv[:].rearrange("p k n -> p (k n)")[:, i * FG * C:(i + 1) * FG * C].rearrange("p (t c) -> p t c", t=FG)
             for i in range(2)]
        gb = view(2 * C).rearrange("p (a c) -> p a c", a=2)
        ystat = view(2 * FG * 6).rearrange("p (a t s) -> p a t s", a=2, s=6)
        ysc = view(2 * 6 * FG).rearrange("p (a s t) -> p a s t", a=2, s=6)
        assert o <= WORK, (o, WORK)

        def acc_tile(t):
            return acc[:, t * TW:(t + 1) * TW]

        var_ready = sem("var_ready")
        root_ready = sem("root_ready")
        x_measured = sem("x_measured")
        x_loaded = sems("x_loaded", 7)
        wg_loaded = sem("wg_loaded")
        w_loaded = sem("w_loaded")
        id_set = sem("id_set")
        iota_set = sem("iota_set")
        acc_zero = sem("acc_zero")
        dve_own = sem("dve_own")
        lastd_loaded = sem("lastd_loaded")
        lastd_clear = sem("lastd_clear")
        cmp_done = sem("cmp_done")
        u_counted = sem("u_counted")
        t_ready = sem("t_ready")
        ucol_ready = sem("ucol_ready")
        steps_gathered = sem("steps_gathered")
        f_ready = sem("f_ready")
        steps_turned = sem("steps_turned")
        steps_kept = sem("steps_kept")
        wg_ready = sem("wg_ready")
        pool_own = sem("pool_own")
        w_summed = sem("w_summed")
        wqk_ready = sem("wqk_ready")
        wvt_turned = sem("wvt_turned")
        wvt_kept = sem("wvt_kept")
        wvo_made = sem("wvo_made")
        wvo_kept = sem("wvo_kept")
        bvx_ready = sem("bvx_ready")
        crow_ready = sem("crow_ready")
        xn_ready = sem("xn_ready")
        xn_turned = sem("xn_turned")
        xnt_kept = sem("xnt_kept")
        h_made = sem("h_made")
        h_kept = sem("h_kept")
        a_kept = sem("a_kept")
        xx_stored = sems("xx_stored", A1)
        h_stored = sems("h_stored", A1)
        ext_ready = sem("ext_ready")
        ext_all = sem("ext_all")
        flag_ready = sem("flag_ready")
        c_ready = sem("c_ready")
        seg_idx = sem("seg_idx")
        seg_begun = sem("seg_begun")
        seg_in = sem("seg_in")
        seg_hot = sem("seg_hot")
        seg_spread = sem("seg_spread")
        seg_own = sem("seg_own")
        idx_ready = sem("idx_ready")
        batch_begun = sem("batch_begun")
        gathered = sems("gathered", R3)
        hot_ready = sem("hot_ready")
        hot_turned = sem("hot_turned")
        hotT_kept = sem("hotT_kept")
        a2c_picked = sem("a2c_picked")
        z_own = sem("z_own")
        u_ready = sem("u_ready")
        ex_ready = sem("ex_ready")
        msg_ready = sem("msg_ready")
        summed = sem("summed")
        added = sem("added")
        load_begun = sem("load_begun")
        xnt_loaded = sem("xnt_loaded")
        xn_loaded = sem("xn_loaded")
        qk_made = sem("qk_made")
        roots = sem("roots")
        q2_squared = sem("q2_squared")
        q_own = sem("q_own")
        k2_ready = sem("k2_ready")
        k2_squared = sem("k2_squared")
        kx_added = sem("kx_added")
        q2_turned = sem("q2_turned")
        q2t_kept = sem("q2t_kept")
        q2t_stored = sem("q2t_stored")
        kx_kept = sem("kx_kept")
        kx_turned = sem("kx_turned")
        kxt_kept = sem("kxt_kept")
        kvw_made = sem("kvw_made")
        kvw_ready = sem("kvw_ready")
        mix_loaded = sems("mix_loaded", R3)
        mix_made = sem("mix_made")
        mix_added = sem("mix_added")
        msg_scaled = sem("msg_scaled")
        x1_made = sem("x1_made")
        x2_late = sem("x2_late")
        x2_scaled = sem("x2_scaled")
        x2_ready = sem("x2_ready")
        mean_made = sem("mean_made")
        mean_kept = sem("mean_kept")
        logits_made = sem("logits_made")
        soft_in = sem("soft_in")
        soft_out = sem("soft_out")
        route_ready = sem("route_ready")
        w1_loaded = sem("w1_loaded")
        e_loaded = sem("e_loaded")
        wsel_made = sem("wsel_made")
        w2_scaled = sem("w2_scaled")
        b2_ready = sem("b2_ready")
        b2_made = sem("b2_made")
        x2_staged = sem("x2_staged")
        x2_turned = sem("x2_turned")
        x2t_kept = sem("x2t_kept")
        hid_made = sem("hid_made")
        hid_kept = sem("hid_kept")
        y_made = sem("y_made")
        y_added = sem("y_added")
        y_own = sem("y_own")
        y_ready = sem("y_ready")
        out_stored = sems("out_stored", 2)

        block = ctx.enter_context(nc.Block())

        xv = x[0:(NT - 1) * P, :].rearrange("(t p) c -> p t c", p=P)
        XC = (NT - 1) // 6
        NX1, NX = 2 * TOP, 2 * TOP + 2
        NWG, NW = 3, 9
        TT = 3
        TA = A1 * Q_MID

        def phases(eng, batch):
            def three(i, side, first=False):
                for q in range(R3):
                    batch(i, q, side, first)
            three(0, "qk")
            with eng.Fori(1, A2_LAST) as i:
                three(i, "qk")
            three(A2_LAST, "qk")
            three(KV, "kv")
            three(B_FIRST, "mix", True)
            with eng.Fori(B_FIRST + 1, B_LAST) as i:
                three(i, "mix")
            three(B_LAST, "mix_end")
            with eng.Fori(B_LAST + 1, IT) as i:
                three(i, "")
            batch(IT, 0, "", False)

        def first_pass(eng, tile):
            for p in range(A1):
                tile(p, p, 0)
            for p in range(A1):
                tile((Q_MID - 1) * A1 + p, p, Q_MID - 1)
            yield
            with eng.Fori(Q_MID, NT // A1) as i:
                for p in range(A1):
                    tile(i * A1 + p, p, i)
            tile(NT - 1, 0, NT // A1)

        def table_chunks(t):
            n = t - (TA - TT) if isinstance(t, int) else -1
            return range(KCH * n // TT, KCH * (n + 1) // TT) if 0 <= n < TT else ()

        def all_stored(eng, sems_):
            for p in range(A1):
                eng.wait_ge(sems_[p], 16 * ((NT - 1 - p) // A1 + 1))

        @block.sync
        def _(sp):
            sp.wait_ge(lastd_clear, 1)
            for c in range(UCH):
                n = min(P, U - c * P)
                sp.dma_start(lastd[0:n, c:c + 1], dst[c * P:c * P + n, EG - 1:EG],
                             allow_slow_non_contiguous=True).then_inc(lastd_loaded, 16)
            for c in range(6):
                sp.dma_start(X[:, c * XC:(c + 1) * XC, :], xv[:, c * XC:(c + 1) * XC, :]).then_inc(x_loaded[c], 16)
            sp.wait_ge(dve_own, 1)
            sp.dma_start(X[0:LAST, NT - 1, :], x[(NT - 1) * P:N, :]).then_inc(x_loaded[6], 16)

            def tile(t, p, n):
                sp.wait_ge(xnt_kept, t + 1)
                sp.dma_start(xx_d[bass.ds(t, 1)].rearrange("o p c -> p (o c)"), xx_a[p]).then_inc(xx_stored[p], 16)
                sp.wait_ge(h_kept, t + 1)
                sp.dma_start(h_tab[bass.ds(t * P, P), :], h_a[p][:, 0:TW]).then_inc(h_stored[p], 16)
            for _ in first_pass(sp, tile):
                pass
            all_stored(sp, xx_stored)

            def store_q2t(t):
                sp.wait_ge(q2t_kept, t + 1)
                sp.dma_start(q2t_d[bass.ds(t, 1)].rearrange("o p c -> p (o c)"),
                             q2t_c[:].rearrange("p k n -> p (k n)")).then_inc(q2t_stored, 16)

            def batch(i, q, side, first):
                if side == "qk" and q == 0:
                    wait(sp, qk_made, i)
                    sp.dma_start(xnt_c[:].rearrange("p k n -> p (k n)"),
                                 xnt_d[bass.ds(i, 1)].rearrange("o p c -> p (o c)")).then_inc(xnt_loaded, 16)
                    wait(sp, kx_added, i)
                    sp.sem_inc(load_begun, 1)
                    sp.dma_start(xn_c[:, 0:C], xn_d[bass.ds(i, 1)].rearrange("o p c -> p (o c)")).then_inc(xn_loaded, 16)
                    if not (isinstance(i, int) and i == 0):
                        store_q2t(i - 1)
                if side == "kv" and q == 0:
                    store_q2t(NT - 1)
                if side == "mix" or (side == "mix_end" and q == 0):
                    t = (i - B_FIRST) * R3 + q
                    if first and q == 0:
                        sp.wait_ge(q2t_stored, 16 * NT)
                        sp.wait_ge(q2_turned, NT)
                    wait(sp, mix_made, t - R3 + 1)
                    sp.dma_start(mix_in[q][0], xnt_d[bass.ds(t, 1)].rearrange("o p c -> p (o c)")).then_inc(mix_loaded[q], 16)
                    sp.dma_start(mix_in[q][1], q2t_d[bass.ds(t, 1)].rearrange("o p c -> p (o c)")).then_inc(mix_loaded[q], 16)
            phases(sp, batch)

            sp.wait_ge(x2_ready, 1)
            sp.dma_start(gb[:, 0, :], gamma.unsqueeze(0).to_broadcast([P, C])).then_inc(e_loaded, 16)
            sp.dma_start(gb[:, 1, :], beta.unsqueeze(0).to_broadcast([P, C])).then_inc(e_loaded, 16)
            sp.wait_ge(route_ready, 1)
            which = [sp.value_load(route_i[0:1, e:e + 1], min_val=0, max_val=NE - 1) for e in range(TOP)]
            for e, n in enumerate(which):
                sp.dma_start(w1_sb[:, e], W1[bass.ds(n, 1)].rearrange("o (k p) f -> p (o k) f", p=P)).then_inc(w1_loaded, 16)
                sp.dma_start(b1_sb[:, e, :], b1[bass.ds(n, 1)].rearrange("o (f p) -> p (o f)", p=P),
                             allow_slow_non_contiguous=True).then_inc(w1_loaded, 16)
            for e, n in enumerate(which):
                sp.dma_start(b2r[:, e, :], b2[bass.ds(n, 1)]).then_inc(e_loaded, 16)
                sp.dma_start(w2_sb[:, e], W2[bass.ds(n, 1)].rearrange("o (f p) d -> p (o f) d", p=P)).then_inc(e_loaded, 16)

            def store(g, p):
                sp.wait_ge(y_ready, g + 1)
                if isinstance(g, int) and g == NG:
                    sp.dma_start(out[g * FG * P:N, :], y[p][0:LAST, 0, :]).then_inc(out_stored[p], 16)
                    return
                sp.dma_start(out[bass.ds(g * FG * P, FG * P), :].rearrange("(t p) c -> p t c", p=P),
                             y[p][:, :, :]).then_inc(out_stored[p], 16)
            with sp.Fori(0, NG // 2) as i:
                store(i * 2, 0)
                store(i * 2 + 1, 1)
            store(NG, 0)
            sp.wait_ge(out_stored[0], 16 * (NG // 2 + 1))
            sp.wait_ge(out_stored[1], 16 * (NG // 2))

        @block.gpsimd
        def _(pool):
            nc.gpsimd.memset(ident[:], 0.0).then_inc(id_set, 1)
            nc.gpsimd.memset(ones[:], 1.0).then_inc(id_set, 1)
            pool.wait_ge(id_set, 1)
            nc.gpsimd.affine_select(out=ident[:], in_=ident[:], compare_op=ALU.not_equal, fill=1.0, base=0,
                                    pattern=[[-1, P]], channel_multiplier=1).then_inc(id_set, 1)
            nc.gpsimd.iota(iotai, pattern=[[1, KS]], base=0, channel_multiplier=0).then_inc(iota_set, 1)
            nc.gpsimd.iota(kcol.bitcast(I32), pattern=[[P, KCH]], base=0, channel_multiplier=1).then_inc(iota_set, 1)
            nc.gpsimd.iota(uio.bitcast(I32), pattern=[[P, UCH]], base=0, channel_multiplier=1).then_inc(iota_set, 1)
            nc.gpsimd.memset(acc[:, A_COLS:], 0.0).then_inc(acc_zero, 1)

            pool.wait_ge(ucol_ready, 1)
            for c in range(KCH):
                for g, table in ((g_src, src), (g_dst, dst)):
                    nc.gpsimd.indirect_dma_start(
                        out=g[:, c, :], out_offset=None, in_=table,
                        in_offset=bass.IndirectOffsetOnAxis(ap=ucol_i[:, c:c + 1], axis=0)).then_inc(steps_gathered, 16)
            pl = nc.gpsimd
            link = Chain(pool, pool_own)
            w4 = wqkv[:, :, 0:2 * C].rearrange("p k (a n) -> p k a n", a=2)
            pool.wait_ge(w_summed, 2)
            link(pl.tensor_scalar(small[:, 8:12], small[:, 0:4], -1.0 / C, None, ALU.mult))
            link(pl.tensor_scalar(small[0:1, 12:14], small[0:1, 4:6], -1.0 / C, None, ALU.mult))
            for k in range(KC):
                for a in range(2):
                    link(pl.tensor_scalar(w4[:, k, a, :], w4[:, k, a, :], small[:, 8 + 2 * k + a:9 + 2 * k + a], None, ALU.add))
            for a in range(2):
                link(pl.tensor_scalar(bqk[:, a, :], bqk[:, a, :], small[0:1, 12 + a:13 + a], None, ALU.add))
            link(pl.memset(xn_c[:, C:C + 1], 1.0))
            pool.sem_inc(wqk_ready, 1)

            pool.wait_ge(ext_ready, 1)
            nc.gpsimd.partition_all_reduce(amax[:, 1, :], amax[:, 0, :], P, RMAX).then_inc(ext_all, 1)

            for stored in (h_stored, xx_stored):
                all_stored(pool, stored)

            def batch(i, q, side, first):
                b = i * R3 + q
                pool.wait_ge(idx_ready, b + 1)
                wait(pool, summed, SB * (b - R3 + 1))
                pool.sem_inc(batch_begun, 1)
                for j in range(TB):
                    nc.gpsimd.indirect_dma_start(
                        out=ring[q][:, j, :], out_offset=None, in_=h_tab,
                        in_offset=bass.IndirectOffsetOnAxis(ap=idx[:, q, j:j + 1], axis=0)).then_inc(gathered[q], 16)
                if isinstance(i, int) and i == 0 and q == R3 - 1:
                    pool.wait_ge(flag_ready, 1)
                    wide = pool.value_load(flag[0:1, 0:1], min_val=0, max_val=1)
                    with pool.If(wide > 0):
                        seg_gathers()

            def seg_gathers():
                with pool.Fori(0, NB * TB) as j:
                    pool.wait_ge(seg_hot, j + 1)
                    nc.gpsimd.tensor_copy(seg_i[:], srcT[:, bass.ds(j, 1)]).then_inc(seg_idx, 1)
                    pool.wait_ge(seg_idx, j + 1)
                    pool.sem_inc(seg_begun, 1)
                    nc.gpsimd.indirect_dma_start(
                        out=seg_rows, out_offset=None, in_=h_tab,
                        in_offset=bass.IndirectOffsetOnAxis(ap=seg_i[:, 0:1], axis=0)).then_inc(seg_in, 16)
                pool.wait_ge(seg_hot, NB * TB + 1)

            phases(pool, batch)

            def stage(g, p, n):
                wait(pool, x2_turned, g - 1)
                a3 = acc[:].rearrange("p (t w) -> p t w", w=TW)
                nc.gpsimd.tensor_copy(x2s[p][:, 0:n, :], a3[:, bass.ds(g * FG, n), 0:C]).then_inc(x2_staged, 1)

            pool.wait_ge(x2_ready, XD)
            pool.wait_ge(x2_late, NT - XD)
            stage(0, 0, FG)
            stage(1, 1, FG)
            with pool.Fori(1, NG // 2) as i:
                stage(i * 2, 0, FG)
                stage(i * 2 + 1, 1, FG)
            stage(NG, 0, 1)

        @block.scalar
        def _(act):
            for loaded, dst_ap, src_ap in (
                (wg_loaded, wg[:, :, 0:C], W.rearrange("(k p) n -> p k n", p=P)),
                (wg_loaded, attn[:, 0, :], attn_l.rearrange("a h j -> a (h j)").to_broadcast([P, C])),
                (wg_loaded, attn[:, 1, :], attn_r.rearrange("a h j -> a (h j)").to_broadcast([P, C])),
                (w_loaded, wqkv[:], W_qkv.rearrange("(k p) n -> p k n", p=P)),
                (w_loaded, wout[:], W_out.rearrange("(k p) n -> p k n", p=P)),
                (w_loaded, bqk[:].rearrange("a k n -> a (k n)"), b_qkv[0:2 * C].unsqueeze(0)),
                (w_loaded, bv_col[:, 0:1], b_qkv[2 * C:2 * C + P].unsqueeze(1)),
                (w_loaded, bv_col[:, 1:2], b_qkv[2 * C + P:3 * C].unsqueeze(1)),
                (w_loaded, rows[:, 0, :], gnn_bias.unsqueeze(0)),
                (w_loaded, rows[:, 1, :], b_out.unsqueeze(0)),
                (w_loaded, wr_sb[:], Wr.rearrange("(k p) n -> p k n", p=P)),
                (w_loaded, route[:, 0, :], br.unsqueeze(0)),
            ):
                act.dma_start(dst_ap, src_ap).then_inc(loaded, 16)
            def root(n, r):
                act.wait_ge(var_ready, n + 1)
                nc.scalar.activation(r, r, ACT.Sqrt).then_inc(root_ready, 1)

            root(0, rstd[:, 0:TA])

            def turned_xn(t, p, n):
                act.wait_ge(xn_turned, t + 1)
                wait(act, h_made, t - A1 + 1)
                wait(act, xx_stored[p], n * 16)
                nc.scalar.copy(xnt_a[p].rearrange("p k n -> p (k n)"), bank[p % 2][:, 0:C]).then_inc(xnt_kept, 1)

            def tile(t, p, n):
                if not (isinstance(t, int) and t in (TA - 1, NT - 1)):
                    turned_xn(t + 1, (p + 1) % A1, n + (p + 1) // A1)
                act.wait_ge(h_made, t + 1)
                wait(act, h_stored[p], n * 16)
                wait(act, a_kept, t - A1 + 1)
                nc.scalar.copy(h_a[p], bank[2 + p % 2][:, 0:C + 2 * H]).then_inc(h_kept, 1)
                for c in table_chunks(t):
                    act.wait_ge(steps_turned, c + 1)
                    pt = bank[6 + c % 2][:].rearrange("p (a g k) -> p a k g", a=2, g=G)
                    nc.scalar.copy(srcT[:, c * P * G:(c + 1) * P * G].rearrange("p (k g) -> p k g", g=G),
                                   pt[:, 0]).then_inc(steps_kept, 1)
                    nc.scalar.copy(dstT[:, c * P * G:(c + 1) * P * G].rearrange("p (k g) -> p k g", g=G),
                                   pt[:, 1]).then_inc(steps_kept, 1)
            turned_xn(0, 0, 0)
            for _ in first_pass(act, tile):
                root(1, rstd[:, TA:NT])
                turned_xn(TA, 0, Q_MID)
            act.wait_ge(steps_kept, 2 * KCH)

            def index(b, q):
                nc.scalar.copy(idx[:, q, :], srcT[:, bass.ds(b * TB, TB)]).then_inc(idx_ready, 1)

            def turned(b, q):
                wait(act, a2c_picked, b - R3 + 1)
                for k in range(2):
                    act.wait_ge(hot_turned, b * 2 + k + 1)
                    nc.scalar.copy(hotT[q][:, k * 4:k * 4 + 4, :].rearrange("p j d -> p (j d)"),
                                   bank[k][:]).then_inc(hotT_kept, 1)

            def weights(b, q):
                act.wait_ge(u_ready, b + 1)
                nc.scalar.activation(ring[q][:, :, C:TW], zb[:, q, 0, :].rearrange("p (j h) -> p j h", h=H),
                                     ACT.Exp).then_inc(ex_ready, 1)

            for q in range(R3):
                index(q, q)
            act.wait_ge(wvt_turned, 1)
            nc.scalar.copy(wvT.rearrange("p k n -> p (k n)"), bank[5][:]).then_inc(wvt_kept, 1)
            for stored in (h_stored, xx_stored):
                all_stored(act, stored)
            act.wait_ge(a_kept, NT)
            act.wait_ge(acc_zero, 1)
            nc.scalar.copy(acc[:, 0:A_COLS], acc[:, A_COLS:2 * A_COLS]).then_inc(acc_zero, 1)
            act.wait_ge(hot_ready, 1)
            turned(0, 0)
            weights(0, 0)

            def batch(i, q, side, first):
                b = i * R3 + q
                last = isinstance(i, int) and i == IT
                if not last:
                    act.wait_ge(gathered[q], 16 * TB * (i + 1))
                    index(b + R3, q)
                    turned(b + 1, (q + 1) % R3)
                    weights(b + 1, (q + 1) % R3)
                if side == "qk":
                    if q == 1:
                        act.wait_ge(qk_made, i + 1)
                        wait(act, q2_turned, i)
                        nc.scalar.activation(q2[:], bank[5][:, 0:C], ACT.Square, accum_out=qs[:, 0:1]).then_inc(q2_squared, 1)
                        nc.scalar.activation(k2[:], bank[5][:, C:2 * C], ACT.Square, accum_out=qs[:, 1:2]).then_inc(q2_squared, 1)
                    if q == 2:
                        act.wait_ge(k2_ready, i + 1)
                        nc.scalar.activation(sq[:], q2[:], ACT.Square, accum_out=nq[:, bass.ds(i, 1)]).then_inc(k2_squared, 1)
                        act.wait_ge(k2_squared, i * 2 + 1)
                        nc.scalar.activation(sq[:], k2[:], ACT.Square).then_inc(k2_squared, 1)
                if (side == "qk" and q == 0 and not (isinstance(i, int) and i == 0)):
                    keep_q2t(i - 1)
                if side == "kv" and q == 0:
                    keep_q2t(NT - 1)
                    act.wait_ge(k2_squared, 2 * NT)
                    nc.scalar.activation(nq[:], nq[:], ACT.Sqrt).then_inc(roots, 1)
                    act.wait_ge(kx_kept, 1)
                    nc.scalar.activation(small[:, 16:16 + KC], kx[:, :, C + 1], ACT.Sqrt).then_inc(roots, 1)
                if side == "kv" and q == 1:
                    act.wait_ge(kx_turned, 1)
                    nc.scalar.copy(wqkv[:].rearrange("p k n -> p (k n)")[:, 0:2 * C], bank[5][:]).then_inc(kxt_kept, 1)

            def keep_q2t(t):
                act.wait_ge(q2_turned, t + 1)
                wait(act, q2t_stored, 16 * t)
                nc.scalar.copy(q2t_c[:].rearrange("p k n -> p (k n)"), bank[5][:, 0:C]).then_inc(q2t_kept, 1)

            phases(act, batch)

            for n, (a, e, e_act) in enumerate(((0, XH, XH), (XH, NT, XD))):
                root(2 + n, rstd[:, a:e])
                act.wait_ge(x2_scaled, n + 1)
                for t in range(a, e_act):
                    nc.scalar.activation(acc_tile(t)[:, 0:C], X[:, t, :], ACT.Identity, bias=sc[:, 3, t:t + 1],
                                         scale=rstd[:, t:t + 1]).then_inc(x2_ready, 1)
            act.wait_ge(mean_made, 1)
            nc.scalar.copy(sq[0:1, :], bank[0][0:1, 0:C]).then_inc(mean_kept, 1)
            act.wait_ge(mean_made, 2)
            nc.scalar.copy(mcol[:], bank[1][:, 16:16 + KC]).then_inc(mean_kept, 1)
            act.wait_ge(soft_in, 1)
            nc.scalar.activation(route[:, 2, :], route[:, 1, :], ACT.Exp).then_inc(soft_out, 1)
            act.wait_ge(soft_in, 2)
            nc.scalar.activation(route[:, 6, :], route[:, 5, :], ACT.Exp).then_inc(soft_out, 1)
            act.wait_ge(soft_in, 3)
            nc.scalar.activation(route[:, 12, 0:1], route[:, 11, 0:1], ACT.Exp).then_inc(soft_out, 1)

            def x2_out(g, p, n):
                act.wait_ge(x2_turned, g + 1)
                for k in range(KC):
                    nc.scalar.copy(x2t[p][:, k, 0:n * P], bank[k][:, 0:n * P]).then_inc(x2t_kept, 1)

            def hidden(g, p, n, roots=True):
                for f in range(TOP * FC):
                    if f == FC and roots:
                        root(g + 2, ysc[:, p, 5, :])
                    act.wait_ge(hid_made, g * (TOP * FC) + f + 1)
                    nc.scalar.activation(hT[p][:, f, 0:n * P], bank[HB[f]][:, 0:n * P], ACT.Gelu,
                                         bias=b1_sb[:, f // FC, f % FC:f % FC + 1]).then_inc(hid_kept, 1)
            x2_out(0, 0, FG)
            act.wait_ge(w1_loaded, 16 * NX1)
            hidden(0, 0, FG, False)
            x2_out(1, 1, FG)
            hidden(1, 1, FG, False)
            with act.Fori(1, NG // 2) as i:
                for p in range(2):
                    x2_out(i * 2 + p, p, FG)
                    hidden(i * 2 + p, p, FG)
            x2_out(NG, 0, 1)
            hidden(NG, 0, 1)
            root(NG + 3, ysc[:, 1, 5, :])
            root(NG + 4, ysc[:, 0, 5, 0:1])

        @block.tensor
        def _(pe):
            mm = nc.tensor.matmul
            turn = nc.tensor.transpose
            pe.wait_ge(id_set, 3)
            pe.wait_ge(cmp_done, 1)
            for c in range(KCH):
                mm(bank[6][:, c:c + 1], cmp[:, c * P:(c + 1) * P], ones[:, 0:1], start=True, stop=True)
            for k in range(2):
                ins = mm(bank[7 - k][0:1, 8:8 + KS // 2], ones[:, 0:1], cmp[:, k * (KS // 2):(k + 1) * (KS // 2)],
                         start=True, stop=True)
            ins.then_inc(u_counted, 1)

            pe.wait_ge(wg_ready, 1)

            def xn_in(t, p):
                pe.wait_ge(xn_ready, t + 1)
                wait(pe, xnt_kept, t - 1)
                for k in range(KC):
                    ins = turn(bank[p % 2][:, k * P:(k + 1) * P], xn_a[p][:, k * P:(k + 1) * P], ident[:])
                ins.then_inc(xn_turned, 1)

            def tile(t, p, n):
                if not (isinstance(t, int) and t in (TA - 1, NT - 1)):
                    xn_in(t + 1, (p + 1) % A1)
                pe.wait_ge(xnt_kept, t + 1)
                wait(pe, h_kept, t - 1)
                for k in range(KC):
                    ins = mm(bank[2 + p % 2][:, 0:C + 2 * H], xnt_a[p][:, k, :], wg[:, k, :], start=(k == 0), stop=(k == KC - 1))
                ins.then_inc(h_made, 1)
                for c in table_chunks(t):
                    if c == 0:
                        pe.wait_ge(f_ready, 2)
                    wait(pe, steps_kept, 2 * (c - 1))
                    for a, f in enumerate((f_src, f_dst)):
                        for g in range(G):
                            o_ = (a * G + g) * P
                            ins = turn(bank[6 + c % 2][:, o_:o_ + P], f[:, c, g * P:(g + 1) * P], ident[:])
                    ins.then_inc(steps_turned, 1)
            xn_in(0, 0)
            for _ in first_pass(pe, tile):
                xn_in(TA, 0)

            pe.wait_ge(w_loaded, 16 * NW)
            for d in range(KC):
                for j in range(KC):
                    ins = turn(bank[5][:, (d * KC + j) * P:(d * KC + j + 1) * P],
                               wqkv[:, j, 2 * C + d * P:2 * C + (d + 1) * P], ident[:])
            ins.then_inc(wvt_turned, 1)
            pe.wait_ge(wvt_kept, 1)
            for j in range(KC):
                for d in range(KC):
                    mm(bank[4][:, j * C:(j + 1) * C], wvT[:, d, j * P:(j + 1) * P], wout[:, d, :],
                       start=(d == 0), stop=(d == KC - 1))
            pe.wait_ge(bvx_ready, 1)
            pe.wait_ge(t_ready, 1)
            for d in range(KC):
                ins = mm(bank[7][:, 0:C], bvx[:, d, :], wout[:, d, :], start=(d == 0), stop=(d == KC - 1))
            ins.then_inc(wvo_made, 1)

            def turned(b, q):
                pe.wait_ge(hot_ready, b + 1)
                for k in range(2):
                    wait(pe, hotT_kept, b * 2 + k - 1)
                    for j in range(4):
                        ins = turn(bank[k][:, j * P:(j + 1) * P], hot[q][:, k * 4 + j, :], ident[:])
                    ins.then_inc(hot_turned, 1)

            def pick(b, q):
                _, ts = nc.values_load_multi_w_load_instructions(
                    t_a2c[0:1, bass.ds(b * SB, SB)], engines=[mybir.EngineType.PE], min_val=0,
                    max_val=(NT - 1) * PARTS * AW, skip_runtime_bounds_check_because="steps' node tiles are clamped")
                pe.wait_ge(hotT_kept, b * 2 + 2)
                wait(pe, u_ready, b)
                for j in range(TB):
                    for k in range(PARTS):
                        ins = mm(bank[2][:, j * AW:(j + 1) * AW], hotT[q][:, j, :],
                                 a2p[:, bass.ds(ts[j // G] + k * AW, AW)], start=(k == 0), stop=(k == PARTS - 1))
                ins.then_inc(a2c_picked, 1)

            pe.wait_ge(h_kept, NT)
            turned(0, 0)
            pe.wait_ge(wvo_kept, 1)
            pe.wait_ge(flag_ready, 1)
            wide = pe.value_load(flag[0:1, 0:1], min_val=0, max_val=1)
            with pe.If(wide > 0):
                with pe.Fori(0, NB * TB) as j:
                    pe.wait_ge(seg_hot, j + 2)
                    turn(bank[2][:, 0:P], seg_onehot, ident[:])
                    for k in range(2):
                        ins = mm(bank[3 + k][:], ones[:], seg_diag[:, k * 4:k * 4 + 4, :].rearrange("p h e -> p (h e)"),
                                 start=True, stop=True)
                    ins.then_inc(seg_spread, 1)
                pe.wait_ge(seg_spread, NB * TB)
            pe.wait_ge(t_ready, 1)
            pe.wait_ge(c_ready, 1)
            pick(0, 0)
            pe.wait_ge(wqk_ready, 1)

            def batch(i, q, side, first):
                b = i * R3 + q
                last = isinstance(i, int) and i == IT
                if not last:
                    turned(b + 1, (q + 1) % R3)
                for s in range(SB):
                    if s % 2 == 0:
                        pe.wait_ge(msg_ready, b * 2 + s // 2 + 1)
                    if s == 2 and not last:
                        pick(b + 1, (q + 1) % R3)
                    wait(pe, added, b * SB + s - 1)
                    for g in range(G):
                        ins = mm(bank[3 + s % 2][:, 0:TW], hot[q][:, s * G + g, :], ring[q][:, s * G + g, :],
                                 start=(g == 0), stop=(g == G - 1))
                    ins.then_inc(summed, 1)
                if side == "qk":
                    if q == 0:
                        pe.wait_ge(xnt_loaded, (i + 1) * 16)
                        wait(pe, q2t_kept, i)
                        mm(bank[5][:], ones[0:1, :], bqk[:].rearrange("a k n -> a (k n)"), start=True, stop=False)
                        for k in range(KC):
                            ins = mm(bank[5][:], xnt_c[:, k, :], wqkv[:, k, 0:2 * C], start=False, stop=(k == KC - 1))
                        ins.then_inc(qk_made, 1)
                    if q == 2:
                        end = isinstance(i, int) and i == A2_LAST
                        begin = isinstance(i, int) and i == 0
                        n = LAST if end else P
                        pe.wait_ge(xn_loaded, (i + 1) * 16)
                        pe.wait_ge(k2_squared, i * 2 + 2)
                        for k in range(KC):
                            mm(bank[6 + k][:, 0:C + 1], k2[0:n, k * P:(k + 1) * P], xn_c[0:n, :],
                               start=begin, stop=end, skip_group_check=True)
                            ins = mm(bank[6 + k][:, C + 1:C + 2], sq[0:n, k * P:(k + 1) * P], ones[0:n, 0:1],
                                     start=False, stop=end, skip_group_check=True)
                        ins.then_inc(kx_added, 1)
                        for k in range(KC):
                            ins = turn(bank[5][:, k * P:(k + 1) * P], q2[:, k * P:(k + 1) * P], ident[:])
                        ins.then_inc(q2_turned, 1)
                if side == "kv" and q == 1:
                    pe.wait_ge(kx_kept, 1)
                    pe.wait_ge(q2t_kept, NT)
                    for j in range(KC):
                        for k in range(KC):
                            ins = turn(bank[5][:, (j * KC + k) * P:(j * KC + k + 1) * P], kx[:, k, j * P:(j + 1) * P], ident[:])
                    ins.then_inc(kx_turned, 1)
                if side == "kv" and q == 2:
                    pe.wait_ge(kxt_kept, 1)
                    kxT = wqkv[:].rearrange("p k n -> p (k n)")
                    for k in range(KC):
                        for j in range(KC):
                            ins = mm(bank[6 + k][:, 0:C], kxT[:, (j * KC + k) * P:(j * KC + k + 1) * P], wvo[:, j, :],
                                     start=(j == 0), stop=(j == KC - 1))
                    ins.then_inc(kvw_made, 1)
                if side == "mix" or (side == "mix_end" and q == 0):
                    t = (i - B_FIRST) * R3 + q
                    if first and q == 0:
                        pe.wait_ge(kvw_ready, 1)
                        pe.wait_ge(crow_ready, 1)
                    pe.wait_ge(mix_loaded[q], (i - B_FIRST + 1) * 32)
                    xt, q2t = (a.rearrange("p (k n) -> p k n", k=KC) for a in mix_in[q])
                    wait(pe, mix_added, t * 2)
                    mm(bank[5][:, 0:C], ones[0:1, :], rows[0:1, 2, :], start=True, stop=False)
                    for k in range(KC):
                        mm(bank[5][:, 0:C], xt[:, k, :], wvo[:, k, :], start=False, stop=(k == KC - 1))
                    for k in range(KC):
                        ins = mm(bank[6][:, 0:C], q2t[:, k, :], kvw[:, k, :], start=(k == 0), stop=(k == KC - 1))
                    ins.then_inc(mix_made, 1)

            phases(pe, batch)

            def x2_in(g, p, n):
                pe.wait_ge(x2_staged, g + 1)
                wait(pe, x2t_kept, g * KC)
                for k in range(KC):
                    for j in range(n):
                        ins = turn(bank[k][:, j * P:(j + 1) * P], x2s[p][:, j, k * P:(k + 1) * P], ident[:])
                ins.then_inc(x2_turned, 1)

            by_act, by_dve = list(range(XH, XD)), list(range(XD, NT))
            order = list(range(XH))
            for k in range(max(len(by_act), len(by_dve))):
                order += by_act[k:k + 1] + by_dve[k:k + 1]
            for k, t in enumerate(order):
                n = LAST if t == NT - 1 else P
                if t < XD:
                    pe.wait_ge(x2_ready, t + 1)
                else:
                    pe.wait_ge(x2_late, t - XD + 1)
                ins = mm(bank[0][0:1, 0:C], ones[0:n, 0:1], acc_tile(t)[0:n, 0:C], start=(k == 0), stop=(k == NT - 1))
            ins.then_inc(mean_made, 1)
            pe.wait_ge(mean_kept, 1)
            for k in range(KC):
                ins = mm(bank[1][:, 16 + k:17 + k], sq[0:1, k * P:(k + 1) * P], ones[0:1, 0:1], start=True, stop=True)
            ins.then_inc(mean_made, 1)
            pe.wait_ge(mean_kept, 2)
            for k in range(KC):
                ins = mm(bank[1][0:1, 0:NE], mcol[:, k:k + 1], wr_sb[:, k, :], start=(k == 0), stop=(k == KC - 1))
            ins.then_inc(logits_made, 1)
            pe.wait_ge(soft_in, 1)
            x2_in(0, 0, FG)
            pe.wait_ge(route_ready, 1)
            mm(bank[4][:, 0:TOP], ones[0:1, :], route[0:1, 14, 0:TOP], start=True, stop=True).then_inc(wsel_made, 1)

            def hidden(g, p, n):
                pe.wait_ge(x2t_kept, (g + 1) * KC)
                for f in range(TOP * FC):
                    before = HB_BEFORE[f]
                    wait(pe, hid_kept, g * (TOP * FC) + before)
                    for k in range(KC):
                        ins = mm(bank[HB[f]][:, 0:n * P], w1_sb[:, f // FC, k, (f % FC) * P:(f % FC + 1) * P],
                                 x2t[p][:, k, 0:n * P], start=(k == 0), stop=(k == KC - 1))
                    ins.then_inc(hid_made, 1)

            def down(g, p, n):
                pe.wait_ge(hid_kept, (g + 1) * (TOP * FC))
                for j in range(n):
                    wait(pe, y_added, g * FG + j - FG + 1)
                    for f in range(TOP * FC):
                        ins = mm(bank[4 + j][:, 0:C], hT[p][:, f, j * P:(j + 1) * P], w2_sb[:, f // FC, f % FC, :],
                                 start=(f == 0), stop=(f == TOP * FC - 1))
                    ins.then_inc(y_made, 1)
            pe.wait_ge(w1_loaded, 16 * NX1)
            hidden(0, 0, FG)
            x2_in(1, 1, FG)
            pe.wait_ge(b2_ready, 1)
            mm(bank[6][:, 0:C], ones[0:1, :], b2r[0:1, 2, :], start=True, stop=True).then_inc(b2_made, 1)
            pe.wait_ge(w2_scaled, 1)
            for g in range(2):
                hidden(g + 1, 1 - g, FG)
                x2_in(g + 2, g, FG)
                down(g, g, FG)
            with pe.Fori(1, NG // 2 - 1) as i:
                for p in range(2):
                    hidden(i * 2 + p + 1, 1 - p, FG)
                    x2_in(i * 2 + p + 2, p, FG)
                    down(i * 2 + p, p, FG)
            hidden(NG - 1, 1, FG)
            x2_in(NG, 0, 1)
            down(NG - 2, 0, FG)
            hidden(NG, 0, 1)
            down(NG - 1, 1, FG)
            down(NG, 0, 1)

        @block.vector
        def _(dve):
            v = nc.vector
            own = Chain(dve, dve_own)

            def ln_stats(link, n, st, s, m, r):
                v.tensor_tensor(s[1], st[:, :, 2], st[:, :, 5], ALU.add).then_inc(link.sem, 1)
                v.tensor_tensor(s[2], st[:, :, 1], st[:, :, 4], ALU.add).then_inc(link.sem, 1)
                link.n = link.n + 2
                link(v.tensor_tensor(s[0], st[:, :, 1], st[:, :, 4], ALU.subtract))
                link(v.scalar_tensor_tensor(out=s[0], in0=s[0], scalar=C / 4.0, in1=s[0], op0=ALU.mult, op1=ALU.mult))
                v.tensor_scalar(m, s[2], 0.5, None, ALU.mult).then_inc(link.sem, 1)
                link.n = link.n + 1
                link(v.tensor_tensor(s[1], s[1], s[0], ALU.add))
                v.tensor_scalar(r, s[1], 1.0 / C, LN_EPS, ALU.mult, ALU.add).then_inc(var_ready, 1)
                dve.wait_ge(root_ready, n + 1)
                link(v.reciprocal(r, r))

            own(v.memset(X[:, NT - 1, :], 0.0))
            v.memset(lastd, 1 << 20).then_inc(lastd_clear, 1)

            dve.wait_ge(iota_set, 3)
            v.tensor_copy(iota_p[:], iotai[:, 0:P])
            v.tensor_copy(kio, iotai).then_inc(dve_own, 1)
            own.n += 1
            own(v.tensor_copy(ucol, kcol.bitcast(I32)))
            v.tensor_copy(kcol, ucol)
            own(v.tensor_copy(tcol[:, 0:UCH], uio.bitcast(I32)))
            dve.wait_ge(lastd_loaded, 16 * UCH)
            dve.wait_ge(lastd_clear, 1)
            own(v.tensor_scalar(lastt, lastd, 7, None, ALU.arith_shift_right))
            own(v.tensor_scalar(fcol, lastt, float(NT - 1), None, ALU.min))
            own(v.tensor_tensor(fcol, fcol, tcol[:, 0:UCH], ALU.add))
            own(v.tensor_scalar(cmp, kio, fcol[:, 0:1], None, ALU.is_gt))
            for c in range(1, UCH):
                ins = v.scalar_tensor_tensor(out=cmp, in0=kio, scalar=fcol[:, c:c + 1], in1=cmp, op0=ALU.is_gt, op1=ALU.add)
                own(ins)
            dve.sem_inc(cmp_done, 1)

            def measure(c):
                dve.wait_ge(x_loaded[c], 16)
                for t in range(c * XC, min((c + 1) * XC, NT)):
                    v.bn_stats(stat[:, t, :], X[:, t, :]).then_inc(x_measured, 1)

            measure(0)
            dve.wait_ge(wg_loaded, 16 * NWG)
            for a in range(2):
                for k in range(KC):
                    ins = v.tensor_tensor(prod[:, k, :], wg[:, k, 0:C], attn[:, a, :], ALU.mult)
                    ins.then_inc(dve_own, 1)
                    own.n += 1
                dve.wait_ge(dve_own, own.n)
                for k in range(KC):
                    ins = v.tensor_reduce(wg[:, k, C + a * H:C + (a + 1) * H], prod[:, k, :].rearrange("p (h j) -> p h j", h=H),
                                          AX.X, ALU.add)
                    own(ins)
            dve.sem_inc(wg_ready, 1)

            measure(1)

            dve.wait_ge(u_counted, 1)
            v.tensor_scalar(ucol, bank[6][:, 0:KCH], float(U), None, ALU.min).then_inc(dve_own, 1)
            own(v.tensor_copy(urow[0:1, 0, 0:KS // 2], bank[7][0:1, 8:8 + KS // 2]))
            own.n += 1
            own(v.tensor_copy(urow[0:1, 0, KS // 2:KS], bank[6][0:1, 8:8 + KS // 2]))
            v.tensor_copy(ucol_i, ucol).then_inc(ucol_ready, 1)
            own(v.tensor_tensor(tcol, kcol, bank[6][:, 0:KCH], ALU.subtract))
            own(v.tensor_scalar(tcol, tcol, float(NT - 1), float(P), ALU.min, ALU.mult))
            own(v.tensor_tensor(urow[0:1, 1, :], kio[0:1, :], urow[0:1, 0, :], ALU.subtract))
            own(v.tensor_scalar(urow[0:1, 1, :], urow[0:1, 1, :], float(NT - 1), None, ALU.min))
            v.tensor_scalar(t_acc[:], urow[0:1, 1, :], float(TW), None, ALU.mult).then_inc(dve_own, 1)
            own.n += 1
            own(v.tensor_scalar(t_a2c[:], urow[0:1, 1, :], float(PARTS * AW), None, ALU.mult))
            dve.sem_inc(t_ready, 1)

            dve.wait_ge(x_measured, TA)
            ln_stats(own, 0, stat[:, 0:TA, :], [sc[:, n, 0:TA] for n in range(4)], mean[:, 0:TA], rstd[:, 0:TA])

            dve.wait_ge(w_loaded, 16 * NW)
            own(v.tensor_copy(bvx, bv_col[:].unsqueeze(2).to_broadcast([P, KC, P])))
            dve.sem_inc(bvx_ready, 1)

            def tile(t, p, n):
                wait(dve, xn_turned, t - A1 + 1)
                wait(dve, xx_stored[p], n * 16)
                v.tensor_scalar(xn_a[p].unsqueeze(1), X[:, bass.ds(t, 1), :], mean[:, bass.ds(t, 1)],
                                rstd[:, bass.ds(t, 1)], ALU.subtract, ALU.mult).then_inc(xn_ready, 1)
                if isinstance(t, int) and t == 0:
                    dve.wait_ge(x_loaded[2], 16)
                if isinstance(n, int) and n < Q_MID or not isinstance(t, int) and early_tiles:
                    m = t * 2 + TA
                    for k in range(2):
                        v.bn_stats(stat[:, bass.ds(m + k, 1), :].rearrange("p o s -> p (o s)"),
                                   X[:, bass.ds(m + k, 1), :].rearrange("p o c -> p (o c)")).then_inc(x_measured, 1)
                if isinstance(t, int) and t == XC // 2 - 1:
                    for c in range(3, 7):
                        dve.wait_ge(x_loaded[c], 16)
                if isinstance(t, int) and t == TA - TT - 1:
                    convert()
                if isinstance(t, int) and t == TA - A1:
                    dve.wait_ge(w_loaded, 16 * NW)
                    v.tensor_reduce(small[:, 0:4].rearrange("p (k a) -> p k a", a=2),
                                    wqkv[:, :, 0:2 * C].rearrange("p k (a n) -> p k a n", a=2), AX.X, ALU.add).then_inc(w_summed, 1)
                    v.tensor_reduce(small[0:1, 4:6], bqk[:], AX.X, ALU.add).then_inc(w_summed, 1)
                if not (isinstance(t, int) and t < 3):
                    keep(t - 3, (p - 3) % A1)

            def keep(t, p):
                dve.wait_ge(h_kept, t + 1)
                v.tensor_copy(a1t[:, bass.ds(t, 1), :], h_a[p][:, C:C + H].unsqueeze(1))
                v.tensor_copy(a2c[:, bass.ds(t * AW, H)], h_a[p][:, C + H:C + 2 * H]).then_inc(a_kept, 1)
            def convert():
                dve.wait_ge(steps_gathered, 16 * 2 * KCH)
                v.tensor_copy(f_src.rearrange("p c e -> p (c e)"), g_src.rearrange("p c e -> p (c e)")).then_inc(f_ready, 1)
                for c in range(KCH):
                    ins = v.tensor_scalar(f_dst[:, c, :], g_dst[:, c, :], tcol[:, c:c + 1], None, ALU.subtract)
                ins.then_inc(f_ready, 1)

            early_tiles = True
            for _ in first_pass(dve, tile):
                early_tiles = False
                v.bn_stats(stat[:, NT - 1, :], X[:, NT - 1, :]).then_inc(x_measured, 1)
                dve.wait_ge(x_measured, NT)
                ln_stats(own, 1, stat[:, TA:NT, :], [sc[:, n, TA:NT] for n in range(4)], mean[:, TA:NT], rstd[:, TA:NT])
            for t in range(NT - 3, NT):
                keep(t, t % A1)

            dve.wait_ge(a_kept, NT)
            v.tensor_reduce(amax[:, 0, 0:H], a1t[:].rearrange("p t h -> p h t"), AX.X, ALU.max).then_inc(dve_own, 1)
            own.n += 1
            own(v.tensor_reduce(amax[:, 2, 0:H], a1t[:].rearrange("p t h -> p h t"), AX.X, ALU.min))
            own(v.tensor_scalar(amax[:, 0, H:2 * H], amax[:, 2, 0:H], -1.0, None, ALU.mult))
            dve.sem_inc(ext_ready, 1)

            def one_hots(b, q):
                wait(dve, summed, (b - R3 + 1) * SB)
                v.tensor_tensor(hot[q], iota_p[:].unsqueeze(1).to_broadcast([P, TB, P]),
                                dstT[:, bass.ds(b * TB, TB)].unsqueeze(2).to_broadcast([P, TB, P]),
                                ALU.is_equal).then_inc(hot_ready, 1)

            dve.wait_ge(steps_kept, 2 * KCH)
            one_hots(0, 0)
            one_hots(1, 1)

            dve.wait_ge(wvo_made, 1)
            own(v.tensor_copy(wvo[:].rearrange("p k n -> p (k n)"), bank[4][:]))
            own(v.tensor_copy(bvo[:], bank[7][:, 0:C]))
            own(v.tensor_tensor(rows[:, 2, :], rows[:, 0, :], rows[:, 1, :], ALU.add))
            own(v.tensor_tensor(rows[:, 2, :], rows[:, 2, :], bvo[0:1, :], ALU.add))
            dve.sem_inc(wvo_kept, 1)
            dve.sem_inc(crow_ready, 1)

            dve.wait_ge(ext_all, 1)
            a2v = a2c[:].rearrange("p (t a) -> p t a", a=AW)
            cz = a1t[:]
            own(v.tensor_tensor(amax[:, 3, 0:H], amax[:, 1, 0:H], amax[:, 1, H:2 * H], ALU.add))
            v.tensor_copy(cz, amax[:, 1, 0:H].unsqueeze(1).to_broadcast([P, NT, H])).then_inc(dve_own, 1)
            own.n += 1
            own(v.tensor_reduce(amax[:, 3, H:H + 1], amax[:, 3, 0:H], AX.X, ALU.max))
            own(v.tensor_scalar(flag[:], amax[0:1, 3, H:H + 1], SPREAD, None, ALU.is_gt))
            dve.sem_inc(flag_ready, 1)
            wide = dve.value_load(flag[0:1, 0:1], min_val=0, max_val=1)
            with dve.If(wide > 0):
                for stored in (h_stored, xx_stored):
                    all_stored(dve, stored)
                dve.wait_ge(steps_kept, 2 * KCH)
                dve.wait_ge(acc_zero, 2)
                seg = acc[:].rearrange("p (t w) -> p t w", w=TW)[:, :, C:TW]
                link = Chain(dve, seg_own)
                link(v.memset(seg, -BIG))
                dve.sem_inc(seg_hot, 1)
                with dve.Fori(0, NB * SB) as k:
                    t = dve.value_load(t_acc[0:1, bass.ds(k, 1)], min_val=0, max_val=(NT - 1) * TW)
                    for g in range(G):
                        j = k * G + g
                        link = Chain(dve, seg_own, j * 5 + 1)
                        link(v.tensor_scalar(seg_onehot, iota_p[:], dstT[:, bass.ds(j, 1)], None, ALU.is_equal))
                        dve.wait_ge(seg_in, (j + 1) * 16)
                        v.tensor_tensor(seg_diag, ident[:].unsqueeze(1).to_broadcast([P, H, P]),
                                        seg_rows[:, C:TW].unsqueeze(2).to_broadcast([P, H, P]), ALU.mult).then_inc(seg_hot, 1)
                        dve.wait_ge(seg_spread, j + 1)
                        link(v.tensor_scalar(seg_mask, bank[2][:, 0:P], -1.0, BIG, ALU.add, ALU.mult))
                        for n in range(2):
                            ins = v.tensor_tensor(seg_z[:, n * 4:n * 4 + 4, :], bank[3 + n][:].rearrange("p (h e) -> p h e", h=4),
                                                  seg_mask.unsqueeze(1).to_broadcast([P, 4, P]), ALU.add)
                        link(ins)
                        link(v.tensor_reduce(amax[:, 3, 0:H], seg_z, AX.X, ALU.max))
                        at = acc[:, bass.ds(t + C, H)]
                        link(v.tensor_tensor(at, at, amax[:, 3, 0:H], ALU.max))
                link = Chain(dve, seg_own, NB * TB * 5 + 1)
                link(v.tensor_scalar(cz, seg, -BIG / 2, None, ALU.is_gt))
                link(v.tensor_tensor(cz, cz, seg, ALU.mult))
                link(v.memset(seg, 0.0))
            own(v.tensor_tensor(cz, a2v[:, :, 0:H], cz, ALU.add))
            own(v.scalar_tensor_tensor(out=a2v[:, :, H:AW], in0=cz, scalar=SLOPE, in1=cz, op0=ALU.mult, op1=ALU.max))
            for k in range(PARTS):
                part = a2p[:].rearrange("p (t k a) -> p t k a", k=PARTS, a=AW)[:, :, k, :]
                own(v.tensor_copy(part, a2v))
                if k < PARTS - 1:
                    own(v.tensor_tensor(a2v, a2v, part, ALU.subtract))
            dve.sem_inc(c_ready, 1)

            for stored in (h_stored, xx_stored):
                all_stored(dve, stored)
            dve.wait_ge(acc_zero, 2)

            def exponents(b, q, n):
                dve.wait_ge(gathered[q], n * 16 * TB)
                dve.wait_ge(a2c_picked, b + 1)
                z = [zb[:, q, k, :].rearrange("p (j h) -> p j h", h=H) for k in range(3)]
                pk = bank[2][:, 0:TB * AW].rearrange("p (j a) -> p j a", a=AW)
                link = Chain(dve, z_own, b * 3)
                link(v.tensor_tensor(z[0], ring[q][:, :, C:TW], pk[:, :, 0:H], ALU.add))
                link(v.scalar_tensor_tensor(out=z[1], in0=z[0], scalar=SLOPE, in1=z[0], op0=ALU.mult, op1=ALU.max))
                link(v.tensor_tensor(z[2], z[1], pk[:, :, H:AW], ALU.subtract))
                v.tensor_scalar(z[0], z[2], 0.0, None, ALU.min).then_inc(u_ready, 1)

            exponents(0, 0, 1)

            def batch(i, q, side, first):
                b = i * R3 + q
                last = isinstance(i, int) and i == IT
                _, ts = nc.values_load_multi_w_load_instructions(
                    t_acc[0:1, bass.ds(b * SB, SB)], engines=[mybir.EngineType.DVE], min_val=0,
                    max_val=(NT - 1) * TW, skip_runtime_bounds_check_because="steps' node tiles are clamped")
                dve.wait_ge(ex_ready, b + 1)
                for k in range(2):
                    m = ring[q][:, k * 4:k * 4 + 4, 0:C].rearrange("p j (h c) -> p j h c", h=H)
                    ex = ring[q][:, k * 4:k * 4 + 4, C:TW].unsqueeze(3).to_broadcast([P, 4, H, HC])
                    v.tensor_tensor(m, m, ex, ALU.mult).then_inc(msg_ready, 1)

                def add(s):
                    dve.wait_ge(summed, b * SB + s + 1)
                    wait(dve, added, b * SB + s)
                    a = acc[:, bass.ds(ts[s], TW)]
                    v.tensor_tensor(a, bank[3 + s % 2][:, 0:TW], a, ALU.add).then_inc(added, 1)
                if side == "mix" and first and q == 0:
                    dve.wait_ge(kvw_made, 1)
                    for k in range(KC):
                        own(v.scalar_tensor_tensor(out=kvw[:, k, :], in0=bvo[:], scalar=kx[:, k, C:C + 1],
                                                   in1=bank[6 + k][:, 0:C], op0=ALU.mult, op1=ALU.add))
                        own(v.tensor_scalar(kvw[:, k, :], kvw[:, k, :], small[:, 20 + k:21 + k], 1.0 / math.sqrt(N),
                                            ALU.mult, ALU.mult))
                    dve.sem_inc(kvw_ready, 1)
                if side == "mix" or (side == "mix_end" and q < 2):
                    t = (i - B_FIRST) * R3 + q - 1
                    if not (first and q == 0):
                        dve.wait_ge(mix_made, t + 1)
                        xt = X[:, bass.ds(t, 1), :]
                        v.tensor_tensor(xt, xt, bank[5][:, 0:C].unsqueeze(1), ALU.add).then_inc(mix_added, 1)
                        dve.wait_ge(mix_added, t * 2 + 1)
                        v.scalar_tensor_tensor(out=xt, in0=bank[6][:, 0:C].unsqueeze(1), scalar=nq[:, bass.ds(t, 1)],
                                               in1=xt, op0=ALU.mult, op1=ALU.add).then_inc(mix_added, 1)
                add(0)
                if not last:
                    one_hots(b + 2, (q + 2) % R3)
                add(1)
                if not last:
                    exponents(b + 1, (q + 1) % R3, i + 1 if q < 2 else i + 2)
                add(2)
                if side == "qk" and q == 2:
                    dve.wait_ge(q2_squared, (i + 1) * 2)
                    lq = Chain(dve, q_own, i * 2)
                    lq(v.tensor_scalar(qs[:, 2:4], qs[:, 0:2], EPS_DIV, None, ALU.add))
                    lq(v.reciprocal(qs[:, 4:6], qs[:, 2:4]))
                    v.tensor_scalar(q2[:], q2[:], qs[:, 4:5], None, ALU.mult)
                    v.tensor_scalar(k2[:], k2[:], qs[:, 5:6], None, ALU.mult).then_inc(k2_ready, 1)
                add(3)
                if side == "kv" and q == 0:
                    dve.wait_ge(kx_added, NT)
                    for k in range(KC):
                        own(v.tensor_copy(kx[:, k, :], bank[6 + k][:, 0:C + 2]))
                    dve.sem_inc(kx_kept, 1)
                if side == "kv" and q == 1:
                    kn = small[:, 16:16 + KC]
                    dve.wait_ge(roots, 2)
                    own(v.tensor_scalar(kn, kn, EPS_NORM, None, ALU.max))
                    own(v.reciprocal(small[:, 20:20 + KC], kn))
                    own(v.tensor_scalar(nq[:], nq[:], EPS_NORM, None, ALU.max))
                    own(v.reciprocal(nq[:], nq[:]))
            phases(dve, batch)

            a3 = acc[:].rearrange("p (t w) -> p t w", w=TW)
            dve.wait_ge(added, NB * SB)
            den = a3[:, :, C:TW]
            own(v.tensor_scalar(a1t[:], den, TINY, None, ALU.max))
            own(v.reciprocal(a1t[:], a1t[:]))
            dve.wait_ge(mix_added, 2 * NT)
            for c in range(NXP + 2):
                if c < NXP:
                    m = a3[:, c * XP:(c + 1) * XP, 0:C].rearrange("p t (h c) -> p t h c", h=H)
                    r_ = a1t[:, c * XP:(c + 1) * XP, :].unsqueeze(3).to_broadcast([P, XP, H, HC])
                    v.tensor_tensor(m, m, r_, ALU.mult).then_inc(msg_scaled, 1)
                if 0 < c <= NXP:
                    dve.wait_ge(msg_scaled, c)
                    xc = X[:, (c - 1) * XP:c * XP, :]
                    v.tensor_tensor(xc, xc, a3[:, (c - 1) * XP:c * XP, 0:C], ALU.add).then_inc(x1_made, 1)
                if c > 1:
                    dve.wait_ge(x1_made, c - 1)
                    for t in range((c - 2) * XP, (c - 1) * XP):
                        ins = v.bn_stats(stat[:, t, :], X[:, t, :])
                    own(ins)
                for n, (a, e) in enumerate(((0, XH), (XH, NT))):
                    if e == (c - 1) * XP:
                        ln_stats(own, 2 + n, stat[:, a:e, :], [sc[:, k, a:e] for k in range(4)], mean[:, a:e], rstd[:, a:e])
                        own(v.scalar_tensor_tensor(out=sc[:, 3, a:e], in0=mean[:, a:e], scalar=-1.0, in1=rstd[:, a:e],
                                                   op0=ALU.mult, op1=ALU.mult))
                        dve.sem_inc(x2_scaled, 1)
            for t in range(XD, NT):
                v.tensor_scalar(acc_tile(t)[:, 0:C], X[:, t, :], mean[:, t:t + 1], rstd[:, t:t + 1],
                                ALU.subtract, ALU.mult).then_inc(x2_late, 1)

            def r(n, w=NE):
                return route[0:1, n, 0:w]
            io = iota_p[0:1, 0:NE]
            dve.wait_ge(logits_made, 1)
            own(v.scalar_tensor_tensor(out=r(1), in0=bank[1][0:1, 0:NE], scalar=1.0 / N, in1=r(0), op0=ALU.mult, op1=ALU.add))
            own(v.tensor_reduce(r(3, 1), r(1), AX.X, ALU.max))
            own(v.tensor_scalar(r(1), r(1), r(3, 1), None, ALU.subtract))
            dve.sem_inc(soft_in, 1)
            dve.wait_ge(soft_out, 1)
            own(v.tensor_reduce(r(3, 1), r(2), AX.X, ALU.add))
            own(v.reciprocal(r(4, 1), r(3, 1)))
            own(v.tensor_scalar(r(2), r(2), r(4, 1), None, ALU.mult))
            own(v.tensor_scalar(r(4), r(2), float(N), TINY, ALU.mult, ALU.max))
            own(v.reciprocal(r(4), r(4)))
            own(v.tensor_scalar(r(4), r(4), CAPACITY, 1.0, ALU.mult, ALU.min))
            own(v.tensor_tensor(r(5), r(2), r(4), ALU.mult))
            own(v.tensor_reduce(r(3, 1), r(5), AX.X, ALU.max))
            own(v.tensor_scalar(r(5), r(5), r(3, 1), None, ALU.subtract))
            dve.sem_inc(soft_in, 1)
            dve.wait_ge(soft_out, 2)
            own(v.tensor_reduce(r(3, 1), r(6), AX.X, ALU.add))
            own(v.reciprocal(r(4, 1), r(3, 1)))
            own(v.tensor_scalar(r(7), r(6), r(4, 1), None, ALU.mult))
            for e in range(TOP):
                own(v.tensor_reduce(r(8 + e, 1), r(7), AX.X, ALU.max))
                own(v.tensor_scalar(r(10), r(7), r(8 + e, 1), float(NE), ALU.is_lt, ALU.mult))
                own(v.tensor_tensor(r(10), r(10), io, ALU.add))
                own(v.tensor_reduce(route[0:1, 13, e:e + 1], r(10), AX.X, ALU.min))
                if e == 0:
                    own(v.tensor_scalar(r(10), io, route[0:1, 13, e:e + 1], 4.0, ALU.is_equal, ALU.mult))
                    own(v.tensor_tensor(r(7), r(7), r(10), ALU.subtract))
            own(v.tensor_tensor(r(11, 1), r(9, 1), r(8, 1), ALU.subtract))
            dve.sem_inc(soft_in, 1)
            own(v.tensor_copy(route_i[0:1, 0:TOP], route[0:1, 13, 0:TOP]))
            dve.wait_ge(soft_out, 3)
            own(v.tensor_scalar(r(15, 1), r(12, 1), 1.0, None, ALU.add))
            own(v.reciprocal(route[0:1, 14, 0:1], r(15, 1)))
            own(v.tensor_tensor(route[0:1, 14, 1:2], route[0:1, 14, 0:1], r(12, 1), ALU.mult))
            dve.sem_inc(route_ready, 1)
            dve.wait_ge(wsel_made, 1)
            own(v.tensor_copy(wsel[:], bank[4][:, 0:TOP]))
            dve.wait_ge(e_loaded, 16 * NX)
            own(v.tensor_scalar(b2r[:, 2, :], b2r[:, 0, :], wsel[0:1, 0:1], None, ALU.mult))
            own(v.scalar_tensor_tensor(out=b2r[:, 2, :], in0=b2r[:, 1, :], scalar=wsel[0:1, 1:2], in1=b2r[:, 2, :],
                                       op0=ALU.mult, op1=ALU.add))
            dve.sem_inc(b2_ready, 1)
            for e in range(TOP):
                w = w2_sb[:, e].rearrange("p f d -> p (f d)")
                own(v.tensor_scalar(w, w, wsel[:, e:e + 1], None, ALU.mult))
            dve.wait_ge(b2_made, 1)
            own(v.tensor_copy(b2w, bank[6][:, 0:C]))
            dve.sem_inc(w2_scaled, 1)

            def finish(g, p, n):
                link = Chain(dve, y_own, g * (n_links))
                base = link.n
                wait(dve, out_stored[p], 16 * ((g - p) // 2))
                for j in range(n):
                    dve.wait_ge(y_made, g * FG + j + 1)
                    v.tensor_tensor(y[p][:, j, :], bank[4 + j][:, 0:C],
                                    acc[:, bass.ds((g * FG + j) * TW, C)], ALU.add).then_inc(y_added, 1)
                dve.wait_ge(y_added, g * FG + n)
                yy = y[p][:, 0:n, :]

                def wide(a):
                    return a.unsqueeze(1).to_broadcast([P, n, C])
                link(v.tensor_tensor(yy, yy, wide(b2w), ALU.add))
                for j in range(n):
                    ins = v.bn_stats(ystat[:, p, j, :], y[p][:, j, :])
                link(ins)
                ln_stats(link, 4 + g, ystat[:, p, 0:n, :], [ysc[:, p, k, 0:n] for k in range(4)], ysc[:, p, 4, 0:n], ysc[:, p, 5, 0:n])
                for j in range(n):
                    ins = v.tensor_scalar(y[p][:, j, :], y[p][:, j, :], ysc[:, p, 4, j:j + 1], ysc[:, p, 5, j:j + 1],
                                          ALU.subtract, ALU.mult)
                link(ins)
                link(v.tensor_tensor(yy, yy, wide(gb[:, 0, :]), ALU.mult))
                link(v.tensor_tensor(yy, yy, wide(gb[:, 1, :]), ALU.add))
                v.tensor_tensor(yy, yy, X[:, bass.ds(g * FG, n), :], ALU.add).then_inc(y_ready, 1)
            n_links = 12
            finish(0, 0, FG)
            finish(1, 1, FG)
            with dve.Fori(1, NG // 2) as i:
                finish(i * 2, 0, FG)
                finish(i * 2 + 1, 1, FG)
            finish(NG, 0, 1)


_IN = ['x', 'src', 'dst', 'L0_gnn_W', 'L0_gnn_attn_l', 'L0_gnn_attn_r', 'L0_gnn_bias', 'L0_mix_W_qkv', 'L0_mix_b_qkv',
       'L0_mix_W_out', 'L0_mix_b_out', 'L0_ffn_Wr', 'L0_ffn_br', 'L0_ffn_W1', 'L0_ffn_b1', 'L0_ffn_W2', 'L0_ffn_b2',
       'L0_ffn_gamma', 'L0_ffn_beta']


def kernel(**inputs):
    import numpy as np
    import concourse.bacc as bacc
    from concourse.bass_utils import run_bass_kernel_spmd

    nc = bacc.Bacc("TRN2", target_bir_lowering=False, num_devices=1)
    arrays, args = {}, []
    for name in _IN:
        a = np.ascontiguousarray(inputs[name])
        if name in ('src', 'dst'):
            rows = np.full(((U + 1) * EG,), 0 if name == 'src' else NONE, a.dtype)
            rows[:E] = a
            a = rows.reshape(U + 1, EG)
        arrays[name] = a
        args.append(nc.dram_tensor(name, a.shape, mybir.dt.from_np(a.dtype), kind="ExternalInput").ap())
    args.append(nc.dram_tensor("out", (N, C), F32, kind="ExternalOutput").ap())
    build(nc, *args)
    r = run_bass_kernel_spmd(nc, [arrays], core_ids=[0])
    return r.results[0]["out"]
```
